# Optimizing a Trainium2 kernel written in Bass

```python
import numpy as np
import jax
import jax.numpy as jnp

def _softmax(x, axis=-1):
    return jax.nn.softmax(x, axis=axis)

def _gelu(x):
    return jax.nn.gelu(x, approximate=True)

def _silu(x):
    return jax.nn.silu(x)

def _sigmoid(x):
    return jax.nn.sigmoid(x)

def _layernorm(x, axis=-1, eps=1e-05):
    m = jnp.mean(x, axis=axis, keepdims=True)
    v = jnp.var(x, axis=axis, keepdims=True)
    return (x - m) / jnp.sqrt(v + eps)

def _scatter_add(tgt, idx, src, axis=0):
    return tgt.at[idx].add(src)

def _segment_sum(src, seg, n):
    return jax.ops.segment_sum(src, seg, n)
kernel_name = 'mk_decoder_preln_d2_seqx_r4_1274da'

def setup_inputs(seed: int=0):
    np.random.seed(seed)
    _w = jnp.asarray

    def _rec_inputs():
        import jax
        import jax.numpy as jnp
        _rk = jax.random.key(seed)
        x = 7.22e-05 + 1 * jax.random.normal(jax.random.fold_in(_rk, 1), (8, 512, 256), jnp.float32)
        _lenS = 512 - jax.random.randint(jax.random.fold_in(_rk, 7), (8,), 0, max(1, 512 // 4) + 1, jnp.int32)
        _lenS2 = 512 - jax.random.randint(jax.random.fold_in(_rk, 8), (8,), 0, max(1, 512 // 4) + 1, jnp.int32)
        _ctx_1024P = jax.random.normal(jax.random.fold_in(_rk, 11), (8, 16, 256), jnp.float32)
        _ctx_1024c = jax.random.dirichlet(jax.random.fold_in(_rk, 511), 0.3 * jnp.ones((16,), jnp.float32), (8, 512))
        _ctx_1024t = jnp.einsum('bsk,bkd->bsd', _ctx_1024c, _ctx_1024P)
        _ctx_1024t = _ctx_1024t * jax.lax.rsqrt(jnp.mean(jnp.square(_ctx_1024t)) + 1e-12) * 0.953939
        ctx_1024 = 4.13588e-05 + 0.999923 * (_ctx_1024t + 0.3 * jax.random.normal(jax.random.fold_in(_rk, 611), (8, 512, 256), jnp.float32))
        _validS = jnp.arange(512)[None, :] < _lenS[:, None]
        _validS2 = jnp.arange(512)[None, :] < _lenS2[:, None]
        _causal = jnp.tril(jnp.ones((512, 512), dtype=bool))
        mask_Bx1xSxS2_bk1 = jnp.broadcast_to(_validS2[:, None, None, :], (8, 1, 512, 512))
        return (x, ctx_1024, mask_Bx1xSxS2_bk1)
    x, ctx_1024, mask_Bx1xSxS2_bk1 = _rec_inputs()

    def _L0_attn_setup():
        import jax, jax.numpy as jnp
        import numpy as np
        N_HEADS = 16
        EPS = 1e-06
        key = jax.random.key(seed)
        ks = jax.random.split(key, 5)
        B, N, D, H = (4, 512, 256, N_HEADS)
        x = jax.random.normal(ks[0], (B, N, D), dtype=jnp.float32)
        Wq = jax.random.normal(ks[1], (D, D), dtype=jnp.float32) * D ** (-0.5)
        Wk = jax.random.normal(ks[2], (D, D), dtype=jnp.float32) * D ** (-0.5)
        Wv = jax.random.normal(ks[3], (D, D), dtype=jnp.float32) * D ** (-0.5)
        Wo = jax.random.normal(ks[4], (D, D), dtype=jnp.float32) * D ** (-0.5)
        q_scale = jnp.ones((H,), dtype=jnp.float32)
        k_scale = jnp.ones((H,), dtype=jnp.float32)
        return {'x': x, 'Wq': Wq, 'Wk': Wk, 'Wv': Wv, 'Wo': Wo, 'q_scale': q_scale, 'k_scale': k_scale}
    _L0_attn_all = _L0_attn_setup()
    _L0_attn_in = {k: v for k, v in _L0_attn_all.items() if k in ('Wq', 'Wk', 'Wv', 'Wo', 'q_scale', 'k_scale')}
    del _L0_attn_all

    def _L0_xattn_setup():
        import jax, jax.numpy as jnp
        import numpy as np
        B, S, D, H = (4, 512, 256, 16)
        HD = D // H
        key = jax.random.key(seed)
        ks = jax.random.split(key, 12)
        scale = 1.0 / np.sqrt(D)
        inp = {'queries': jax.random.normal(ks[0], (B, S, D), jnp.float32), 'keys': jax.random.normal(ks[1], (B, S, D), jnp.float32), 'values': jax.random.normal(ks[2], (B, S, D), jnp.float32), 'mask': jax.random.randint(ks[3], (B, 1, S, S), 0, 2).astype(bool), 'Wq': jax.random.normal(ks[4], (D, D), jnp.float32) * scale, 'bq': jnp.zeros((D,), jnp.float32), 'Wk': jax.random.normal(ks[5], (D, D), jnp.float32) * scale, 'bk': jnp.zeros((D,), jnp.float32), 'Wv': jax.random.normal(ks[6], (D, D), jnp.float32) * scale, 'bv': jnp.zeros((D,), jnp.float32), 'Wo': jax.random.normal(ks[7], (D, D), jnp.float32) * scale, 'bo': jnp.zeros((D,), jnp.float32)}
        return inp
    _L0_xattn_all = _L0_xattn_setup()
    _L0_xattn_in = {k: v for k, v in _L0_xattn_all.items() if k in ('Wq', 'bq', 'Wk', 'bk', 'Wv', 'bv', 'Wo', 'bo')}
    del _L0_xattn_all

    def _L0_ffn_setup():
        import jax, jax.numpy as jnp
        import numpy as np
        E, H, I = (8, 256, 1024)
        B, S = (4, 512)
        key = jax.random.key(seed)
        k0, k1, k2, k3 = jax.random.split(key, 4)
        s = 0.02
        return {'hidden_states': jax.random.normal(k0, (B, S, H), dtype=jnp.float32), 'w1': jax.random.normal(k1, (E, H, I), dtype=jnp.float32) * s, 'b1': jnp.zeros((E, I), dtype=jnp.float32), 'w2': jax.random.normal(k2, (E, I, H), dtype=jnp.float32) * s, 'b2': jnp.zeros((E, H), dtype=jnp.float32), 'wr': jax.random.normal(k3, (H, E), dtype=jnp.float32) * s, 'br': jnp.zeros((E,), dtype=jnp.float32)}
    _L0_ffn_all = _L0_ffn_setup()
    _L0_ffn_in = {k: v for k, v in _L0_ffn_all.items() if k in ('w1', 'b1', 'w2', 'b2', 'wr', 'br')}
    del _L0_ffn_all

    def _L1_attn_setup():
        import jax, jax.numpy as jnp
        import numpy as np
        H = 256
        F = 1024
        B, S = (4, 1024)
        EPS = 1e-05

        def _layernorm(x, scale, bias):
            mu = jnp.mean(x, axis=-1, keepdims=True)
            var = jnp.var(x, axis=-1, keepdims=True)
            return (x - mu) * jax.lax.rsqrt(var + EPS) * scale + bias
        key = jax.random.key(seed)
        ks = jax.random.split(key, 4)
        x = jax.random.normal(ks[0], (B, S, H), dtype=jnp.float32)
        W_ret = jax.random.normal(ks[1], (H, H), dtype=jnp.float32) * 0.02
        b_ret = jnp.zeros((H,), dtype=jnp.float32)
        ln1_scale = jnp.ones((H,), dtype=jnp.float32)
        ln1_bias = jnp.zeros((H,), dtype=jnp.float32)
        W1 = jax.random.normal(ks[2], (H, F), dtype=jnp.float32) * 0.02
        b1 = jnp.zeros((F,), dtype=jnp.float32)
        W2 = jax.random.normal(ks[3], (F, H), dtype=jnp.float32) * 0.02
        b2 = jnp.zeros((H,), dtype=jnp.float32)
        ln2_scale = jnp.ones((H,), dtype=jnp.float32)
        ln2_bias = jnp.zeros((H,), dtype=jnp.float32)
        return {'x': x, 'W_ret': W_ret, 'b_ret': b_ret, 'ln1_scale': ln1_scale, 'ln1_bias': ln1_bias, 'W1': W1, 'b1': b1, 'W2': W2, 'b2': b2, 'ln2_scale': ln2_scale, 'ln2_bias': ln2_bias}
    _L1_attn_all = _L1_attn_setup()
    _L1_attn_in = {k: v for k, v in _L1_attn_all.items() if k in ('W_ret', 'b_ret', 'ln1_scale', 'ln1_bias', 'W1', 'b1', 'W2', 'b2', 'ln2_scale', 'ln2_bias')}
    del _L1_attn_all

    def _L1_xattn_setup():
        import jax, jax.numpy as jnp
        import numpy as np
        D_MODEL = 256
        N_HEADS = 16
        D_K = D_MODEL // N_HEADS
        key = jax.random.key(seed)
        ks = jax.random.split(key, 11)
        B, L, S = (2, 512, 512)
        scale = 1.0 / np.sqrt(D_MODEL)
        return {'x_q': jax.random.normal(ks[0], (B, L, D_MODEL), jnp.float32), 'x_k': jax.random.normal(ks[1], (B, S, D_MODEL), jnp.float32), 'x_v': jax.random.normal(ks[2], (B, S, D_MODEL), jnp.float32), 'W_Q': jax.random.normal(ks[3], (D_MODEL, D_MODEL), jnp.float32) * scale, 'b_Q': jax.random.normal(ks[4], (D_MODEL,), jnp.float32) * 0.01, 'W_K': jax.random.normal(ks[5], (D_MODEL, D_MODEL), jnp.float32) * scale, 'b_K': jax.random.normal(ks[6], (D_MODEL,), jnp.float32) * 0.01, 'W_V': jax.random.normal(ks[7], (D_MODEL, D_MODEL), jnp.float32) * scale, 'b_V': jax.random.normal(ks[8], (D_MODEL,), jnp.float32) * 0.01, 'W_O': jax.random.normal(ks[9], (D_MODEL, D_MODEL), jnp.float32) * scale, 'b_O': jax.random.normal(ks[10], (D_MODEL,), jnp.float32) * 0.01}
    _L1_xattn_all = _L1_xattn_setup()
    _L1_xattn_in = {k: v for k, v in _L1_xattn_all.items() if k in ('W_Q', 'b_Q', 'W_K', 'b_K', 'W_V', 'b_V', 'W_O', 'b_O')}
    del _L1_xattn_all

    def _L1_ffn_setup():
        import jax, jax.numpy as jnp
        import numpy as np
        EPS = 1e-08
        key = jax.random.key(seed)
        kx, kw = jax.random.split(key)
        x = jax.random.normal(kx, (8, 1024, 256), dtype=jnp.float32)
        weight = jax.random.normal(kw, (256, 256), dtype=jnp.float32) * (1.0 / np.sqrt(256))
        return {'x': x, 'weight': weight}
    _L1_ffn_all = _L1_ffn_setup()
    _L1_ffn_in = {k: v for k, v in _L1_ffn_all.items() if k in ('weight',)}
    del _L1_ffn_all
    return {'x': x, 'ctx_1024': ctx_1024, 'mask_Bx1xSxS2_bk1': mask_Bx1xSxS2_bk1, 'L0_attn_Wq': _L0_attn_in['Wq'], 'L0_attn_Wk': _L0_attn_in['Wk'], 'L0_attn_Wv': _L0_attn_in['Wv'], 'L0_attn_Wo': _L0_attn_in['Wo'], 'L0_attn_q_scale': _L0_attn_in['q_scale'], 'L0_attn_k_scale': _L0_attn_in['k_scale'], 'L0_xattn_Wq': _L0_xattn_in['Wq'], 'L0_xattn_bq': _L0_xattn_in['bq'], 'L0_xattn_Wk': _L0_xattn_in['Wk'], 'L0_xattn_bk': _L0_xattn_in['bk'], 'L0_xattn_Wv': _L0_xattn_in['Wv'], 'L0_xattn_bv': _L0_xattn_in['bv'], 'L0_xattn_Wo': _L0_xattn_in['Wo'], 'L0_xattn_bo': _L0_xattn_in['bo'], 'L0_ffn_w1': _L0_ffn_in['w1'], 'L0_ffn_b1': _L0_ffn_in['b1'], 'L0_ffn_w2': _L0_ffn_in['w2'], 'L0_ffn_b2': _L0_ffn_in['b2'], 'L0_ffn_wr': _L0_ffn_in['wr'], 'L0_ffn_br': _L0_ffn_in['br'], 'L1_attn_W_ret': _L1_attn_in['W_ret'], 'L1_attn_b_ret': _L1_attn_in['b_ret'], 'L1_attn_ln1_scale': _L1_attn_in['ln1_scale'], 'L1_attn_ln1_bias': _L1_attn_in['ln1_bias'], 'L1_attn_W1': _L1_attn_in['W1'], 'L1_attn_b1': _L1_attn_in['b1'], 'L1_attn_W2': _L1_attn_in['W2'], 'L1_attn_b2': _L1_attn_in['b2'], 'L1_attn_ln2_scale': _L1_attn_in['ln2_scale'], 'L1_attn_ln2_bias': _L1_attn_in['ln2_bias'], 'L1_xattn_W_Q': _L1_xattn_in['W_Q'], 'L1_xattn_b_Q': _L1_xattn_in['b_Q'], 'L1_xattn_W_K': _L1_xattn_in['W_K'], 'L1_xattn_b_K': _L1_xattn_in['b_K'], 'L1_xattn_W_V': _L1_xattn_in['W_V'], 'L1_xattn_b_V': _L1_xattn_in['b_V'], 'L1_xattn_W_O': _L1_xattn_in['W_O'], 'L1_xattn_b_O': _L1_xattn_in['b_O'], 'L1_ffn_weight': _L1_ffn_in['weight']}

def reference(x, ctx_1024, mask_Bx1xSxS2_bk1, L0_attn_Wq, L0_attn_Wk, L0_attn_Wv, L0_attn_Wo, L0_attn_q_scale, L0_attn_k_scale, L0_xattn_Wq, L0_xattn_bq, L0_xattn_Wk, L0_xattn_bk, L0_xattn_Wv, L0_xattn_bv, L0_xattn_Wo, L0_xattn_bo, L0_ffn_w1, L0_ffn_b1, L0_ffn_w2, L0_ffn_b2, L0_ffn_wr, L0_ffn_br, L1_attn_W_ret, L1_attn_b_ret, L1_attn_ln1_scale, L1_attn_ln1_bias, L1_attn_W1, L1_attn_b1, L1_attn_W2, L1_attn_b2, L1_attn_ln2_scale, L1_attn_ln2_bias, L1_xattn_W_Q, L1_xattn_b_Q, L1_xattn_W_K, L1_xattn_b_K, L1_xattn_W_V, L1_xattn_b_V, L1_xattn_W_O, L1_xattn_b_O, L1_ffn_weight):
    import jax
    import jax.numpy as jnp

    def _L0_attn_ref(x, Wq, Wk, Wv, Wo, q_scale, k_scale):
        import jax, jax.numpy as jnp
        import numpy as np
        N_HEADS = 16
        EPS = 1e-06
        B, N, D = x.shape
        H = N_HEADS
        hd = D // H
        q = jax.nn.silu(x @ Wq.T)
        k = jax.nn.silu(x @ Wk.T)
        v = jax.nn.silu(x @ Wv.T)
        q = q.reshape(B, N, H, hd).transpose(0, 2, 1, 3)
        k = k.reshape(B, N, H, hd).transpose(0, 2, 1, 3)
        v = v.reshape(B, N, H, hd).transpose(0, 2, 1, 3)
        r_q = jnp.linalg.norm(q, axis=-1, keepdims=True)
        r_k = jnp.linalg.norm(k, axis=-1, keepdims=True)
        q_dir = q / (r_q + EPS)
        k_dir = k / (r_k + EPS)
        scores = jnp.einsum('bhnd,bhmd->bhnm', q_dir, k_dir)
        sq = q_scale[None, :, None, None]
        sk = k_scale[None, :, None, None]
        scores = scores * (r_q * sq) * (jnp.swapaxes(r_k, -2, -1) * sk)
        mask = jnp.tril(jnp.ones((N, N), dtype=bool))
        scores = jnp.where(mask, scores, -jnp.inf)
        probs = jax.nn.softmax(scores, axis=-1)
        out = jnp.einsum('bhnm,bhmd->bhnd', probs, v)
        out = out.transpose(0, 2, 1, 3).reshape(B, N, D)
        return out @ Wo.T

    def _L0_xattn_ref(queries, keys, values, mask, Wq, bq, Wk, bk, Wv, bv, Wo, bo):
        import jax, jax.numpy as jnp
        import numpy as np
        B, S, D, H = (4, 512, 256, 16)
        HD = D // H
        b, sq, d = queries.shape

        def split_heads(x):
            return x.reshape(b, x.shape[1], H, HD).transpose(0, 2, 1, 3)
        q = split_heads(queries @ Wq + bq)
        k = split_heads(keys @ Wk + bk)
        v = split_heads(values @ Wv + bv)
        scores = jnp.einsum('bhqd,bhkd->bhqk', q, k) / jnp.sqrt(jnp.float32(HD))
        scores = jnp.where(mask, jnp.float32(-1000000000000000.0), scores)
        attn = jax.nn.softmax(scores, axis=-1)
        ctx = jnp.einsum('bhqk,bhkd->bhqd', attn, v)
        ctx = ctx.transpose(0, 2, 1, 3).reshape(b, sq, d)
        return ctx @ Wo + bo

    def _L0_ffn_ref(hidden_states, w1, b1, w2, b2, wr, br):
        import jax, jax.numpy as jnp
        import numpy as np
        E, H, I = (8, 256, 1024)
        B, S = (4, 512)
        b, s, h = hidden_states.shape
        x = hidden_states.reshape(-1, h)
        logits = x @ wr + br
        probs = jax.nn.softmax(logits, axis=-1)
        top_p, top_i = jax.lax.top_k(probs, 2)
        gate = top_p[:, 0] / (top_p[:, 0] + top_p[:, 1])
        top1 = top_i[:, 0]
        out = jnp.zeros_like(x)
        n_experts = w1.shape[0]
        for e in range(n_experts):
            hmid = jax.nn.gelu(x @ w1[e] + b1[e], approximate=False)
            hout = hmid @ w2[e] + b2[e]
            mask = top1 == e
            out = out + jnp.where(mask[:, None], hout * gate[:, None], 0.0)
        return out.reshape(b, s, h)

    def _L1_attn_ref(x, W_ret, b_ret, ln1_scale, ln1_bias, W1, b1, W2, b2, ln2_scale, ln2_bias):
        import jax, jax.numpy as jnp
        import numpy as np
        H = 256
        F = 1024
        B, S = (4, 1024)
        EPS = 1e-05

        def _layernorm(x, scale, bias):
            mu = jnp.mean(x, axis=-1, keepdims=True)
            var = jnp.var(x, axis=-1, keepdims=True)
            return (x - mu) * jax.lax.rsqrt(var + EPS) * scale + bias
        sig = jax.nn.sigmoid(jnp.einsum('bsh,hk->bsk', x, W_ret) + b_ret)

        def ema_step(carry, s_t):
            xi = 0.5 * s_t + 0.5 * carry
            return (xi, xi)
        _, ret = jax.lax.scan(ema_step, jnp.zeros((x.shape[0], x.shape[2]), x.dtype), jnp.transpose(sig, (1, 0, 2)))
        retention_output = jnp.transpose(ret, (1, 0, 2))
        h = _layernorm(x + retention_output, ln1_scale, ln1_bias)
        ffn = jnp.einsum('bsf,fh->bsh', jax.nn.gelu(jnp.einsum('bsh,hf->bsf', h, W1) + b1), W2) + b2
        out = _layernorm(h + ffn, ln2_scale, ln2_bias)
        return out

    def _L1_xattn_ref(x_q, x_k, x_v, W_Q, b_Q, W_K, b_K, W_V, b_V, W_O, b_O):
        import jax, jax.numpy as jnp
        import numpy as np
        D_MODEL = 256
        N_HEADS = 16
        D_K = D_MODEL // N_HEADS
        B, L, _ = x_q.shape
        S = x_k.shape[1]
        H, dk = (N_HEADS, D_K)
        Q = (x_q @ W_Q + b_Q).reshape(B, L, H, dk).transpose(0, 2, 1, 3)
        K = (x_k @ W_K + b_K).reshape(B, S, H, dk).transpose(0, 2, 1, 3)
        V = (x_v @ W_V + b_V).reshape(B, S, H, dk).transpose(0, 2, 1, 3)
        scores = jnp.einsum('bhld,bhsd->bhls', Q, K) / jnp.sqrt(jnp.float32(dk))
        attn = jax.nn.softmax(scores, axis=-1)
        ctx = jnp.einsum('bhls,bhsd->bhld', attn, V)
        ctx = ctx.transpose(0, 2, 1, 3).reshape(B, L, H * dk)
        out = ctx @ W_O + b_O
        return out

    def _L1_ffn_ref(x, weight):
        import jax, jax.numpy as jnp
        import numpy as np
        EPS = 1e-08
        w_scale = jnp.mean(jnp.abs(weight)) + EPS
        u = weight / w_scale
        w_quant = u + jax.lax.stop_gradient(jnp.clip(jnp.round(u), -1.0, 1.0) - u)
        a_scale = jnp.max(jnp.abs(x), axis=-1, keepdims=True) + EPS
        z = jnp.clip(x / a_scale * 127.0, -128.0, 127.0)
        a_quant = z + jax.lax.stop_gradient(jnp.round(z) - z)
        y = jnp.einsum('bsi,oi->bso', a_quant, w_quant)
        y = y * (w_scale * a_scale / 127.0)
        return y
    x = x + _L0_attn_ref(_layernorm(x, axis=-1), L0_attn_Wq, L0_attn_Wk, L0_attn_Wv, L0_attn_Wo, L0_attn_q_scale, L0_attn_k_scale)
    x = x + _L0_xattn_ref(_layernorm(x, axis=-1), ctx_1024, ctx_1024, mask_Bx1xSxS2_bk1, L0_xattn_Wq, L0_xattn_bq, L0_xattn_Wk, L0_xattn_bk, L0_xattn_Wv, L0_xattn_bv, L0_xattn_Wo, L0_xattn_bo)
    x = x + _L0_ffn_ref(_layernorm(x, axis=-1), L0_ffn_w1, L0_ffn_b1, L0_ffn_w2, L0_ffn_b2, L0_ffn_wr, L0_ffn_br)
    x = x + _L1_attn_ref(_layernorm(x, axis=-1), L1_attn_W_ret, L1_attn_b_ret, L1_attn_ln1_scale, L1_attn_ln1_bias, L1_attn_W1, L1_attn_b1, L1_attn_W2, L1_attn_b2, L1_attn_ln2_scale, L1_attn_ln2_bias)
    x = x + _L1_xattn_ref(_layernorm(x, axis=-1), ctx_1024, ctx_1024, L1_xattn_W_Q, L1_xattn_b_Q, L1_xattn_W_K, L1_xattn_b_K, L1_xattn_W_V, L1_xattn_b_V, L1_xattn_W_O, L1_xattn_b_O)
    x = x + _L1_ffn_ref(_layernorm(x, axis=-1), L1_ffn_weight)
    return x

_drawn_inputs = setup_inputs


def setup_inputs(seed=0):
    import zlib

    import numpy as np

    out = dict(_drawn_inputs(seed))
    spreads = {'L0_attn_q_scale': (1.0, 0.2),
     'L0_attn_k_scale': (1.0, 0.2),
     'L0_xattn_bq': (0.0, 0.345),
     'L0_xattn_bk': (0.0, 2.0),
     'L0_xattn_bv': (0.0, 0.1),
     'L0_xattn_bo': (0.0, 0.1),
     'L0_ffn_b1': (0.0, 0.481),
     'L0_ffn_b2': (0.0, 0.1),
     'L0_ffn_br': (0.0, 0.1),
     'L1_attn_b_ret': (0.0, 0.658),
     'L1_attn_ln1_scale': (1.0, 0.2),
     'L1_attn_ln1_bias': (0.0, 0.1),
     'L1_attn_b1': (0.0, 0.519),
     'L1_attn_b2': (0.0, 0.1),
     'L1_attn_ln2_scale': (1.0, 0.2),
     'L1_attn_ln2_bias': (0.0, 0.1)}
    factors = {'L1_xattn_b_Q': 60.199, 'L1_xattn_b_K': 64.0, 'L1_xattn_b_V': 8.0, 'L1_xattn_b_O': 8.0}
    for name, (base, spread) in spreads.items():
        noise = np.random.default_rng([zlib.crc32(name.encode()), seed]).standard_normal(out[name].shape)
        drawn = base * np.exp(spread * noise) if base else spread * noise
        out[name] = jnp.asarray(drawn.astype(out[name].dtype))
    for name, factor in factors.items():
        out[name] = (out[name] * factor).astype(out[name].dtype)
    return out
```

```python
import concourse.bass as bass
from concourse import mybir
from concourse.alu_op_type import AluOpType as ALU
from contextlib import ExitStack

F32 = mybir.dt.float32
BF16 = mybir.dt.bfloat16
U8 = mybir.dt.uint8
U32 = mybir.dt.uint32
I32 = mybir.dt.int32
ACT = mybir.ActivationFunctionType
AX = mybir.AxisListType
ds = bass.ds

P = 128
B, N, D, H = 8, 512, 256, 16
HD = D // H
TB = N // P
NT = B * TB
KC = D // P
F = 1024
FC = F // P
E = 8
VW = 32
REP = 6
SROWS = REP * HD
MROWS = SROWS + 3
Q_REPS = [(0, 0), (1, 0), (2, 0), (3, 1), (4, 1), (5, 2)]
K_REPS = [(0, 0), (1, 1), (2, 2), (3, 0), (4, 1), (5, 0)]
NEG = -float(2 ** 50)
NEG_CAUSAL = -float(2 ** 100)
QUADS = H // 4
STEPS = QUADS * TB
UNITS = H * TB
ALLX = (0, 1)


SEM_BASE, SEM_BANK = 99, 72


class Phase:

    def __init__(self, k, tag):
        self.k, self.nc, self.tag = k, k.nc, tag
        self.ctx, self.sems = ExitStack(), {}
        self.low = SEM_BASE + SEM_BANK * (k.phases % 2)
        self.others = range(SEM_BASE + SEM_BANK * ((k.phases + 1) % 2), SEM_BASE + SEM_BANK * ((k.phases + 1) % 2) + SEM_BANK)
        self.clears = k.phases > 0
        k.phases += 1

    def __enter__(self):
        return self

    def __exit__(self, *e):
        self.ctx.close()

    def sb(self, name, shape, dt=F32):
        return self.ctx.enter_context(self.nc.sbuf_tensor(f"{self.tag}_{name}", shape, dt))

    def two(self, name, shape, dt=F32):
        return [self.sb(f"{name}{p}", shape, dt) for p in ALLX]

    def banks(self):
        return [self.ctx.enter_context(self.nc.psum_tensor(f"{self.tag}_bank{i}", [P, 512], F32)) for i in range(8)]

    def sem(self, name):
        if name not in self.sems:
            assert len(self.sems) < SEM_BANK
            self.sems[name] = self.ctx.enter_context(self.nc.semaphore(f"{self.tag}_{name}", num=self.low + len(self.sems)))
        return self.sems[name]

    def pair(self, name):
        return [self.sem(f"{name}_even"), self.sem(f"{name}_odd")]

    def own_sem(self, name):
        return self.ctx.enter_context(self.nc.semaphore(f"{self.tag}_{name}", num=self.k.next_own_sem()))

    def clear_others(self, pool):
        if self.clears:
            pool.sem_clear(self.others)


class Kernel:

    def __init__(self, nc, ctx):
        self.nc, self.ctx, self.phases, self.own_sems = nc, ctx, 0, 0

    def next_own_sem(self):
        self.own_sems += 1
        return SEM_BASE + 2 * SEM_BANK + self.own_sems - 1


def batches(eng):
    for par in ALLX:
        yield 0, par, par
    with eng.Fori(1, B // 2) as it:
        for par in ALLX:
            yield it, par, it * 2 + par


def wait_apart(ph, eng, sem, value):
    eng.wait_ge(sem, value)
    eng.sem_inc(ph.sem("waits_passed"), 1)


def before(pair, it, par, each):
    return (pair[0], it * each + each) if par else (pair[1], it * each)


def phase_start(k, x_dram):
    nc = k.nc
    ph = Phase(k, "start")
    sb = lambda name, shape, dt: k.ctx.enter_context(nc.sbuf_tensor(name, shape, dt))
    k.x = sb("x_res", [P, NT, D], F32)
    k.ident = sb("ident", [P, P], F32)
    k.minus_half = sb("minus_half", [P, TB], F32)
    loaded, made = ph.sem("x_loaded"), ph.sem("const_made")
    with nc.Block() as block:
        @block.sync
        def _(sp):
            sp.dma_start(k.x[:, :, :], x_dram.rearrange("b (i p) d -> p (b i) d", p=P)).then_inc(loaded, 16)
            sp.wait_ge(loaded, 16)

        @block.gpsimd
        def _(pool):
            nc.gpsimd.memset(k.minus_half[:, :], -0.5).then_inc(made, 1)
            nc.gpsimd.memset(k.ident[:, :], 0.0).then_inc(made, 1)
            pool.wait_ge(made, 2)
            nc.gpsimd.affine_select(out=k.ident[:, :], in_=k.ident[:, :], compare_op=ALU.not_equal, fill=1.0,
                                    base=0, pattern=[[-1, P]], channel_multiplier=1).then_inc(made, 1)
            pool.wait_ge(made, 3)
    ph.ctx.close()


class Norm:

    def __init__(self, ph, tag, eps):
        self.ph, self.nc, self.k, self.eps = ph, ph.nc, ph.k, eps
        self.stats = ph.two(f"{tag}_stats", [P, TB, 6])
        self.mv = ph.two(f"{tag}_mean_var", [P, TB, 2])
        self.ve = ph.two(f"{tag}_var_eps", [P, TB])
        self.rstd = ph.two(f"{tag}_rstd", [P, TB])
        self.s_stats, self.s_mv = ph.pair(f"{tag}_stats"), ph.pair(f"{tag}_mean_var")
        self.s_ve, self.s_rstd = ph.pair(f"{tag}_var_eps"), ph.pair(f"{tag}_rstd")

    def statistics(self, dve, par, n, src):
        nc = self.nc
        for i in range(TB):
            nc.vector.bn_stats(self.stats[par][:, i, :], src(i)).then_inc(self.s_stats[par], 1)
        wait_apart(self.ph, dve, self.s_stats[par], n * TB + TB)
        for i in range(TB):
            nc.vector.bn_aggr(self.mv[par][:, i, :], self.stats[par][:, i, :]).then_inc(self.s_mv[par], 1)
        dve.wait_ge(self.s_mv[par], n * TB + TB)
        nc.vector.tensor_scalar_add(self.ve[par][:, :], self.mv[par][:, :, 1], self.eps).then_inc(self.s_ve[par], 1)

    def power(self, pool, par, n):
        pool.wait_ge(self.s_ve[par], n + 1)
        self.nc.gpsimd.tensor_tensor(self.rstd[par][:, :], self.ve[par][:, :], self.k.minus_half[:, :],
                                     ALU.pow).then_inc(self.s_rstd[par], 1)

    def apply(self, dve, par, n, src, dst, done):
        dve.wait_ge(self.s_rstd[par], n + 1)
        for i in range(TB):
            self.nc.vector.tensor_scalar(dst(i), src(i), self.mv[par][:, i, 0:1], self.rstd[par][:, i:i + 1],
                                         ALU.subtract, ALU.mult).then_inc(done, 1)


EPS_X = 1e-5
EPS_NORM = 1e-6
QK4 = [(0, 0), (0, 1), (1, 0), (1, 1)]


def rows(w_dram):
    return w_dram.rearrange("(c p) n -> p c n", p=P)


def over_partitions(row):
    return row.rearrange("(a n) -> a n", a=1).broadcast_to((P, row.shape[0]))


def phase_project(k, tag, w, ctx_dram=None):
    nc, own = k.nc, ctx_dram is None
    with Phase(k, tag) as ph:
        ps = ph.banks()
        wq, wk, wv = (ph.sb(x, [P, KC, D]) for x in ("wq", "wk", "wv"))
        small = ph.sb("small", [P, 4])
        norm = Norm(ph, "ln", EPS_X)
        xn, xnT = ph.two("xn", [P, TB, D]), ph.two("xnT", [P, KC, N])
        qk = [[ph.sb(f"qk{s}{m}", [P, N]) for m in range(KC)] for s in range(2)]
        rest = [[ph.sb(f"rest{s}{m}", [P, N]) for m in range(KC)] for s in range(2)]
        parts = ph.two("parts", [P, 2, KC, 3, N], BF16)
        vst = ph.two("v", [P, TB, H, VW])
        if own:
            work = [[ph.sb(f"work{s}{m}", [P, N]) for m in range(KC)] for s in range(2)]
            root = [[ph.sb(f"root{s}{m}", [P, N]) for m in range(KC)] for s in range(2)]
            same_head = ph.sb("same_head", [P, P])
            s_sq, s_n2, s_rt = ph.pair("square"), ph.pair("norm2"), ph.pair("root")
            s_den, s_rec, s_fac, s_sc = (ph.pair(x) for x in ("denominator", "reciprocal", "factor", "scaled"))
        else:
            cx, cxT = ph.two("cx", [P, TB, D]), ph.two("cxT", [P, KC, N])
            bv = ph.sb("bv", [P, D])
            s_cx, s_cT, s_cxT = ph.pair("ctx_loaded"), ph.pair("ctx_turned"), ph.pair("ctxT")
        s_w, s_zero, s_ones, s_same = (ph.sem(x) for x in ("weights", "v_zeroed", "v_ones", "same_head"))
        s_xn, s_xT, s_xnT = ph.pair("xn"), ph.pair("x_turned"), ph.pair("xnT")
        s_mm, s_ev = ph.pair("qk_product"), ph.pair("qk_out")
        s_vm, s_vev = ph.pair("v_product"), ph.pair("v_out")
        s_hi, s_rest, s_mid, s_lo = ph.pair("high"), ph.pair("rest"), ph.pair("middle"), ph.pair("low")
        s_st = ph.pair("stored")
        w_all = 16 * (4 if own else 5)
        with nc.Block() as block:
            @block.sync
            def _(sp):
                for dst, src in ((wq, w["q"]), (wk, w["k"]), (wv, w["v"])):
                    sp.dma_start(dst[:, :, :], rows(src)).then_inc(s_w, 16)
                if own:
                    sp.dma_start(small[:, :], w["factors"]).then_inc(s_w, 16)
                else:
                    sp.dma_start(small[:, :], w["bqk"]).then_inc(s_w, 16)
                    sp.dma_start(bv[:, :], over_partitions(w["bv"])).then_inc(s_w, 16)
                for it, par, b in batches(sp):
                    if not own:
                        sp.wait_ge(s_cT[par], it)
                        sp.dma_start(cx[par][:, :, :], ctx_dram[ds(b, 1)].rearrange("b (i p) d -> p (b i) d", p=P)
                                     ).then_inc(s_cx[par], 16)
                    for made in (s_hi, s_mid, s_lo):
                        sp.wait_ge(made[par], it * 4 + 4)
                    for s, m in QK4:
                        sp.dma_start(k.split[ds(b, 1), s, :, m * P:(m + 1) * P, :].rearrange("b c p t -> p (b c) t"),
                                     parts[par][:, s, m, :, :]).then_inc(s_st[par], 16)
                    sp.wait_ge(s_vev[par], it * 4 + 4)
                    sp.dma_start(k.values[ds(b, 1)].rearrange("b (i p) f -> p (b i) f", p=P),
                                 vst[par][:, :, :, :].rearrange("p i h w -> p i (h w)")).then_inc(s_st[par], 16)
                for par in ALLX:
                    sp.wait_ge(s_st[par], B // 2 * 80)

            @block.gpsimd
            def _(pool):
                ph.clear_others(pool)
                for p in ALLX:
                    nc.gpsimd.memset(vst[p][:, :, :, :], 0.0).then_inc(s_zero, 1)
                if own:
                    nc.gpsimd.memset(same_head[:, :], 1.0).then_inc(s_same, 1)
                    pool.wait_ge(s_same, 1)
                    view = same_head[:, :].rearrange("p (h e) -> p h e", e=HD)
                    nc.gpsimd.affine_select(out=view, in_=view, compare_op=ALU.is_ge, fill=0.0, base=0,
                                            pattern=[[-HD, P // HD], [0, HD]], channel_multiplier=1).then_inc(s_same, 1)
                    pool.wait_ge(s_same, 2)
                    nc.gpsimd.affine_select(out=view, in_=view, compare_op=ALU.is_ge, fill=0.0, base=HD - 1,
                                            pattern=[[HD, P // HD], [0, HD]], channel_multiplier=-1).then_inc(s_same, 1)
                for it, par, b in batches(pool):
                    norm.power(pool, par, it)
                    if own:
                        for j, (s, m) in enumerate(QK4):
                            pool.wait_ge(*before(s_fac, it, par, 4))
                            pool.wait_ge(s_ev[par], it * 4 + j + 1)
                            nc.gpsimd.tensor_tensor(work[s][m][:, :], qk[s][m][:, :], qk[s][m][:, :],
                                                    ALU.mult).then_inc(s_sq[par], 1)
                    for j, (s, m) in enumerate(QK4):
                        pool.wait_ge(s_rest[par], it * 4 + j + 1)
                        pool.wait_ge(s_mid[par], it * 4 + j + 1)
                        nc.gpsimd.tensor_tensor(parts[par][:, s, m, 2, :], rest[s][m][:, :], parts[par][:, s, m, 1, :],
                                                ALU.subtract).then_inc(s_lo[par], 1)

            @block.tensor
            def _(pe):
                pe.wait_ge(s_w, w_all)
                if own:
                    pe.wait_ge(s_same, 3)
                for it, par, b in batches(pe):
                    pe.wait_ge(s_xn[par], it * TB + TB)
                    pe.wait_ge(*before(s_xnT, it, par, KC))
                    for c in range(KC):
                        for i in range(TB):
                            last = nc.tensor.transpose(ps[c][:, i * P:(i + 1) * P], xn[par][:, i, c * P:(c + 1) * P], k.ident[:, :])
                    last.then_inc(s_xT[par], 1)
                    pe.wait_ge(*before(s_vev, it, par, 4))
                    if not own:
                        pe.wait_ge(s_cx[par], it * 16 + 16)
                        for c in range(KC):
                            for i in range(TB):
                                last = nc.tensor.transpose(ps[6 + c][:, i * P:(i + 1) * P], cx[par][:, i, c * P:(c + 1) * P], k.ident[:, :])
                        last.then_inc(s_cT[par], 1)
                    pe.wait_ge(s_xnT[par], it * KC + KC)
                    pe.wait_ge(*before(s_rt if own else s_ev, it, par, 4))
                    for j, (s, m) in enumerate(QK4):
                        src, ww = (xnT, wq) if s == 0 else (xnT if own else cxT, wk)
                        if j == 2 and not own:
                            pe.wait_ge(s_cxT[par], it * KC + KC)
                        for c in range(KC):
                            last = nc.tensor.matmul(ps[2 + j][:, :], ww[:, c, m * P:(m + 1) * P], src[par][:, c, :],
                                                    start=(c == 0), stop=(c == KC - 1))
                        last.then_inc(s_mm[par], 1)
                    src = xnT if own else cxT
                    for i in range(TB):
                        for c in range(KC):
                            last = nc.tensor.matmul(ps[6 + i // 2][:, (i % 2) * D:(i % 2 + 1) * D], src[par][:, c, i * P:(i + 1) * P],
                                                    wv[:, c, :], start=(c == 0), stop=(c == KC - 1))
                        if i % 2:
                            last.then_inc(s_vm[par], 1)
                    if own:
                        for j, (s, m) in enumerate(QK4):
                            pe.wait_ge(s_sq[par], it * 4 + j + 1)
                            nc.tensor.matmul(ps[2 + j][:, :], same_head[:, :], work[s][m][:, :], start=True, stop=True
                                             ).then_inc(s_n2[par], 1)

            @block.scalar
            def _(act):
                act.wait_ge(s_w, w_all)
                act.wait_ge(s_zero, 2)
                for it, par, b in batches(act):
                    act.wait_ge(s_xT[par], it + 1)
                    act.wait_ge(s_vm[par], it * 2)
                    for c in range(KC):
                        nc.scalar.activation(xnT[par][:, c, :], ps[c][:, :], ACT.Copy).then_inc(s_xnT[par], 1)
                    if not own:
                        act.wait_ge(s_cT[par], it + 1)
                        for c in range(KC):
                            nc.scalar.activation(cxT[par][:, c, :], ps[6 + c][:, :], ACT.Copy).then_inc(s_cxT[par], 1)
                    act.wait_ge(*before(s_rest, it, par, 4))
                    for j, (s, m) in enumerate(QK4):
                        act.wait_ge(s_mm[par], it * 4 + j + 1)
                        if own:
                            nc.scalar.activation(qk[s][m][:, :], ps[2 + j][:, :], ACT.Silu).then_inc(s_ev[par], 1)
                        else:
                            nc.scalar.activation(qk[s][m][:, :], ps[2 + j][:, :], ACT.Identity,
                                                 bias=small[:, j:j + 1]).then_inc(s_ev[par], 1)
                    act.wait_ge(s_st[par], it * 80)
                    if own:
                        for i in range(TB):
                            act.wait_ge(s_vm[par], it * 2 + i // 2 + 1)
                            nc.scalar.activation(vst[par][:, i, :, 0:HD],
                                                 ps[6 + i // 2][:, (i % 2) * D:(i % 2 + 1) * D].rearrange("p (h e) -> p h e", e=HD),
                                                 ACT.Silu).then_inc(s_vev[par], 1)
                        for j, (s, m) in enumerate(QK4):
                            act.wait_ge(s_n2[par], it * 4 + j + 1)
                            nc.scalar.activation(root[s][m][:, :], ps[2 + j][:, :], ACT.Sqrt).then_inc(s_rt[par], 1)
                    for j, (s, m) in enumerate(QK4):
                        act.wait_ge(s_sc[par] if own else s_ev[par], it * 4 + j + 1)
                        nc.scalar.activation(parts[par][:, s, m, 0, :], qk[s][m][:, :], ACT.Copy).then_inc(s_hi[par], 1)
                    for j, (s, m) in enumerate(QK4):
                        act.wait_ge(s_rest[par], it * 4 + j + 1)
                        nc.scalar.activation(parts[par][:, s, m, 1, :], rest[s][m][:, :], ACT.Copy).then_inc(s_mid[par], 1)

            @block.vector
            def _(dve):
                dve.wait_ge(s_w, w_all)
                dve.wait_ge(s_zero, 2)
                for p in ALLX:
                    nc.vector.memset(vst[p][:, :, :, HD:HD + 1], 1.0).then_inc(s_ones, 1)
                for it, par, b in batches(dve):
                    src = lambda i: k.x[:, ds(b * TB + i, 1), :].rearrange("p a d -> p (a d)")
                    norm.statistics(dve, par, it, src)
                    dve.wait_ge(s_xT[par], it)
                    norm.apply(dve, par, it, src, lambda i: xn[par][:, i, :], s_xn[par])
                    if own:
                        for j, (s, m) in enumerate(QK4):
                            dve.wait_ge(s_rt[par], it * 4 + j + 1)
                            nc.vector.tensor_scalar_add(work[s][m][:, :], root[s][m][:, :], EPS_NORM).then_inc(s_den[par], 1)
                            dve.wait_ge(s_den[par], it * 4 + j + 1)
                            nc.vector.reciprocal(work[s][m][:, :], work[s][m][:, :]).then_inc(s_rec[par], 1)
                            dve.wait_ge(s_rec[par], it * 4 + j + 1)
                            nc.vector.scalar_tensor_tensor(out=root[s][m][:, :], in0=work[s][m][:, :], scalar=small[:, j:j + 1],
                                                           in1=root[s][m][:, :], op0=ALU.mult, op1=ALU.mult).then_inc(s_fac[par], 1)
                            dve.wait_ge(s_fac[par], it * 4 + j + 1)
                            nc.vector.tensor_tensor(qk[s][m][:, :], qk[s][m][:, :], root[s][m][:, :], ALU.mult).then_inc(s_sc[par], 1)
                    else:
                        dve.wait_ge(s_st[par], it * 80)
                        for i in range(TB):
                            dve.wait_ge(s_vm[par], it * 2 + i // 2 + 1)
                            nc.vector.tensor_tensor(vst[par][:, i, :, 0:HD],
                                                    ps[6 + i // 2][:, (i % 2) * D:(i % 2 + 1) * D].rearrange("p (h e) -> p h e", e=HD),
                                                    bv[:, :].rearrange("p (h e) -> p h e", e=HD), ALU.add).then_inc(s_vev[par], 1)
                    dve.wait_ge(*before(s_lo, it, par, 4))
                    for j, (s, m) in enumerate(QK4):
                        dve.wait_ge(s_hi[par], it * 4 + j + 1)
                        nc.vector.tensor_tensor(rest[s][m][:, :], qk[s][m][:, :], parts[par][:, s, m, 0, :],
                                                ALU.subtract).then_inc(s_rest[par], 1)


def phase_core(k, tag, scale, causal=False, mask=None):
    nc = k.nc
    with Phase(k, tag) as ph:
        p_ctx = ph.ctx
        s_bank = [p_ctx.enter_context(nc.psum_tensor(f"{tag}_s{j}", [P, N], F32)) for j in range(2)]
        t_bank = [p_ctx.enter_context(nc.psum_tensor(f"{tag}_t{j}", [P, 2, N], F32)) for j in range(2)]
        o_bank = p_ctx.enter_context(nc.psum_tensor(f"{tag}_o", [P, N], F32))
        m_bank = p_ctx.enter_context(nc.psum_tensor(f"{tag}_m", [P, N], F32))
        qs, ks = ph.two("qs", [P, H, N], BF16), ph.two("ks", [P, H, N], BF16)
        vs = ph.two("vs", [P, TB, H * VW])
        probs = ph.two("probs", [P, 4, N])
        rowmax = ph.two("rowmax", [P, TB, H])
        scratch = ph.two("scratch", [P, N])
        negmax, negrest = ph.sb("negmax", [H // 2, N]), ph.sb("negrest", [H // 2, N])
        negpart = ph.two("negpart", [H // 2, 3, N], BF16)
        turned = ph.two("turned", [P, N])
        recip = ph.sb("recip", [P, 4 * TB])
        attn = ph.two("attn", [P, TB, D])
        masked = causal or mask is not None
        neg = NEG_CAUSAL if causal else NEG
        if masked:
            neg_ident = ph.sb("neg_ident", [P, P], BF16)
        if causal:
            ahead_k = ph.sb("ahead_k", [P, P], BF16)
            ahead_q = ph.sb("ahead_q", [P, N])
        if mask is not None:
            raw_q, raw_k = ph.two("raw_q", [P, TB, N], U8), ph.two("raw_k", [P, TB, N], U8)
            add_q, one_k = ph.two("add_q", [P, TB, N], BF16), ph.two("one_k", [P, TB, N], BF16)
            s_raw, s_addq, s_onek = ph.pair("mask_loaded"), ph.pair("mask_added"), ph.pair("mask_ones")
        s_const, s_rows1 = ph.sem("constants"), ph.sem("one_rows")
        s_ld = [ph.pair(f"stacks_loaded_half{h}") for h in range(2)]
        s_v = ph.pair("values_loaded")
        s_s, s_max = ph.pair("scores"), ph.pair("maxima")
        s_mt, s_nm, s_nh, s_nr, s_nmid, s_nlo = (ph.sem(x) for x in ("max_turned", "neg", "neg_high", "neg_rest", "neg_middle", "neg_low"))
        s_mrow = [ph.pair(f"max_rows_half{h}") for h in range(2)]
        s_t, s_exp = ph.pair("scoresT"), ph.pair("probs")
        s_pv, s_out = ph.pair("probs_used"), ph.sem("quad_out")
        s_ot, s_rc, s_norm = ph.pair("quad_turned"), ph.sem("reciprocals"), ph.sem("normalised")
        s_store = ph.pair("attn_stored")
        LOADS = len(Q_REPS) + len(K_REPS)

        def stack_loads(eng, b, par, half, reps, s, dst):
            for r, part in reps:
                src = k.split[ds(b, 1), s, part, half * P:(half + 1) * P, :].rearrange("b (h e) t -> e (b h) t", e=HD)
                eng.dma_start(dst[par][r * HD:(r + 1) * HD, half * 8:half * 8 + 8, :], src).then_inc(s_ld[half][par], 16)

        with nc.Block() as block:
            @block.sync
            def _(sp):
                def load_stacks(half, b, par):
                    stack_loads(sp, b, par, half, Q_REPS, 0, qs)
                    stack_loads(sp, b, par, half, K_REPS, 1, ks)

                def load_values(b, par):
                    sp.dma_start(vs[par][:, :, :], k.values[ds(b, 1)].rearrange("b (i p) f -> p (b i) f", p=P)).then_inc(s_v[par], 16)

                def load_mask(b, par):
                    for raw, src in ((raw_q, mask[0]), (raw_k, mask[1])):
                        sp.dma_start(raw[par][:, :, :], src[ds(b, 1)].rearrange("b (i p) t -> p (b i) t", p=P)).then_inc(s_raw[par], 16)

                def store(b, it, par, nth):
                    sp.wait_ge(s_norm, nth * QUADS + QUADS)
                    sp.dma_start(k.attn[ds(b, 1)].rearrange("b (i p) d -> p (b i) d", p=P), attn[par][:, :, :]).then_inc(s_store[par], 16)

                for par in ALLX:
                    for half in range(2):
                        load_stacks(half, par, par)
                    if mask is not None:
                        load_mask(par, par)
                    load_values(par, par)
                with sp.Fori(0, B // 2 - 1) as it:
                    for par in ALLX:
                        nth = it * 2 + par
                        if mask is not None:
                            sp.wait_ge(s_addq[par], it + 1)
                            sp.wait_ge(s_onek[par], it + 1)
                            load_mask(nth + 2, par)
                        for half in range(2):
                            sp.wait_ge(s_t[1], nth * STEPS + (half + 1) * STEPS // 2)
                            load_stacks(half, nth + 2, par)
                        wait_apart(ph, sp, s_pv[1], nth * (STEPS // 2) + STEPS // 2)
                        load_values(nth + 2, par)
                        store(nth, it, par, nth)
                for par in ALLX:
                    store(B - 2 + par, B // 2 - 1, par, B - 2 + par)
                for par in ALLX:
                    sp.wait_ge(s_store[par], B // 2 * 16)

            @block.gpsimd
            def _(pool):
                ph.clear_others(pool)
                n = 0
                for p in ALLX:
                    nc.gpsimd.memset(ks[p][SROWS:MROWS, :, :], 1.0).then_inc(s_rows1, 1)
                    pool.wait_ge(s_rows1, p + 1)
                if masked:
                    nc.gpsimd.memset(neg_ident[:, :], 0.0).then_inc(s_const, 1)
                    pool.wait_ge(s_const, 1)
                    nc.gpsimd.affine_select(out=neg_ident[:, :], in_=neg_ident[:, :], compare_op=ALU.not_equal, fill=neg,
                                            base=0, pattern=[[-1, P]], channel_multiplier=1).then_inc(s_const, 1)
                    n = 2
                if causal:
                    nc.gpsimd.memset(ahead_k[:, :], 1.0).then_inc(s_const, 1)
                    nc.gpsimd.memset(ahead_q[:, :], 0.0).then_inc(s_const, 1)
                    pool.wait_ge(s_const, n + 2)
                    nc.gpsimd.affine_select(out=ahead_k[:, :], in_=ahead_k[:, :], compare_op=ALU.is_gt, fill=0.0,
                                            base=0, pattern=[[-1, P]], channel_multiplier=1).then_inc(s_const, 1)
                    nc.gpsimd.affine_select(out=ahead_q[:, N - P:N], in_=ahead_q[:, N - P:N], compare_op=ALU.is_ge, fill=neg,
                                            base=0, pattern=[[-1, P]], channel_multiplier=1).then_inc(s_const, 1)
                    n += 4
                if n:
                    pool.wait_ge(s_const, n)

                def masks(it, par):
                    wait_apart(ph, pool, s_raw[par], it * 32 + 32)
                    nc.gpsimd.tensor_scalar(add_q[par][:, :, :], raw_q[par][:, :, :], neg, None, ALU.mult).then_inc(s_addq[par], 1)
                    nc.gpsimd.tensor_copy(one_k[par][:, :, :], raw_k[par][:, :, :]).then_inc(s_onek[par], 1)

                if mask is not None:
                    for par in ALLX:
                        masks(0, par)
                    with pool.Fori(0, B // 2 - 1) as it:
                        for par in ALLX:
                            for j in range(2):
                                pool.wait_ge(s_max[j], (it * 2 + par + 1) * (UNITS // 2))
                            pool.wait_ge(s_t[1], (it * 2 + par + 1) * STEPS)
                            masks(it + 1, par)

            def unit(u):
                h, i = u // TB, u % TB
                return h, i, ((i + 1) * P if causal else N)

            @block.tensor
            def _(pe):
                def scores(u, nth, par):
                    h, i, n = unit(u)
                    pe.wait_ge(s_max[u % 2], nth * (UNITS // 2) + u // 2)
                    nc.tensor.matmul(s_bank[u % 2][:, 0:n], qs[par][0:SROWS, h, i * P:(i + 1) * P], ks[par][0:SROWS, h, 0:n],
                                     start=True, stop=True).then_inc(s_s[u % 2], 1)

                def turn(half, nth, par, emptied, count):
                    for j in range(2):
                        pe.wait_ge(s_max[j], nth * (UNITS // 2) + (half + 1) * UNITS // 4)
                    if emptied is not None:
                        pe.wait_ge(emptied, count)
                    for i in range(TB):
                        last = nc.tensor.transpose(m_bank[0:H // 2, i * P:(i + 1) * P], rowmax[par][:, i, half * 8:half * 8 + 8], k.ident[:, :])
                    last.then_inc(s_mt, 1)

                def turn_quad(q, nth, emptied, count):
                    pe.wait_ge(s_out, nth * QUADS + q + 1)
                    pe.wait_ge(emptied, count)
                    for i in range(TB):
                        last = nc.tensor.transpose(m_bank[:, i * P:(i + 1) * P], turned[q % 2][:, i * P:(i + 1) * P], k.ident[:, :])
                    last.then_inc(s_ot[q % 2], 1)

                def sum_values(s, nth, par):
                    q, kt = s // TB, s % TB
                    for j in range(2):
                        pe.wait_ge(s_exp[j], nth * STEPS + s + 1)
                    if kt == 0:
                        pe.wait_ge(s_out, nth * QUADS + q)
                    c0 = kt * P if causal else 0
                    for j in range(4):
                        last = nc.tensor.matmul(o_bank[j * VW:(j + 1) * VW, c0:N], vs[par][:, kt, (4 * q + j) * VW:(4 * q + j + 1) * VW],
                                                probs[s % 2][:, j, c0:N], start=(kt == 0), stop=(kt == TB - 1))
                    last.then_inc(s_pv[s % 2], 1)

                def scores_t(s, pair, nth, par):
                    q, kt = s // TB, s % TB
                    c0 = kt * P if causal else 0
                    pe.wait_ge(s_exp[pair], nth * STEPS + s)
                    for j in range(2):
                        h = 4 * q + 2 * pair + j
                        out = t_bank[pair][:, j, c0:N]
                        last = nc.tensor.matmul(out, ks[par][0:MROWS, h, kt * P:(kt + 1) * P], qs[par][0:MROWS, h, c0:N],
                                                start=True, stop=not masked)
                        if mask is not None:
                            last = nc.tensor.matmul(out, neg_ident[:, :], one_k[par][:, kt, :], start=False, stop=True)
                        if causal:
                            last = nc.tensor.matmul(t_bank[pair][:, j, c0:c0 + P], neg_ident[:, :], ahead_k[:, :], start=False, stop=True)
                    last.then_inc(s_t[pair], 1)

                def wait_loaded(half, it, par):
                    pe.wait_ge(s_ld[half][par], it * 16 * LOADS + 16 * LOADS)

                def batch(it, par, nth, ahead):
                    nit, npar = (it, 1) if par == 0 else (it + 1, 0)
                    if mask is not None:
                        pe.wait_ge(s_onek[par], it + 1)
                    pe.wait_ge(s_v[par], it * 16 + 16)
                    for s in range(STEPS):
                        if s % (STEPS // 2) == 0:
                            pe.wait_ge(s_mrow[s // (STEPS // 2)][par], it * 48 + 48)
                            if ahead:
                                wait_loaded(s // (STEPS // 2), nit, npar)
                        u = 4 * s
                        scores_t(s, 0, nth, par)
                        if ahead:
                            scores(u, nth + 1, npar)
                        scores_t(s, 1, nth, par)
                        if ahead:
                            scores(u + 1, nth + 1, npar)
                        if s:
                            sum_values(s - 1, nth, par)
                        if ahead:
                            scores(u + 2, nth + 1, npar)
                            scores(u + 3, nth + 1, npar)
                        if s % TB == 1 and s > TB:
                            q = s // TB - 1
                            if q == 2 and ahead:
                                turn_quad(q, nth, s_nm, (nth + 1) * 2 + 1)
                            else:
                                turn_quad(q, nth, s_norm, nth * QUADS + q)
                        if s == STEPS // 2 + 2 and ahead:
                            turn(0, nth + 1, npar, s_norm, nth * QUADS + 2)
                    sum_values(STEPS - 1, nth, par)
                    if ahead:
                        turn(1, nth + 1, npar, s_norm, nth * QUADS + 3)
                        turn_quad(QUADS - 1, nth, s_nm, (nth + 1) * 2 + 2)
                    else:
                        turn_quad(QUADS - 1, nth, s_norm, nth * QUADS + 3)

                pe.wait_ge(s_rows1, 2)
                if masked:
                    pe.wait_ge(s_const, 6 if causal else 2)
                for half in range(2):
                    wait_loaded(half, 0, 0)
                    for u in range(half * UNITS // 2, (half + 1) * UNITS // 2):
                        scores(u, 0, 0)
                    turn(half, 0, 0, s_nm if half else None, half)
                for par in ALLX:
                    batch(0, par, par, True)
                with pe.Fori(1, B // 2 - 1) as it:
                    for par in ALLX:
                        batch(it, par, it * 2 + par, True)
                batch(B // 2 - 1, 0, B - 2, True)
                batch(B // 2 - 1, 1, B - 1, False)

            @block.scalar
            def _(act):
                def exps(s, pair, nth):
                    kt = s % TB
                    c0 = kt * P if causal else 0
                    act.wait_ge(s_t[pair], nth * STEPS + s + 1)
                    act.wait_ge(s_pv[s % 2], nth * (STEPS // 2) + s // 2)
                    nc.scalar.activation(probs[s % 2][:, 2 * pair:2 * pair + 2, c0:N], t_bank[pair][:, :, c0:N], ACT.Exp,
                                         scale=scale).then_inc(s_exp[pair], 1)

                def quad_out(q, nth):
                    act.wait_ge(s_pv[1], nth * (STEPS // 2) + 2 * q + 2)
                    act.wait_ge(s_ot[q % 2], nth * 2 + q // 2)
                    nc.scalar.activation(turned[q % 2][:, :], o_bank[:, :], ACT.Copy).then_inc(s_out, 1)

                def split_max(half, done, npar, sent):
                    act.wait_ge(s_mt, done + 1)
                    act.wait_ge(s_nlo, done)
                    act.wait_ge(s_mrow[half][1 - npar], sent * 48)
                    nc.scalar.activation(negmax[:, :], m_bank[0:H // 2, :], ACT.Copy, scale=-1.0).then_inc(s_nm, 1)
                    act.wait_ge(s_nm, done + 1)
                    nc.scalar.activation(negpart[half][:, 0, :], negmax[:, :], ACT.Copy).then_inc(s_nh, 1)
                    act.wait_ge(s_nr, done + 1)
                    nc.scalar.activation(negpart[half][:, 1, :], negrest[:, :], ACT.Copy).then_inc(s_nmid, 1)
                    act.wait_ge(s_nlo, done + 1)
                    for c in range(3):
                        act.dma_start(qs[npar][SROWS + c:SROWS + c + 1, half * 8:half * 8 + 8, :], negpart[half][:, c:c + 1, :]
                                      ).then_inc(s_mrow[half][npar], 16)

                def batch(it, par, nth, ahead):
                    npar = 1 - par
                    for s in range(STEPS):
                        exps(s, 0, nth)
                        exps(s, 1, nth)
                        if s % TB == 0 and s:
                            quad_out(s // TB - 1, nth)
                        if s == STEPS // 2 + 3 and ahead:
                            split_max(0, nth * 2 + 2, npar, it + 1)
                    quad_out(QUADS - 1, nth)
                    if ahead:
                        split_max(1, nth * 2 + 3, npar, it + 1)

                for half in range(2):
                    split_max(half, half, 0, 0)
                for par in ALLX:
                    batch(0, par, par, True)
                with act.Fori(1, B // 2 - 1) as it:
                    for par in ALLX:
                        batch(it, par, it * 2 + par, True)
                batch(B // 2 - 1, 0, B - 2, True)
                batch(B // 2 - 1, 1, B - 1, False)
                for half in range(2):
                    for par in ALLX:
                        act.wait_ge(s_mrow[half][par], B // 2 * 48)

            @block.vector
            def _(dve):
                def maxima(u, nth, par):
                    h, i, n = unit(u)
                    wait_apart(ph, dve, s_s[u % 2], nth * (UNITS // 2) + u // 2 + 1)
                    out = rowmax[par][:, i, h:h + 1]
                    if masked:
                        add = ahead_q[:, N - n:N] if causal else add_q[par][:, i, :]
                        nc.vector.tensor_tensor_reduce(out=scratch[u % 2][:, 0:n], in0=s_bank[u % 2][:, 0:n], in1=add, scale=1.0,
                                                       scalar=-3.0e38, op0=ALU.add, op1=ALU.max, accum_out=out).then_inc(s_max[u % 2], 1)
                    else:
                        nc.vector.reduce_max(out, s_bank[u % 2][:, 0:n], AX.X).then_inc(s_max[u % 2], 1)

                def rests(half, done):
                    dve.wait_ge(s_nh, done + 1)
                    nc.vector.tensor_tensor(negrest[:, :], negmax[:, :], negpart[half][:, 0, :], ALU.subtract).then_inc(s_nr, 1)
                    dve.wait_ge(s_nmid, done + 1)
                    nc.vector.tensor_tensor(negpart[half][:, 2, :], negrest[:, :], negpart[half][:, 1, :], ALU.subtract).then_inc(s_nlo, 1)

                def normalise(q, it, nth, par):
                    dve.wait_ge(s_ot[q % 2], nth * 2 + q // 2 + 1)
                    if q == 0:
                        dve.wait_ge(s_store[par], it * 16)
                    dve.wait_ge(s_norm, nth * QUADS + q)
                    sums = m_bank[:, :].rearrange("p (g w) -> p g w", w=VW)
                    nc.vector.reciprocal(recip[:, :].rearrange("p (g a) -> p g a", a=1), sums[:, :, HD:HD + 1]).then_inc(s_rc, 1)
                    dve.wait_ge(s_rc, nth * QUADS + q + 1)
                    nc.vector.tensor_tensor(attn[par][:, :, q * 4 * HD:(q + 1) * 4 * HD].rearrange("p i (j e) -> p i j e", e=HD),
                                            m_bank[:, :].rearrange("p (i j w) -> p i j w", i=TB, w=VW)[:, :, :, 0:HD],
                                            recip[:, :].rearrange("p (i j a) -> p i j a", i=TB, a=1).broadcast_to((P, TB, 4, HD)),
                                            ALU.mult).then_inc(s_norm, 1)

                def batch(it, par, nth, ahead):
                    nit, npar = (it, 1) if par == 0 else (it + 1, 0)
                    if mask is not None and ahead:
                        dve.wait_ge(s_addq[npar], nit + 1)
                    for s in range(STEPS):
                        if ahead:
                            for u in range(4 * s, 4 * s + 4):
                                maxima(u, nth + 1, npar)
                        if s % TB == 1 and s > TB:
                            normalise(s // TB - 1, it, nth, par)
                        if s == STEPS // 2 + 3 and ahead:
                            rests(0, nth * 2 + 2)
                    if ahead:
                        rests(1, nth * 2 + 3)
                    normalise(QUADS - 1, it, nth, par)

                if masked:
                    dve.wait_ge(s_const, 6 if causal else 2)
                if mask is not None:
                    dve.wait_ge(s_addq[0], 1)
                for half in range(2):
                    for u in range(half * UNITS // 2, (half + 1) * UNITS // 2):
                        maxima(u, 0, 0)
                    rests(half, half)
                for par in ALLX:
                    batch(0, par, par, True)
                with dve.Fori(1, B // 2 - 1) as it:
                    for par in ALLX:
                        batch(it, par, it * 2 + par, True)
                batch(B // 2 - 1, 0, B - 2, True)
                batch(B // 2 - 1, 1, B - 1, False)


def phase_output(k, tag, w_out, b_out=None):
    nc = k.nc
    with Phase(k, tag) as ph:
        ps = ph.banks()
        wo = ph.sb("wo", [P, KC, D])
        bias = ph.sb("bias", [P, D])
        at, atT = ph.two("at", [P, TB, D]), ph.two("atT", [P, KC, N])
        s_w, s_at, s_turn, s_atT = ph.sem("weights"), ph.pair("attn_loaded"), ph.pair("attn_turned"), ph.pair("attnT")
        s_y, s_x, s_b = ph.pair("product"), ph.pair("x_updated"), ph.pair("bias_added")
        w_all = 16 * (1 if b_out is None else 2)
        with nc.Block() as block:
            @block.sync
            def _(sp):
                sp.dma_start(wo[:, :, :], rows(w_out)).then_inc(s_w, 16)
                if b_out is not None:
                    sp.dma_start(bias[:, :], over_partitions(b_out)).then_inc(s_w, 16)
                for it, par, b in batches(sp):
                    sp.wait_ge(s_turn[par], it * KC)
                    sp.dma_start(at[par][:, :, :], k.attn[ds(b, 1)].rearrange("b (i p) d -> p (b i) d", p=P)).then_inc(s_at[par], 16)

            @block.gpsimd
            def _(pool):
                ph.clear_others(pool)
                if b_out is not None:
                    pool.wait_ge(s_w, w_all)
                    for it, par, b in batches(pool):
                        for i in range(TB):
                            xi = k.x[:, ds(b * TB + i, 1), :]
                            nc.gpsimd.tensor_tensor(xi, xi, bias[:, :].rearrange("p (a d) -> p a d", a=1), ALU.add).then_inc(s_b[par], 1)

            @block.tensor
            def _(pe):
                pe.wait_ge(s_w, w_all)
                for it, par, b in batches(pe):
                    pe.wait_ge(s_at[par], it * 16 + 16)
                    pe.wait_ge(s_atT[par], it * KC)
                    for c in range(KC):
                        for i in range(TB):
                            last = nc.tensor.transpose(ps[4 * par + c][:, i * P:(i + 1) * P], at[par][:, i, c * P:(c + 1) * P], k.ident[:, :])
                        last.then_inc(s_turn[par], 1)
                    pe.wait_ge(s_atT[par], it * KC + KC)
                    pe.wait_ge(s_x[par], it * TB)
                    for i in range(TB):
                        for c in range(KC):
                            last = nc.tensor.matmul(ps[4 * par + 2 + i // 2][:, (i % 2) * D:(i % 2 + 1) * D], atT[par][:, c, i * P:(i + 1) * P],
                                                    wo[:, c, :], start=(c == 0), stop=(c == KC - 1))
                        last.then_inc(s_y[par], 1)

            @block.scalar
            def _(act):
                for it, par, b in batches(act):
                    act.wait_ge(s_y[par], it * TB)
                    for c in range(KC):
                        act.wait_ge(s_turn[par], it * KC + c + 1)
                        nc.scalar.activation(atT[par][:, c, :], ps[4 * par + c][:, :], ACT.Copy).then_inc(s_atT[par], 1)

            @block.vector
            def _(dve):
                for it, par, b in batches(dve):
                    for i in range(TB):
                        dve.wait_ge(s_y[par], it * TB + (i // 2 * 2 + 2))
                        if b_out is not None:
                            dve.wait_ge(s_b[par], it * TB + i + 1)
                        xi = k.x[:, ds(b * TB + i, 1), :]
                        nc.vector.tensor_tensor(xi, xi, ps[4 * par + 2 + i // 2][:, (i % 2) * D:(i % 2 + 1) * D].rearrange("p (a d) -> p a d", a=1),
                                                ALU.add).then_inc(s_x[par], 1)


def phase_store(k, out):
    with Phase(k, "store") as ph:
        done = ph.sem("stored")
        with k.nc.Block() as block:
            @block.sync
            def _(sp):
                sp.dma_start(out.rearrange("b (i p) d -> p (b i) d", p=P), k.x[:, :, :]).then_inc(done, 16)
                sp.wait_ge(done, 16)

            @block.gpsimd
            def _(pool):
                ph.clear_others(pool)
RING = 4
SLOTS = NT + E - 1
ROUND = 1.5 * 2.0 ** 23


def phase_route(k, wr, br, w1, w2):
    nc = k.nc
    with Phase(k, "route") as ph:
        ps = ph.banks()
        norm = Norm(ph, "ln", EPS_X)
        xn = ph.two("xn", [P, TB, D])
        ring = [ph.sb(f"ring{r}", [P, D]) for r in range(RING)]
        xnT = ph.sb("xnT", [P, KC, N])
        wr_s, br_s = ph.sb("wr", [P, KC, E]), ph.sb("br", [P, E])
        logits = ph.sb("logits", [P, NT, E])
        top = ph.sb("top", [P, NT, E])
        index = ph.sb("index", [P, NT, E], U32)
        diff = ph.sb("diff", [P, NT])
        best = ph.sb("best", [P, NT])
        chosen, chosen16 = ph.sb("chosen", [P, NT, E]), ph.sb("chosen16", [P, NT, E], BF16)
        earlier, ones16 = ph.sb("earlier", [P, P], BF16), ph.sb("ones16", [P, P], BF16)
        ones_t = ph.sb("ones_t", [P, NT])
        nth_e = ph.sb("nth_e", [P, E])
        nth_slot = ph.sb("nth_slot", [P, SLOTS])
        count, upto = ph.sb("count", [P, NT, E]), ph.sb("upto", [P, NT, E])
        tiles_i, tiles_f = ph.sb("tiles_i", [P, E], I32), ph.sb("tiles_f", [P, E])
        ends, first = ph.sb("ends", [P, E]), ph.sb("first", [P, E])
        passed = ph.sb("passed", [P, SLOTS, E])
        owner = ph.sb("owner", [P, SLOTS])
        place = ph.sb("place", [P, NT])
        zero = ph.sb("zero", [P, D])
        s_w, s_ew = ph.sem("weights"), ph.sem("expert_weights")
        s_c, s_z = ph.sem("constants"), ph.sem("zero_rows")
        s_xn, s_t, s_xT = ph.pair("xn"), ph.pair("x_turned"), ph.pair("xnT")
        s_l, s_lb = ph.pair("logits"), ph.pair("logits_out")
        s_dve, s_pe, s_act, s_top = ph.sem("routing_steps"), ph.sem("rank_products"), ph.sem("odds"), ph.sem("top")
        s_kept, s_back, s_sc = ph.pair("xn_stored"), [ph.sem(f"xn_back{r}") for r in range(RING)], [ph.own_sem(f"scattered{r}") for r in range(RING)]
        with nc.Block() as block:
            @block.sync
            def _(sp):
                sp.dma_start(wr_s[:, :, :], rows(wr)).then_inc(s_w, 16)
                sp.dma_start(br_s[:, :], over_partitions(br)).then_inc(s_w, 16)
                sp.wait_ge(s_c, 1)
                sp.dma_start(k.slots_in.rearrange("(j p) d -> p j d", p=P),
                             zero[:, :].rearrange("p (a d) -> p a d", a=1).broadcast_to((P, SLOTS, D))).then_inc(s_z, 16)
                for it, par, b in batches(sp):
                    for wide, src in ((k.w1, w1), (k.w2, w2)):
                        sp.dma_start(wide[:, ds(b, 1), :, :].rearrange("p e c n -> p (e c) n"), src[ds(b, 1)].rearrange("e (c p) n -> p (e c) n", p=P)).then_inc(s_ew, 16)
                    sp.wait_ge(s_xn[par], it * TB + TB)
                    sp.dma_start(k.attn[ds(b, 1)].rearrange("b (i p) d -> p (b i) d", p=P), xn[par][:, :, :]).then_inc(s_kept[par], 16)
                for par in ALLX:
                    sp.wait_ge(s_kept[par], B // 2 * 16)
                for t in range(NT):
                    if t >= RING:
                        sp.wait_ge(s_sc[t % RING], 16 * (t // RING))
                    sp.dma_start(ring[t % RING][:, :], k.attn[t // TB, (t % TB) * P:(t % TB + 1) * P, :]).then_inc(s_back[t % RING], 16)
                sp.wait_ge(s_ew, 32 * E)

            @block.gpsimd
            def _(pool):
                ph.clear_others(pool)
                nc.gpsimd.memset(zero[:, :], 0.0).then_inc(s_c, 1)
                nc.gpsimd.memset(earlier[:, :], 1.0).then_inc(s_c, 1)
                nc.gpsimd.memset(ones16[:, :], 1.0).then_inc(s_c, 1)
                nc.gpsimd.memset(ones_t[:, :], 1.0).then_inc(s_c, 1)
                nc.gpsimd.iota(nth_e[:, :], [[1, E]], base=0, channel_multiplier=0, allow_small_or_imprecise_dtypes=True).then_inc(s_c, 1)
                nc.gpsimd.iota(nth_slot[:, :], [[1, SLOTS]], base=0, channel_multiplier=0, allow_small_or_imprecise_dtypes=True).then_inc(s_c, 1)
                pool.wait_ge(s_c, 6)
                nc.gpsimd.affine_select(out=earlier[:, :], in_=earlier[:, :], compare_op=ALU.is_gt, fill=0.0,
                                        base=0, pattern=[[1, P]], channel_multiplier=-1).then_inc(s_c, 1)
                for it, par, b in batches(pool):
                    norm.power(pool, par, it)
                pool.wait_ge(s_z, 16)
                pool.wait_ge(s_dve, ROUTED)
                for t in range(NT):
                    pool.wait_ge(s_back[t % RING], 16 * (t // RING + 1))
                    nc.gpsimd.indirect_dma_start(out=k.slots_in, out_offset=bass.IndirectOffsetOnAxis(ap=k.place[:, t:t + 1], axis=0),
                                                 in_=ring[t % RING][:, :], in_offset=None).then_inc(s_sc[t % RING], 16)
                for r in range(RING):
                    pool.wait_ge(s_sc[r], NT // RING * 16)

            @block.tensor
            def _(pe):
                pe.wait_ge(s_w, 32)
                for it, par, b in batches(pe):
                    pe.wait_ge(s_xn[par], it * TB + TB)
                    pe.wait_ge(s_xT[par], it * KC)
                    for c in range(KC):
                        for i in range(TB):
                            last = nc.tensor.transpose(ps[2 * par + c][:, i * P:(i + 1) * P], xn[par][:, i, c * P:(c + 1) * P], k.ident[:, :])
                    last.then_inc(s_t[par], 1)
                    pe.wait_ge(s_xT[par], it * KC + KC)
                    pe.wait_ge(s_lb[par], it)
                    for i in range(TB):
                        for c in range(KC):
                            last = nc.tensor.matmul(ps[4 + par][:, i * E:(i + 1) * E], xnT[:, c, i * P:(i + 1) * P], wr_s[:, c, :],
                                                    start=(c == 0), stop=(c == KC - 1))
                    last.then_inc(s_l[par], 1)
                pe.wait_ge(s_c, 7)
                pe.wait_ge(s_dve, CHOSEN)
                nc.tensor.matmul(ps[6][:, 0:NT * E], earlier[:, :], chosen16[:, :, :].rearrange("p t e -> p (t e)"), start=True, stop=True).then_inc(s_pe, 1)
                nc.tensor.matmul(ps[7][:, 0:NT * E], ones16[:, :], chosen16[:, :, :].rearrange("p t e -> p (t e)"), start=True, stop=True).then_inc(s_pe, 1)

            @block.scalar
            def _(act):
                for it, par, b in batches(act):
                    act.wait_ge(s_t[par], it + 1)
                    act.wait_ge(*before(s_l, it, par, 1))
                    for c in range(KC):
                        nc.scalar.activation(xnT[:, c, :], ps[2 * par + c][:, :], ACT.Copy).then_inc(s_xT[par], 1)
                act.wait_ge(s_dve, DIFFERED)
                nc.scalar.activation(diff[:, :], diff[:, :], ACT.Exp).then_inc(s_act, 1)

            @block.vector
            def _(dve):
                dve.wait_ge(s_w, 32)
                dve.wait_ge(s_c, 7)
                steps = [0]

                def step(ins):
                    steps[0] += 1
                    ins.then_inc(s_dve, 1)
                    dve.wait_ge(s_dve, steps[0])

                for it, par, b in batches(dve):
                    src = lambda i: k.x[:, ds(b * TB + i, 1), :].rearrange("p a d -> p (a d)")
                    norm.statistics(dve, par, it, src)
                    dve.wait_ge(s_t[par], it)
                    dve.wait_ge(s_kept[par], it * 16)
                    norm.apply(dve, par, it, src, lambda i: xn[par][:, i, :], s_xn[par])
                    dve.wait_ge(s_l[par], it + 1)
                    nc.vector.tensor_tensor(logits[:, ds(b * TB, TB), :], ps[4 + par][:, 0:TB * E].rearrange("p (i e) -> p i e", e=E),
                                            br_s[:, :].rearrange("p (a e) -> p a e", a=1).broadcast_to((P, TB, E)), ALU.add).then_inc(s_lb[par], 1)
                for par in ALLX:
                    dve.wait_ge(s_lb[par], B // 2)
                for t in range(NT):
                    nc.vector.max(top[:, t, :], logits[:, t, :]).then_inc(s_top, 1)
                dve.wait_ge(s_top, NT)
                for t in range(NT):
                    nc.vector.max_index(index[:, t, :], top[:, t, :], logits[:, t, :]).then_inc(s_top, 1)
                dve.wait_ge(s_top, 2 * NT)
                wide = lambda a, n: a.rearrange("p (t a) -> p t a", a=1).broadcast_to((P, a.shape[1], n))
                over_t = lambda a, n: a.rearrange("p (a e) -> p a e", a=1).broadcast_to((P, n, E))
                step(nc.vector.tensor_tensor(diff[:, :], top[:, :, 1], top[:, :, 0], ALU.subtract))
                assert steps[0] == DIFFERED
                step(nc.vector.tensor_copy(best[:, :], index[:, :, 0]))
                step(nc.vector.tensor_tensor(chosen[:, :, :], wide(best[:, :], E), over_t(nth_e[:, :], NT), ALU.is_equal))
                step(nc.vector.tensor_copy(chosen16[:, :, :], chosen[:, :, :]))
                assert steps[0] == CHOSEN
                dve.wait_ge(s_act, 1)
                step(nc.vector.tensor_scalar_add(diff[:, :], diff[:, :], 1.0))
                step(nc.vector.reciprocal(k.gate[:, :], diff[:, :]))
                dve.wait_ge(s_pe, 2)
                step(nc.vector.tensor_copy(count[:, :, :], ps[7][:, 0:NT * E].rearrange("p (t e) -> p t e", e=E)))
                for e in range(E):
                    step(nc.vector.tensor_tensor_scan(upto[:, :, e], ones_t[:, :], count[:, :, e], 0.0, ALU.mult, ALU.add))
                step(nc.vector.tensor_scalar_add(tiles_i[:, :], upto[:, NT - 1, :], float(P - 1)))
                step(nc.vector.tensor_scalar(tiles_i[:, :], tiles_i[:, :], 7, None, ALU.arith_shift_right))
                step(nc.vector.tensor_copy(tiles_f[:, :], tiles_i[:, :]))
                step(nc.vector.tensor_tensor_scan(ends[:, :], ones_t[:, 0:E], tiles_f[:, :], 0.0, ALU.mult, ALU.add))
                step(nc.vector.tensor_tensor(first[:, :], ends[:, :], tiles_f[:, :], ALU.subtract))
                step(nc.vector.tensor_scalar(first[:, :], first[:, :], float(P), None, ALU.mult))
                step(nc.vector.tensor_tensor(upto[:, :, :], upto[:, :, :], count[:, :, :], ALU.subtract))
                step(nc.vector.tensor_tensor(upto[:, :, :], upto[:, :, :], ps[6][:, 0:NT * E].rearrange("p (t e) -> p t e", e=E), ALU.add))
                step(nc.vector.tensor_tensor(upto[:, :, :], upto[:, :, :], over_t(first[:, :], NT), ALU.add))
                step(nc.vector.tensor_tensor(upto[:, :, :], upto[:, :, :], chosen[:, :, :], ALU.mult))
                step(nc.vector.tensor_reduce(place[:, :], upto[:, :, :], AX.X, ALU.add))
                step(nc.vector.tensor_copy(k.place[:, :], place[:, :]))
                step(nc.vector.tensor_tensor(passed[:, :, :], wide(nth_slot[:, :], E), over_t(ends[:, :], SLOTS), ALU.is_ge))
                step(nc.vector.tensor_reduce(owner[:, :], passed[:, :, :], AX.X, ALU.add))
                step(nc.vector.tensor_scalar(k.owner[:, :], owner[:, :], float(E - 1), None, ALU.min))
                assert steps[0] == ROUTED


DIFFERED, CHOSEN = 1, 4
ROUTED = 4 + 2 + 1 + E + 6 + 6 + 3


def phase_experts(k, b1T, b2):
    nc = k.nc
    with Phase(k, "moe") as ph:
        ps = ph.banks()
        xt, xT = ph.two("xt", [P, D]), ph.two("xT", [P, KC, P])
        hid = ph.sb("hid", [P, F])
        hidT = ph.sb("hidT", [P, FC, P])
        y = ph.two("y", [P, D])
        b1s, b2s = ph.sb("b1", [P, E * FC]), ph.sb("b2", [P, E, D])
        s_b, s_x, s_t, s_xT = ph.sem("biases"), ph.pair("x_loaded"), ph.sem("x_turned"), ph.sem("xT")
        s_h, s_ho, s_ht, s_g = ph.sem("hidden"), ph.sem("hidden_out"), ph.sem("hidden_turned"), ph.sem("gelu")
        s_y, s_yo, s_st = ph.sem("product"), ph.sem("y_out"), ph.pair("y_stored")

        def tiles(eng, body):
            body(0, 0, 0, True)
            body(1, 0, 1, False)
            body(2, 1, 0, False)
            with eng.Fori(1, (SLOTS - 1) // 2) as it:
                body(it * 2 + 1, it, 1, False)
                body(it * 2 + 2, it + 1, 0, False)

        with nc.Block() as block:
            @block.sync
            def _(sp):
                sp.dma_start(b1s[:, :], b1T).then_inc(s_b, 16)
                sp.dma_start(b2s[:, :, :], b2.rearrange("(a e) d -> a e d", a=1).broadcast_to((P, E, D))).then_inc(s_b, 16)

                def store(j, par):
                    wait_apart(ph, sp, s_yo, j + 1)
                    sp.dma_start(k.slots_out.rearrange("(j p) d -> j p d", p=P)[ds(j, 1)].rearrange("j p d -> p (j d)"), y[par][:, :]).then_inc(s_st[par], 16)

                def body(j, par, first):
                    if not first:
                        wait_apart(ph, sp, s_t, j - 1)
                    sp.dma_start(xt[par][:, :], k.slots_in.rearrange("(j p) d -> j p d", p=P)[ds(j, 1)].rearrange("j p d -> p (j d)")).then_inc(s_x[par], 16)
                    if not first:
                        store(j - 2, par)
                body(0, 0, True)
                body(1, 1, True)
                with sp.Fori(1, (SLOTS - 1) // 2) as it:
                    body(it * 2, 0, False)
                    body(it * 2 + 1, 1, False)
                body(SLOTS - 1, 0, False)
                store(SLOTS - 2, 1)
                store(SLOTS - 1, 0)
                sp.wait_ge(s_st[0], (SLOTS + 1) // 2 * 16)
                sp.wait_ge(s_st[1], SLOTS // 2 * 16)

            @block.gpsimd
            def _(pool):
                ph.clear_others(pool)

            @block.tensor
            def _(pe):
                def turn_x(j, before_par, par):
                    pe.wait_ge(s_x[par], before_par * 16 + 16)
                    pe.wait_ge(s_xT, j)
                    for c in range(KC):
                        last = nc.tensor.transpose(ps[0][:, c * P:(c + 1) * P], xt[par][:, c * P:(c + 1) * P], k.ident[:, :])
                    last.then_inc(s_t, 1)

                def up(j, par):
                    e = pe.value_load(k.owner[0:1, ds(j, 1)], min_val=0, max_val=E - 1)
                    pe.wait_ge(s_xT, j + 1)
                    for half in range(2):
                        pe.wait_ge(s_ho, j * 2 + half)
                        for c in range(KC):
                            last = nc.tensor.matmul(ps[1 + half][:, :], xT[par][:, c, :], k.w1[:, ds(e, 1), c, half * 512:half * 512 + 512],
                                                    start=(c == 0), stop=(c == KC - 1))
                        last.then_inc(s_h, 1)

                def down(j, par, left):
                    e = pe.value_load(k.owner[0:1, ds(j, 1)], min_val=0, max_val=E - 1)
                    pe.wait_ge(s_yo, left)
                    for c in range(FC):
                        pe.wait_ge(s_g, j * FC + c + 1)
                        last = nc.tensor.matmul(ps[5 + par][:, 0:D], hidT[:, c, :], k.w2[:, ds(e, 1), c, :],
                                                start=(c == 0), stop=(c == FC - 1))
                    last.then_inc(s_y, 1)

                def turn_h(j):
                    pe.wait_ge(s_g, j * FC)
                    for half in range(2):
                        pe.wait_ge(s_ho, j * 2 + half + 1)
                        for c in range(4):
                            last = nc.tensor.transpose(ps[3 + half][:, c * P:(c + 1) * P], hid[:, (4 * half + c) * P:(4 * half + c + 1) * P], k.ident[:, :])
                        last.then_inc(s_ht, 1)

                def body(j, before_par, par, first):
                    turn_x(j, before_par, par)
                    up(j, par)
                    if not first:
                        down(j - 1, 1 - par, j - 1)
                    turn_h(j)
                tiles(pe, body)
                down(SLOTS - 1, (SLOTS - 1) % 2, SLOTS - 2)

            @block.scalar
            def _(act):
                act.wait_ge(s_b, 32)

                def body(j, before_par, par, first):
                    e = act.value_load(k.owner[0:1, ds(j, 1)], min_val=0, max_val=E - 1)
                    act.wait_ge(s_t, j + 1)
                    nc.scalar.activation(xT[par][:, :, :], ps[0][:, 0:D].rearrange("p (c t) -> p c t", c=KC), ACT.Copy).then_inc(s_xT, 1)
                    act.wait_ge(s_y, j)
                    for c in range(FC):
                        if c % 4 == 0:
                            act.wait_ge(s_ht, j * 2 + c // 4 + 1)
                        nc.scalar.activation(hidT[:, c, :], ps[3 + c // 4][:, (c % 4) * P:(c % 4 + 1) * P], ACT.Gelu,
                                             bias=b1s[:, ds(e * FC + c, 1)]).then_inc(s_g, 1)
                tiles(act, body)

            @block.vector
            def _(dve):
                dve.wait_ge(s_b, 32)

                def out(j, before_par, par):
                    e = dve.value_load(k.owner[0:1, ds(j, 1)], min_val=0, max_val=E - 1)
                    dve.wait_ge(s_y, j + 1)
                    dve.wait_ge(s_st[par], before_par * 16)
                    nc.vector.tensor_tensor(y[par][:, :].rearrange("p (a d) -> p a d", a=1), ps[5 + par][:, 0:D].rearrange("p (a d) -> p a d", a=1),
                                            b2s[:, ds(e, 1), :], ALU.add).then_inc(s_yo, 1)

                def body(j, before_par, par, first):
                    dve.wait_ge(s_ht, j * 2)
                    for half in range(2):
                        dve.wait_ge(s_h, j * 2 + half + 1)
                        nc.vector.tensor_copy(hid[:, half * 512:half * 512 + 512], ps[1 + half][:, :]).then_inc(s_ho, 1)
                    if not first:
                        out(j - 1, before_par if par else before_par - 1, 1 - par)
                tiles(dve, body)
                out(SLOTS - 1, (SLOTS - 1) // 2, (SLOTS - 1) % 2)


def phase_combine(k):
    nc = k.nc
    with Phase(k, "combine") as ph:
        rows_in = [ph.sb(f"rows{r}", [P, D]) for r in range(RING)]
        s_got = [ph.own_sem(f"fetched{r}") for r in range(RING)]
        s_used = ph.sem("added")
        with nc.Block() as block:
            @block.gpsimd
            def _(pool):
                ph.clear_others(pool)
                for t in range(NT):
                    if t >= RING:
                        pool.wait_ge(s_used, t - RING + 1)
                    nc.gpsimd.indirect_dma_start(out=rows_in[t % RING][:, :], out_offset=None, in_=k.slots_out,
                                                 in_offset=bass.IndirectOffsetOnAxis(ap=k.place[:, t:t + 1], axis=0)).then_inc(s_got[t % RING], 16)

            @block.vector
            def _(dve):
                for t in range(NT):
                    dve.wait_ge(s_got[t % RING], 16 * (t // RING + 1))
                    nc.vector.scalar_tensor_tensor(out=k.x[:, t, :], in0=rows_in[t % RING][:, :], scalar=k.gate[:, t:t + 1], in1=k.x[:, t, :],
                                                   op0=ALU.mult, op1=ALU.add).then_inc(s_used, 1)


def moe(k, wr, br, w1, b1T, w2, b2):
    nc = k.nc
    with ExitStack() as ctx:
        sb = lambda name, shape, dt=F32: ctx.enter_context(nc.sbuf_tensor(name, shape, dt))
        k.w1, k.w2 = sb("expert_w1", [P, E, KC, F]), sb("expert_w2", [P, E, FC, D])
        k.gate, k.place, k.owner = sb("gate", [P, NT]), sb("place", [P, NT], U32), sb("owner", [P, SLOTS], I32)
        phase_route(k, wr, br, w1, w2)
        phase_experts(k, b1T, b2)
        phase_combine(k)
def phase_retention(k, w):
    nc = k.nc
    with Phase(k, "ret") as ph:
        ps = ph.banks()
        w_ret, w1, w2 = ph.sb("w_ret", [P, KC, D]), ph.sb("w1", [P, KC, F]), ph.sb("w2", [P, FC, D])
        b_ret, b1 = ph.sb("b_ret", [P, KC]), ph.sb("b1", [P, FC])
        ln1s, ln1b, ln2s, ln2b, b2 = (ph.sb(x, [P, D]) for x in ("ln1s", "ln1b", "ln2s", "ln2b", "b2"))
        half_t = ph.sb("half", [P, N])
        normx, norm1, norm2 = Norm(ph, "lnx", EPS_X), Norm(ph, "ln1", EPS_X), Norm(ph, "ln2", EPS_X)
        xn = ph.sb("xn", [P, TB, D])
        xnT, sig, yT = ph.sb("xnT", [P, KC, N]), ph.sb("sig", [P, KC, N]), ph.sb("yT", [P, KC, N])
        z = ph.sb("z", [P, TB, D])
        h, hT = ph.two("h", [P, TB, D]), ph.sb("hT", [P, KC, N])
        hb = ph.two("hb", [P, TB, D])
        g = ph.sb("g", [P, FC, N])
        o, on = ph.sb("o", [P, TB, D]), ph.sb("on", [P, TB, D])
        s_w, s_half = ph.sem("weights"), ph.sem("half")
        s_xn, s_t, s_xT, s_r, s_sg, s_z, s_y = (ph.sem(x) for x in ("xn", "x_turned", "xnT", "ret_product", "sigmoid", "scanned", "yT"))
        s_yt, s_ln1, s_hm, s_h, s_hb, s_ht, s_hT = (ph.sem(x) for x in ("y_turned", "ln1", "h_scaled", "h", "h_b2", "h_turned", "hT"))
        s_u, s_g, s_v, s_o, s_on, s_om, s_ob, s_x = (ph.sem(x) for x in ("hidden", "gelu", "product", "sum", "ln2", "out_scaled", "out", "x_updated"))
        NW = 10

        def run(eng, body, last=None):
            body(0, 0, 0, True)
            body(1, 0, 1, False)
            with eng.Fori(1, B // 2) as it:
                for par in ALLX:
                    body(it * 2 + par, it, par, False)
            if last is not None:
                last()

        with nc.Block() as block:
            @block.sync
            def _(sp):
                sp.dma_start(w_ret[:, :, :], rows(w["ret"])).then_inc(s_w, 16)
                sp.dma_start(w1[:, :, :], rows(w["w1"])).then_inc(s_w, 16)
                sp.dma_start(w2[:, :, :], rows(w["w2"])).then_inc(s_w, 16)
                sp.dma_start(b_ret[:, :], w["b_ret"]).then_inc(s_w, 16)
                sp.dma_start(b1[:, :], w["b1"]).then_inc(s_w, 16)
                for dst, name in ((ln1s, "ln1s"), (ln1b, "ln1b"), (ln2s, "ln2s"), (ln2b, "ln2b"), (b2, "b2")):
                    sp.dma_start(dst[:, :], over_partitions(w[name])).then_inc(s_w, 16)
                sp.wait_ge(s_w, 16 * NW)

            @block.gpsimd
            def _(pool):
                ph.clear_others(pool)
                nc.gpsimd.memset(half_t[:, :], 0.5).then_inc(s_half, 1)
                pool.wait_ge(s_w, 16 * NW)
                rep = lambda a: a[:, :].rearrange("p (a d) -> p a d", a=1).broadcast_to((P, TB, D))

                def body(b, it, par, first):
                    normx.power(pool, par, it)
                    norm1.power(pool, par, it)
                    pool.wait_ge(s_ln1, b * TB + TB)
                    nc.gpsimd.tensor_tensor(z[:, :, :], z[:, :, :], rep(ln1s), ALU.mult).then_inc(s_hm, 1)
                    pool.wait_ge(s_hm, b + 1)
                    if not first:
                        pool.wait_ge(s_o, (b - 1) * TB)
                    nc.gpsimd.tensor_tensor(h[par][:, :, :], z[:, :, :], rep(ln1b), ALU.add).then_inc(s_h, 1)
                    pool.wait_ge(s_h, b + 1)
                    nc.gpsimd.tensor_tensor(hb[par][:, :, :], h[par][:, :, :], rep(b2), ALU.add).then_inc(s_hb, 1)
                    if not first:
                        finish(b - 1, it if par else it - 1, 1 - par)

                def finish(b, it, par):
                    norm2.power(pool, par, it)
                    pool.wait_ge(s_on, b * TB + TB)
                    nc.gpsimd.tensor_tensor(on[:, :, :], on[:, :, :], rep(ln2s), ALU.mult).then_inc(s_om, 1)
                    pool.wait_ge(s_om, b + 1)
                    nc.gpsimd.tensor_tensor(on[:, :, :], on[:, :, :], rep(ln2b), ALU.add).then_inc(s_ob, 1)
                run(pool, body, lambda: finish(B - 1, B // 2 - 1, 1))

            @block.tensor
            def _(pe):
                pe.wait_ge(s_w, 16 * NW)

                def turn(src, bank, done):
                    for c in range(KC):
                        for i in range(TB):
                            last = nc.tensor.transpose(ps[bank + c][:, i * P:(i + 1) * P], src[:, i, c * P:(c + 1) * P], k.ident[:, :])
                    last.then_inc(done, 1)

                def up(b):
                    pe.wait_ge(s_hT, b * KC + KC)
                    for f in range(FC):
                        if f >= 2:
                            pe.wait_ge(s_g, b * FC + f - 1)
                        for c in range(KC):
                            last = nc.tensor.matmul(ps[4 + f % 2][:, :], w1[:, c, f * P:(f + 1) * P], hT[:, c, :],
                                                    start=(c == 0), stop=(c == KC - 1))
                        last.then_inc(s_u, 1)

                def down(b):
                    pe.wait_ge(s_g, b * FC + FC)
                    pe.wait_ge(s_o, b * TB)
                    for i in range(TB):
                        for f in range(FC):
                            last = nc.tensor.matmul(ps[6 + i // 2][:, (i % 2) * D:(i % 2 + 1) * D], g[:, f, i * P:(i + 1) * P], w2[:, f, :],
                                                    start=(f == 0), stop=(f == FC - 1))
                        last.then_inc(s_v, 1)

                def body(b, it, par, first):
                    pe.wait_ge(s_xn, b * TB + TB)
                    pe.wait_ge(s_ln1, b * TB)
                    turn(xn, 0, s_t)
                    pe.wait_ge(s_xT, b * KC + KC)
                    pe.wait_ge(s_hT, b * KC)
                    for m in range(KC):
                        for c in range(KC):
                            last = nc.tensor.matmul(ps[2 + m][:, :], w_ret[:, c, m * P:(m + 1) * P], xnT[:, c, :], start=(c == 0), stop=(c == KC - 1))
                        last.then_inc(s_r, 1)
                    if not first:
                        up(b - 1)
                    pe.wait_ge(s_y, b * KC + KC)
                    for i in range(TB):
                        for c in range(KC):
                            last = nc.tensor.transpose(ps[i // 2][:, (i % 2) * D + c * P:(i % 2) * D + (c + 1) * P], yT[:, c, i * P:(i + 1) * P], k.ident[:, :])
                    last.then_inc(s_yt, 1)
                    if not first:
                        down(b - 1)
                    pe.wait_ge(s_h, b + 1)
                    pe.wait_ge(s_sg, b * KC + KC)
                    turn(h[par], 2, s_ht)
                def last_net():
                    up(B - 1)
                    down(B - 1)
                run(pe, body, last_net)

            @block.scalar
            def _(act):
                act.wait_ge(s_w, 16 * NW)

                def gelus(b):
                    act.wait_ge(s_v, b * TB)
                    for f in range(FC):
                        act.wait_ge(s_u, b * FC + f + 1)
                        nc.scalar.activation(g[:, f, :], ps[4 + f % 2][:, :], ACT.Gelu_apprx_tanh, bias=b1[:, f:f + 1]).then_inc(s_g, 1)

                def body(b, it, par, first):
                    act.wait_ge(s_t, b + 1)
                    act.wait_ge(s_y, b * KC)
                    for c in range(KC):
                        nc.scalar.activation(xnT[:, c, :], ps[c][:, :], ACT.Copy).then_inc(s_xT, 1)
                    for m in range(KC):
                        act.wait_ge(s_r, b * KC + m + 1)
                        nc.scalar.activation(sig[:, m, :], ps[2 + m][:, :], ACT.Sigmoid, bias=b_ret[:, m:m + 1]).then_inc(s_sg, 1)
                    if not first:
                        gelus(b - 1)
                    act.wait_ge(s_ht, b + 1)
                    for c in range(KC):
                        nc.scalar.activation(hT[:, c, :], ps[2 + c][:, :], ACT.Copy).then_inc(s_hT, 1)
                run(act, body, lambda: gelus(B - 1))

            @block.vector
            def _(dve):
                dve.wait_ge(s_w, 16 * NW)
                dve.wait_ge(s_half, 1)

                def body(b, it, par, first):
                    src = lambda i: k.x[:, ds(b * TB + i, 1), :].rearrange("p a d -> p (a d)")
                    normx.statistics(dve, par, it, src)
                    dve.wait_ge(s_t, b)
                    normx.apply(dve, par, it, src, lambda i: xn[:, i, :], s_xn)
                    for m in range(KC):
                        dve.wait_ge(s_sg, b * KC + m + 1)
                        dve.wait_ge(s_yt, b)
                        nc.vector.tensor_tensor_scan(yT[:, m, :], half_t[:, :], sig[:, m, :], 0.0, ALU.mult, ALU.add).then_inc(s_z, 1)
                        dve.wait_ge(s_z, b * KC + m + 1)
                        nc.vector.scalar_tensor_tensor(out=yT[:, m, :], in0=yT[:, m, :], scalar=0.5, in1=xnT[:, m, :],
                                                       op0=ALU.mult, op1=ALU.add).then_inc(s_y, 1)
                    dve.wait_ge(s_yt, b + 1)
                    y = lambda i: ps[i // 2][:, (i % 2) * D:(i % 2 + 1) * D]
                    norm1.statistics(dve, par, it, y)
                    dve.wait_ge(s_h, b)
                    norm1.apply(dve, par, it, y, lambda i: z[:, i, :], s_ln1)
                    if not first:
                        finish(b - 1, it if par else it - 1, 1 - par)

                def finish(b, it, par):
                    for i in range(TB):
                        dve.wait_ge(s_v, b * TB + i // 2 * 2 + 2)
                        dve.wait_ge(s_hb, b + 1)
                        nc.vector.tensor_tensor(o[:, i, :], ps[6 + i // 2][:, (i % 2) * D:(i % 2 + 1) * D], hb[par][:, i, :], ALU.add).then_inc(s_o, 1)
                    dve.wait_ge(s_o, b * TB + TB)
                    norm2.statistics(dve, par, it, lambda i: o[:, i, :])
                    dve.wait_ge(s_x, b)
                    norm2.apply(dve, par, it, lambda i: o[:, i, :], lambda i: on[:, i, :], s_on)
                    dve.wait_ge(s_ob, b + 1)
                    xb = k.x[:, ds(b * TB, TB), :]
                    nc.vector.tensor_tensor(xb, xb, on[:, :, :], ALU.add).then_inc(s_x, 1)
                run(dve, body, lambda: finish(B - 1, B // 2 - 1, 1))


def phase_bitlinear(k, w, out):
    nc = k.nc
    with Phase(k, "bit") as ph:
        bank = lambda n, dt: ph.ctx.enter_context(nc.psum_tensor(f"bit_{n}", [P, 512], dt))
        t_bank = [[bank(f"t{p}{c}", BF16) for c in range(KC)] for p in ALLX]
        y_bank = [[bank(f"y{p}{j}", F32) for j in range(2)] for p in ALLX]
        wf, wi = ph.sb("w", [P, KC, D]), ph.sb("wi", [P, KC, D], BF16)
        ident16, ones = ph.sb("ident16", [P, P], BF16), ph.sb("ones", [P, P])
        wsum, wscale, winv = ph.sb("wsum", [P, 1]), ph.sb("wscale", [P, 1]), ph.sb("winv", [P, 1])
        norm = Norm(ph, "ln", EPS_X)
        xn, q = ph.two("xn", [P, TB, D]), ph.two("q", [P, TB, D])
        a, inv, factor = ph.two("a", [P, TB]), ph.two("inv", [P, TB]), ph.two("factor", [P, TB])
        qi, qT = ph.two("qi", [P, TB, D], BF16), ph.two("qT", [P, KC, N], BF16)
        s_w, s_c, s_ws, s_wp = ph.sem("weights"), ph.sem("constants"), ph.sem("weight_steps"), ph.sem("weight_sum")
        s_xn, s_a, s_ae, s_inv, s_fac, s_q = (ph.pair(x) for x in ("xn", "amax", "amax_eps", "inverse", "factor", "quant_steps"))
        s_qi, s_t, s_qT, s_y, s_x, s_st = (ph.pair(x) for x in ("quantised", "turned", "qT", "product", "x_updated", "stored"))
        WSTEPS = 7
        with nc.Block() as block:
            @block.sync
            def _(sp):
                sp.dma_start(wf[:, :, :], rows(w)).then_inc(s_w, 16)
                for it, par, b in batches(sp):
                    sp.wait_ge(s_x[par], it * TB + TB)
                    sp.dma_start(out[ds(b, 1)].rearrange("b (i p) d -> p (b i) d", p=P), k.x[:, ds(b * TB, TB), :]).then_inc(s_st[par], 16)
                for par in ALLX:
                    sp.wait_ge(s_st[par], B // 2 * 16)

            @block.gpsimd
            def _(pool):
                ph.clear_others(pool)
                nc.gpsimd.memset(ones[:, :], 1.0).then_inc(s_c, 1)
                nc.gpsimd.tensor_copy(ident16[:, :], k.ident[:, :]).then_inc(s_c, 1)
                for it, par, b in batches(pool):
                    norm.power(pool, par, it)

            @block.tensor
            def _(pe):
                pe.wait_ge(s_c, 2)
                pe.wait_ge(s_ws, 1)
                nc.tensor.matmul(y_bank[0][0][:, 0:1], ones[:, :], wsum[:, :], start=True, stop=True).then_inc(s_wp, 1)
                pe.wait_ge(s_ws, WSTEPS)
                for it, par, b in batches(pe):
                    pe.wait_ge(s_qi[par], it + 1)
                    pe.wait_ge(s_qT[par], it * KC)
                    for c in range(KC):
                        for i in range(TB):
                            last = nc.tensor.transpose(t_bank[par][c][:, i * P:(i + 1) * P], qi[par][:, i, c * P:(c + 1) * P], ident16[:, :])
                    last.then_inc(s_t[par], 1)
                    pe.wait_ge(s_qT[par], it * KC + KC)
                    pe.wait_ge(s_x[par], it * TB)
                    for i in range(TB):
                        for c in range(KC):
                            last = nc.tensor.matmul(y_bank[par][i // 2][:, (i % 2) * D:(i % 2 + 1) * D], qT[par][:, c, i * P:(i + 1) * P], wi[:, c, :],
                                                    start=(c == 0), stop=(c == KC - 1))
                    last.then_inc(s_y[par], 1)

            @block.scalar
            def _(act):
                for it, par, b in batches(act):
                    act.wait_ge(s_t[par], it + 1)
                    act.wait_ge(s_y[par], it)
                    for c in range(KC):
                        nc.scalar.activation(qT[par][:, c, :], t_bank[par][c][:, :], ACT.Copy).then_inc(s_qT[par], 1)

            @block.vector
            def _(dve):
                dve.wait_ge(s_w, 16)
                n = [0]

                def step(ins):
                    n[0] += 1
                    ins.then_inc(s_ws, 1)
                    dve.wait_ge(s_ws, n[0])
                step(nc.vector.tensor_reduce(wsum[:, :], wf[:, :, :], AX.XY, ALU.add, apply_absolute_value=True))
                dve.wait_ge(s_wp, 1)
                step(nc.vector.tensor_scalar(wscale[:, :], y_bank[0][0][:, 0:1], 1.0 / (D * D), 1e-8, ALU.mult, ALU.add))
                step(nc.vector.reciprocal(winv[:, :], wscale[:, :]))
                step(nc.vector.tensor_scalar(wf[:, :, :], wf[:, :, :], winv[:, :], ROUND, ALU.mult, ALU.add))
                step(nc.vector.tensor_scalar(wf[:, :, :], wf[:, :, :], ROUND, 1.0, ALU.subtract, ALU.min))
                step(nc.vector.tensor_scalar(wi[:, :, :], wf[:, :, :], -1.0, None, ALU.max))
                step(nc.vector.tensor_scalar(wscale[:, :], wscale[:, :], 1.0 / 127.0, None, ALU.mult))
                assert n[0] == WSTEPS

                def update(it, par, b):
                    dve.wait_ge(s_y[par], it + 1)
                    for i in range(TB):
                        xi = k.x[:, ds(b * TB + i, 1), :].rearrange("p a d -> p (a d)")
                        nc.vector.scalar_tensor_tensor(out=xi, in0=y_bank[par][i // 2][:, (i % 2) * D:(i % 2 + 1) * D],
                                                       scalar=factor[par][:, i:i + 1], in1=xi, op0=ALU.mult, op1=ALU.add).then_inc(s_x[par], 1)

                for it, par, b in batches(dve):
                    src = lambda i: k.x[:, ds(b * TB + i, 1), :].rearrange("p a d -> p (a d)")
                    norm.statistics(dve, par, it, src)
                    norm.apply(dve, par, it, src, lambda i: xn[par][:, i, :], s_xn[par])
                    dve.wait_ge(s_xn[par], it * TB + TB)
                    nc.vector.tensor_reduce(a[par][:, :], xn[par][:, :, :], AX.X, ALU.max, apply_absolute_value=True).then_inc(s_a[par], 1)
                    dve.wait_ge(s_a[par], it + 1)
                    nc.vector.tensor_scalar_add(a[par][:, :], a[par][:, :], 1e-8).then_inc(s_ae[par], 1)
                    dve.wait_ge(s_ae[par], it + 1)
                    nc.vector.reciprocal(inv[par][:, :], a[par][:, :]).then_inc(s_inv[par], 1)
                    nc.vector.tensor_scalar(factor[par][:, :], a[par][:, :], wscale[:, :], None, ALU.mult).then_inc(s_fac[par], 1)
                    dve.wait_ge(s_inv[par], it + 1)
                    for i in range(TB):
                        nc.vector.tensor_scalar(q[par][:, i, :], xn[par][:, i, :], inv[par][:, i:i + 1], 127.0, ALU.mult, ALU.mult).then_inc(s_q[par], 1)
                    dve.wait_ge(s_q[par], it * 6 + 4)
                    nc.vector.tensor_scalar(q[par][:, :, :], q[par][:, :, :], 127.0, -128.0, ALU.min, ALU.max).then_inc(s_q[par], 1)
                    dve.wait_ge(s_q[par], it * 6 + 5)
                    nc.vector.tensor_scalar(q[par][:, :, :], q[par][:, :, :], ROUND, None, ALU.add).then_inc(s_q[par], 1)
                    dve.wait_ge(s_q[par], it * 6 + 6)
                    dve.wait_ge(s_t[par], it)
                    nc.vector.tensor_scalar(qi[par][:, :, :], q[par][:, :, :], ROUND, None, ALU.subtract).then_inc(s_qi[par], 1)
                    dve.wait_ge(s_fac[par], it + 1)
                    update(it, par, b)


def build(nc, a, out):
    with ExitStack() as ctx:
        k = Kernel(nc, ctx)
        scratch = lambda name, shape, dt: nc.dram_tensor(name, shape, dt, kind="Internal").ap()
        k.split = scratch("qk_split", [B, 2, 3, D, N], BF16)
        k.values = scratch("v_heads", [B, N, H * VW], F32)
        k.attn = scratch("attn_out", [B, N, D], F32)
        k.slots_in = scratch("slots_in", [SLOTS * P, D], F32)
        k.slots_out = scratch("slots_out", [SLOTS * P, D], F32)
        phase_start(k, a["x"])
        phase_project(k, "proj0", dict(q=a["wq0"], k=a["wk0"], v=a["wv0"], factors=a["factors0"]))
        phase_core(k, "core0", 1.0, causal=True)
        phase_output(k, "out0", a["wo0"])
        phase_project(k, "proj1", dict(q=a["wq1"], k=a["wk1"], v=a["wv1"], bqk=a["bqk1"], bv=a["bv1"]), a["ctx"])
        phase_core(k, "core1", HD ** -0.5, mask=(a["mask_q"], a["mask_k"]))
        phase_output(k, "out1", a["wo1"], a["bo1"])
        moe(k, a["wr"], a["br"], a["moe_w1"], a["moe_b1"], a["moe_w2"], a["moe_b2"])
        phase_retention(k, dict(ret=a["w_ret"], b_ret=a["b_ret"], w1=a["ffn_w1"], b1=a["ffn_b1"], w2=a["ffn_w2"], b2=a["ffn_b2"],
                                ln1s=a["ln1s"], ln1b=a["ln1b"], ln2s=a["ln2s"], ln2b=a["ln2b"]))
        phase_project(k, "proj2", dict(q=a["wq2"], k=a["wk2"], v=a["wv2"], bqk=a["bqk2"], bv=a["bv2"]), a["ctx"])
        phase_core(k, "core2", HD ** -0.5)
        phase_output(k, "out2", a["wo2"], a["bo2"])
        phase_bitlinear(k, a["bit_w"], out)


def kernel(**inputs):
    import numpy as np
    import concourse.bacc as bacc
    from concourse import mybir as mb
    from concourse.bass_utils import run_bass_kernel_spmd

    i = {n: np.asarray(v) for n, v in inputs.items()}
    turned = lambda w: np.ascontiguousarray(w.T)
    by_feature = lambda v: np.ascontiguousarray(v.reshape(-1, P).T)
    heads = lambda s: np.repeat(s, HD)
    mask = np.ascontiguousarray(i["mask_Bx1xSxS2_bk1"][:, 0])
    a = {
        "x": i["x"], "ctx": i["ctx_1024"],
        "mask_q": mask, "mask_k": np.ascontiguousarray(mask.transpose(0, 2, 1)),
        "wq0": turned(i["L0_attn_Wq"]), "wk0": turned(i["L0_attn_Wk"]), "wv0": turned(i["L0_attn_Wv"]), "wo0": turned(i["L0_attn_Wo"]),
        "factors0": by_feature(np.concatenate([heads(i["L0_attn_q_scale"]), heads(i["L0_attn_k_scale"])])),
        "wq1": i["L0_xattn_Wq"], "wk1": i["L0_xattn_Wk"], "wv1": i["L0_xattn_Wv"], "wo1": i["L0_xattn_Wo"],
        "bqk1": by_feature(np.concatenate([i["L0_xattn_bq"], i["L0_xattn_bk"]])), "bv1": i["L0_xattn_bv"], "bo1": i["L0_xattn_bo"],
        "wr": i["L0_ffn_wr"], "br": i["L0_ffn_br"], "moe_w1": i["L0_ffn_w1"], "moe_b1": by_feature(i["L0_ffn_b1"]),
        "moe_w2": i["L0_ffn_w2"], "moe_b2": i["L0_ffn_b2"],
        "w_ret": i["L1_attn_W_ret"], "b_ret": by_feature(i["L1_attn_b_ret"]), "ffn_w1": i["L1_attn_W1"], "ffn_b1": by_feature(i["L1_attn_b1"]),
        "ffn_w2": i["L1_attn_W2"], "ffn_b2": i["L1_attn_b2"], "ln1s": i["L1_attn_ln1_scale"], "ln1b": i["L1_attn_ln1_bias"],
        "ln2s": i["L1_attn_ln2_scale"], "ln2b": i["L1_attn_ln2_bias"],
        "wq2": i["L1_xattn_W_Q"], "wk2": i["L1_xattn_W_K"], "wv2": i["L1_xattn_W_V"], "wo2": i["L1_xattn_W_O"],
        "bqk2": by_feature(np.concatenate([i["L1_xattn_b_Q"], i["L1_xattn_b_K"]])), "bv2": i["L1_xattn_b_V"], "bo2": i["L1_xattn_b_O"],
        "bit_w": turned(i["L1_ffn_weight"]),
    }
    nc = bacc.Bacc("TRN2", target_bir_lowering=False, num_devices=1)
    arrays = {f"in_{n}": v for n, v in a.items()}
    args = {n: nc.dram_tensor(f"in_{n}", v.shape, mb.dt.from_np(v.dtype), kind="ExternalInput").ap() for n, v in a.items()}
    out = nc.dram_tensor("out_x", (B, N, D), F32, kind="ExternalOutput").ap()
    build(nc, args, out)
    r = run_bass_kernel_spmd(nc, [arrays], core_ids=[0])
    return r.results[0]["out_x"]
```

```python
import concourse.bass as bass
from concourse import mybir
from concourse.alu_op_type import AluOpType as ALU
from contextlib import ExitStack

F32 = mybir.dt.float32
BF16 = mybir.dt.bfloat16
U8 = mybir.dt.uint8
U32 = mybir.dt.uint32
I32 = mybir.dt.int32
ACT = mybir.ActivationFunctionType
AX = mybir.AxisListType
ds = bass.ds

P = 128
B, N, D, H = 8, 512, 256, 16
HD = D // H
TB = N // P
NT = B * TB
KC = D // P
F = 1024
FC = F // P
E = 8
VW = 32
REP = 6
SROWS = REP * HD
MROWS = SROWS + 3
Q_REPS = [(0, 0), (1, 0), (2, 0), (3, 1), (4, 1), (5, 2)]
K_REPS = [(0, 0), (1, 1), (2, 2), (3, 0), (4, 1), (5, 0)]
NEG = -float(2 ** 50)
NEG_CAUSAL = -float(2 ** 100)
QUADS = H // 4
STEPS = QUADS * TB
UNITS = H * TB
ALLX = (0, 1)


SEM_BASE, SEM_BANK = 99, 72


class Phase:

    def __init__(self, k, tag):
        self.k, self.nc, self.tag = k, k.nc, tag
        self.ctx, self.sems = ExitStack(), {}
        self.low = SEM_BASE + SEM_BANK * (k.phases % 2)
        self.others = range(SEM_BASE + SEM_BANK * ((k.phases + 1) % 2), SEM_BASE + SEM_BANK * ((k.phases + 1) % 2) + SEM_BANK)
        self.clears = k.phases > 0
        k.phases += 1

    def __enter__(self):
        return self

    def __exit__(self, *e):
        self.ctx.close()

    def sb(self, name, shape, dt=F32):
        return self.ctx.enter_context(self.nc.sbuf_tensor(f"{self.tag}_{name}", shape, dt))

    def two(self, name, shape, dt=F32):
        return [self.sb(f"{name}{p}", shape, dt) for p in ALLX]

    def banks(self):
        return [self.ctx.enter_context(self.nc.psum_tensor(f"{self.tag}_bank{i}", [P, 512], F32)) for i in range(8)]

    def sem(self, name):
        if name not in self.sems:
            assert len(self.sems) < SEM_BANK
            self.sems[name] = self.ctx.enter_context(self.nc.semaphore(f"{self.tag}_{name}", num=self.low + len(self.sems)))
        return self.sems[name]

    def pair(self, name):
        return [self.sem(f"{name}_even"), self.sem(f"{name}_odd")]

    def own_sem(self, name):
        return self.ctx.enter_context(self.nc.semaphore(f"{self.tag}_{name}", num=self.k.next_own_sem()))

    def clear_others(self, pool):
        if self.clears:
            pool.sem_clear(self.others)


class Kernel:

    def __init__(self, nc, ctx):
        self.nc, self.ctx, self.phases, self.own_sems = nc, ctx, 0, 0

    def next_own_sem(self):
        self.own_sems += 1
        return SEM_BASE + 2 * SEM_BANK + self.own_sems - 1


def batches(eng):
    for par in ALLX:
        yield 0, par, par
    with eng.Fori(1, B // 2) as it:
        for par in ALLX:
            yield it, par, it * 2 + par


def pipelined(eng):
    for par in ALLX:
        yield 0, par, par, par == 0, 2
    with eng.Fori(1, B // 2 - 1) as it:
        for par in ALLX:
            yield it, par, it * 2 + par, False, 2
    for par in ALLX:
        yield B // 2 - 1, par, B - 2 + par, False, 1 - par


def after(it, par):
    return (it, 1) if par == 0 else (it + 1, 0)


def prior(it, par):
    return (it, 0) if par else (it - 1, 1)


def wait_apart(ph, eng, sem, value):
    eng.wait_ge(sem, value)
    eng.sem_inc(ph.sem("waits_passed"), 1)


def before(pair, it, par, each):
    return (pair[0], it * each + each) if par else (pair[1], it * each)


def phase_start(k, x_dram):
    nc = k.nc
    ph = Phase(k, "start")
    sb = lambda name, shape, dt: k.ctx.enter_context(nc.sbuf_tensor(name, shape, dt))
    k.x = sb("x_res", [P, NT, D], F32)
    k.ident = sb("ident", [P, P], F32)
    k.minus_half = sb("minus_half", [P, TB], F32)
    made = ph.sem("const_made")
    k.x_first, k.x_rest = (k.ctx.enter_context(nc.semaphore(name, num=k.next_own_sem())) for name in ("x_first", "x_rest"))
    with nc.Block() as block:
        @block.sync
        def _(sp):
            tiles = x_dram.rearrange("b (i p) d -> p (b i) d", p=P)
            sp.dma_start(k.x[:, 0:2 * TB, :], tiles[:, 0:2 * TB, :]).then_inc(k.x_first, 16)
            sp.dma_start(k.x[:, 2 * TB:NT, :], tiles[:, 2 * TB:NT, :]).then_inc(k.x_rest, 16)

        @block.gpsimd
        def _(pool):
            nc.gpsimd.memset(k.minus_half[:, :], -0.5).then_inc(made, 1)
            nc.gpsimd.memset(k.ident[:, :], 0.0).then_inc(made, 1)
            pool.wait_ge(made, 2)
            nc.gpsimd.affine_select(out=k.ident[:, :], in_=k.ident[:, :], compare_op=ALU.not_equal, fill=1.0,
                                    base=0, pattern=[[-1, P]], channel_multiplier=1).then_inc(made, 1)
            pool.wait_ge(made, 3)
    ph.ctx.close()


class Norm:

    def __init__(self, ph, tag, eps):
        self.ph, self.nc, self.k, self.eps = ph, ph.nc, ph.k, eps
        self.stats = ph.two(f"{tag}_stats", [P, TB, 6])
        self.mv = ph.two(f"{tag}_mean_var", [P, TB, 2])
        self.ve = ph.two(f"{tag}_var_eps", [P, TB])
        self.rstd = ph.two(f"{tag}_rstd", [P, TB])
        self.s_stats, self.s_mv = ph.pair(f"{tag}_stats"), ph.pair(f"{tag}_mean_var")
        self.s_ve, self.s_rstd = ph.pair(f"{tag}_var_eps"), ph.pair(f"{tag}_rstd")

    def statistics(self, dve, par, n, src):
        nc = self.nc
        for i in range(TB):
            nc.vector.bn_stats(self.stats[par][:, i, :], src(i)).then_inc(self.s_stats[par], 1)
        wait_apart(self.ph, dve, self.s_stats[par], n * TB + TB)
        for i in range(TB):
            nc.vector.bn_aggr(self.mv[par][:, i, :], self.stats[par][:, i, :]).then_inc(self.s_mv[par], 1)
        dve.wait_ge(self.s_mv[par], n * TB + TB)
        nc.vector.tensor_scalar_add(self.ve[par][:, :], self.mv[par][:, :, 1], self.eps).then_inc(self.s_ve[par], 1)

    def power(self, pool, par, n):
        pool.wait_ge(self.s_ve[par], n + 1)
        self.nc.gpsimd.tensor_tensor(self.rstd[par][:, :], self.ve[par][:, :], self.k.minus_half[:, :],
                                     ALU.pow).then_inc(self.s_rstd[par], 1)

    def apply(self, dve, par, n, src, dst, done):
        dve.wait_ge(self.s_rstd[par], n + 1)
        for i in range(TB):
            self.nc.vector.tensor_scalar(dst(i), src(i), self.mv[par][:, i, 0:1], self.rstd[par][:, i:i + 1],
                                         ALU.subtract, ALU.mult).then_inc(done, 1)


EPS_X = 1e-5
EPS_NORM = 1e-6
QK4 = [(0, 0), (0, 1), (1, 0), (1, 1)]


def rows(w_dram):
    return w_dram.rearrange("(c p) n -> p c n", p=P)


def over_partitions(row):
    return row.rearrange("(a n) -> a n", a=1).broadcast_to((P, row.shape[0]))


def phase_project(k, tag, w, ctx_dram=None):
    nc, own = k.nc, ctx_dram is None
    with Phase(k, tag) as ph:
        ps = ph.banks()
        wq, wk, wv = (ph.sb(x, [P, KC, D]) for x in ("wq", "wk", "wv"))
        small = ph.sb("small", [P, 4])
        norm = Norm(ph, "ln", EPS_X)
        xn, xnT = ph.two("xn", [P, TB, D]), ph.two("xnT", [P, KC, N])
        qk = [[ph.sb(f"qk{par}_{j}", [P, N]) for j in range(4)] for par in ALLX]
        rest = [ph.sb(f"rest{j}", [P, N]) for j in range(4)]
        parts = ph.two("parts", [P, 2, KC, 3, N], BF16)
        vst = ph.two("v", [P, TB, H, VW])
        if own:
            square = [ph.sb(f"square{j}", [P, N]) for j in range(4)]
            root, ratio, factor = (ph.sb(x, [P, N]) for x in ("root", "ratio", "factor"))
            head_of = ph.sb("head_of", [P, 32])
            spread = ph.sb("spread", [P, 4, P])
            spreadT = ph.sb("spreadT", [P, 4, P])
            s_sq, s_n2, s_rt = ph.pair("square"), ph.pair("norm2"), ph.pair("root")
            s_den, s_rec, s_fac, s_sc = (ph.pair(x) for x in ("denominator", "reciprocal", "factor", "scaled"))
            s_bc, s_spread = ph.pair("factor_spread"), ph.sem("spread_steps")
        else:
            cx, cxT = ph.two("cx", [P, TB, D]), ph.two("cxT", [P, KC, N])
            bv = ph.sb("bv", [P, D])
            s_cx, s_cT, s_cxT = ph.pair("ctx_loaded"), ph.pair("ctx_turned"), ph.pair("ctxT")
        s_w, s_zero, s_ones, s_same = (ph.sem(x) for x in ("weights", "v_zeroed", "v_ones", "heads_matched"))
        s_xn, s_xT, s_xnT = ph.pair("xn"), ph.pair("x_turned"), ph.pair("xnT")
        s_mm, s_ev = ph.pair("qk_product"), ph.pair("qk_out")
        s_vm, s_vev = ph.pair("v_product"), ph.pair("v_out")
        s_hi, s_rest, s_mid, s_lo = ph.pair("high"), ph.pair("rest"), ph.pair("middle"), ph.pair("low")
        s_st = ph.pair("stored")
        w_all = 16 * (4 if own else 5)
        with nc.Block() as block:
            @block.sync
            def _(sp):
                for dst, src in ((wq, w["q"]), (wk, w["k"]), (wv, w["v"])):
                    sp.dma_start(dst[:, :, :], rows(src)).then_inc(s_w, 16)
                if own:
                    sp.dma_start(small[:, :], w["factors"]).then_inc(s_w, 16)
                else:
                    sp.dma_start(small[:, :], w["bqk"]).then_inc(s_w, 16)
                    sp.dma_start(bv[:, :], over_partitions(w["bv"])).then_inc(s_w, 16)
                sp.wait_ge(s_ones, 2)
                for it, par, b in batches(sp):
                    sp.wait_ge(s_vev[par], it * 4 + 4)
                    sp.dma_start(k.values[ds(b, 1)].rearrange("b (i p) f -> p (b i) f", p=P),
                                 vst[par][:, :, :, :].rearrange("p i h w -> p i (h w)")).then_inc(s_st[par], 16)
                    for j, (s, m) in enumerate(QK4):
                        for made in (s_hi, s_mid, s_lo):
                            sp.wait_ge(made[par], it * 4 + j + 1)
                        sp.dma_start(k.split[ds(b, 1), s, :, m * P:(m + 1) * P, :].rearrange("b c p t -> p (b c) t"),
                                     parts[par][:, s, m, :, :]).then_inc(s_st[par], 16)
                for par in ALLX:
                    sp.wait_ge(s_st[par], B // 2 * 80)

            @block.gpsimd
            def _(pool):
                ph.clear_others(pool)
                if own:
                    nc.gpsimd.memset(head_of[:, :], 1.0).then_inc(s_same, 1)
                    pool.wait_ge(s_same, 1)
                    nc.gpsimd.affine_select(out=head_of[:, :], in_=head_of[:, :], compare_op=ALU.is_ge, fill=0.0, base=0,
                                            pattern=[[-HD, 32]], channel_multiplier=1).then_inc(s_same, 1)
                    pool.wait_ge(s_same, 2)
                    nc.gpsimd.affine_select(out=head_of[:, :], in_=head_of[:, :], compare_op=ALU.is_ge, fill=0.0, base=HD - 1,
                                            pattern=[[HD, 32]], channel_multiplier=-1).then_inc(s_same, 1)
                for p in ALLX:
                    norm.power(pool, p, 0)
                for p in ALLX:
                    nc.gpsimd.memset(vst[p][:, :, :, :], 0.0).then_inc(s_zero, 1)

                def low(it, par):
                    for j, (s, m) in enumerate(QK4):
                        pool.wait_ge(s_rest[par], it * 4 + j + 1)
                        pool.wait_ge(s_mid[par], it * 4 + j + 1)
                        nc.gpsimd.tensor_tensor(parts[par][:, s, m, 2, :], rest[j][:, :], parts[par][:, s, m, 1, :],
                                                ALU.subtract).then_inc(s_lo[par], 1)

                for it, par, b, first, left in pipelined(pool):
                    if left == 2:
                        norm.power(pool, par, it + 1)
                    if own:
                        if not first:
                            pool.wait_ge(*before(s_n2, it, par, 1))
                        for j in range(4):
                            pool.wait_ge(s_ev[par], it * 4 + j + 1)
                            nc.gpsimd.tensor_tensor(square[j][:, :], qk[par][j][:, :], qk[par][j][:, :], ALU.mult).then_inc(s_sq[par], 1)
                    if not first:
                        low(*prior(it, par))
                low(B // 2 - 1, 1)

            @block.tensor
            def _(pe):
                def turn_x(it, par):
                    pe.wait_ge(s_xn[par], it * TB + TB)
                    pe.wait_ge(*before(s_xnT, it, par, KC))
                    if own:
                        pe.wait_ge(s_rt[par], it)
                    for c in range(KC):
                        for i in range(TB):
                            last = nc.tensor.transpose(ps[c][:, i * P:(i + 1) * P], xn[par][:, i, c * P:(c + 1) * P], k.ident[:, :])
                    last.then_inc(s_xT[par], 1)

                def turn_ctx(it, par):
                    pe.wait_ge(s_cx[par], it * 16 + 16)
                    pe.wait_ge(*before(s_cxT, it, par, KC))
                    pe.wait_ge(s_vev[par], it * 4)
                    for c in range(KC):
                        for i in range(TB):
                            last = nc.tensor.transpose(ps[6 + c][:, i * P:(i + 1) * P], cx[par][:, i, c * P:(c + 1) * P], k.ident[:, :])
                    last.then_inc(s_cT[par], 1)

                def products(j, it, par):
                    s, m = QK4[j]
                    src, ww = (xnT, wq) if s == 0 else (xnT if own else cxT, wk)
                    pe.wait_ge(*before(s_ev, it, par, 4))
                    for c in range(KC):
                        last = nc.tensor.matmul(ps[2 + j][:, :], ww[:, c, m * P:(m + 1) * P], src[par][:, c, :],
                                                start=(c == 0), stop=(c == KC - 1))
                    last.then_inc(s_mm[par], 1)

                def spread_factors(j, it, par):
                    pe.wait_ge(s_fac[par], it + 1)
                    if j < 2:
                        pe.wait_ge(s_vev[par], it * 4 + 4)
                    else:
                        pe.wait_ge(s_sc[par], it * 4 + j - 1)
                    nc.tensor.matmul(ps[6 + j % 2][:, :], spreadT[:, j, :], factor[:, :], start=True, stop=True).then_inc(s_bc[par], 1)

                pe.wait_ge(s_w, w_all)
                turn_x(0, 0)
                if own:
                    pe.wait_ge(s_spread, 5)
                    for j in range(4):
                        last = nc.tensor.transpose(ps[7][:, j * P:(j + 1) * P], spread[:, j, :], k.ident[:, :])
                    last.then_inc(s_spread, 1)
                else:
                    turn_ctx(0, 0)
                for it, par, b, first, left in pipelined(pe):
                    if own:
                        pe.wait_ge(s_spread, 7)
                    pe.wait_ge(s_xnT[par], it * KC + KC)
                    products(0, it, par)
                    products(1, it, par)
                    if left:
                        nit, npar = after(it, par)
                        turn_x(nit, npar)
                        if not own:
                            turn_ctx(nit, npar)
                    if own:
                        for m in range(2):
                            products(2 + m, it, par)
                            if not first:
                                spread_factors(2 * m, *prior(it, par))
                                spread_factors(2 * m + 1, *prior(it, par))
                    else:
                        pe.wait_ge(s_cxT[par], it * KC + KC)
                        products(2, it, par)
                        products(3, it, par)
                        if left:
                            pe.wait_ge(s_cxT[npar], nit * KC + KC)
                        else:
                            pe.wait_ge(*before(s_vev, it, par, 4))
                    src = xnT if own else cxT
                    for i in range(TB):
                        if own and not first and i % 2 == 0:
                            pit, ppar = prior(it, par)
                            pe.wait_ge(s_sc[ppar], pit * 4 + 3 + i // 2)
                        for c in range(KC):
                            last = nc.tensor.matmul(ps[6 + i // 2][:, (i % 2) * D:(i % 2 + 1) * D], src[par][:, c, i * P:(i + 1) * P],
                                                    wv[:, c, :], start=(c == 0), stop=(c == KC - 1))
                        if i % 2:
                            last.then_inc(s_vm[par], 1)
                    if own:
                        if left:
                            pe.wait_ge(s_xnT[npar], nit * KC + KC)
                        pe.wait_ge(s_sq[par], it * 4 + 4)
                        for j in range(4):
                            last = nc.tensor.matmul(ps[0][32 * j:32 * j + 32, :], head_of[:, :], square[j][:, :], start=True, stop=True)
                        last.then_inc(s_n2[par], 1)
                if own:
                    for j in range(4):
                        spread_factors(j, B // 2 - 1, 1)

            @block.scalar
            def _(act):
                def copies_x(it, par):
                    act.wait_ge(s_xT[par], it + 1)
                    act.wait_ge(s_vm[par], it * 2)
                    for c in range(KC):
                        nc.scalar.activation(xnT[par][:, c, :], ps[c][:, :], ACT.Copy).then_inc(s_xnT[par], 1)

                def copies_ctx(it, par):
                    act.wait_ge(s_cT[par], it + 1)
                    for c in range(KC):
                        nc.scalar.activation(cxT[par][:, c, :], ps[6 + c][:, :], ACT.Copy).then_inc(s_cxT[par], 1)

                def load_ctx(b, par):
                    act.dma_start(cx[par][:, :, :], ctx_dram[ds(b, 1)].rearrange("b (i p) d -> p (b i) d", p=P)).then_inc(s_cx[par], 16)

                def out(j, it, par):
                    act.wait_ge(s_mm[par], it * 4 + j + 1)
                    if own:
                        nc.scalar.activation(qk[par][j][:, :], ps[2 + j][:, :], ACT.Silu).then_inc(s_ev[par], 1)
                    else:
                        nc.scalar.activation(qk[par][j][:, :], ps[2 + j][:, :], ACT.Identity, bias=small[:, j:j + 1]).then_inc(s_ev[par], 1)

                def high(j, it, par):
                    act.wait_ge(s_sc[par] if own else s_ev[par], it * 4 + j + 1)
                    s, m = QK4[j]
                    nc.scalar.activation(parts[par][:, s, m, 0, :], qk[par][j][:, :], ACT.Copy).then_inc(s_hi[par], 1)

                def middle(j, it, par):
                    act.wait_ge(s_rest[par], it * 4 + j + 1)
                    s, m = QK4[j]
                    nc.scalar.activation(parts[par][:, s, m, 1, :], rest[j][:, :], ACT.Copy).then_inc(s_mid[par], 1)

                def split(it, par, outs):
                    act.wait_ge(s_st[par], it * 80)
                    for j in range(4):
                        if j % 2 == 0:
                            for other in outs[j // 2:j // 2 + 1]:
                                out(*other)
                        high(j, it, par)
                        if j >= 2:
                            middle(j - 2, it, par)
                    middle(2, it, par)
                    middle(3, it, par)

                if not own:
                    for par in ALLX:
                        load_ctx(par, par)
                act.wait_ge(s_w, w_all)
                copies_x(0, 0)
                if own:
                    act.wait_ge(s_spread, 6)
                    nc.scalar.activation(spreadT[:, :, :].rearrange("p j f -> p (j f)"), ps[7][:, :], ACT.Copy).then_inc(s_spread, 1)
                else:
                    copies_ctx(0, 0)
                act.wait_ge(s_zero, 2)
                for it, par, b, first, left in pipelined(act):
                    if not own and left == 2:
                        act.wait_ge(s_cT[par], it + 1)
                        load_ctx(b + 2, par)
                    act.wait_ge(s_rest[par], it * 4)
                    out(0, it, par)
                    out(1, it, par)
                    if left:
                        copies_x(*after(it, par))
                        if not own:
                            copies_ctx(*after(it, par))
                    late = [(2, it, par), (3, it, par)]
                    if first:
                        for other in late:
                            out(*other)
                    else:
                        split(*prior(it, par), late)
                    if own:
                        act.wait_ge(s_st[par], it * 80)
                        for i in range(TB):
                            act.wait_ge(s_vm[par], it * 2 + i // 2 + 1)
                            nc.scalar.activation(vst[par][:, i, :, 0:HD],
                                                 ps[6 + i // 2][:, (i % 2) * D:(i % 2 + 1) * D].rearrange("p (h e) -> p h e", e=HD),
                                                 ACT.Silu).then_inc(s_vev[par], 1)
                        act.wait_ge(s_n2[par], it + 1)
                        if not first:
                            act.wait_ge(*before(s_fac, it, par, 1))
                        nc.scalar.activation(root[:, :], ps[0][:, :], ACT.Sqrt).then_inc(s_rt[par], 1)
                split(B // 2 - 1, 1, [])

            @block.vector
            def _(dve):
                src = lambda b: (lambda i: k.x[:, ds(b * TB + i, 1), :].rearrange("p a d -> p (a d)"))

                def factors(it, par):
                    dve.wait_ge(s_rt[par], it + 1)
                    nc.vector.tensor_scalar_add(ratio[:, :], root[:, :], EPS_NORM).then_inc(s_den[par], 1)
                    dve.wait_ge(s_den[par], it + 1)
                    nc.vector.reciprocal(ratio[:, :], ratio[:, :]).then_inc(s_rec[par], 1)
                    dve.wait_ge(s_rec[par], it + 1)
                    dve.wait_ge(*before(s_bc, it, par, 4))
                    nc.vector.tensor_tensor(factor[:, :], ratio[:, :], root[:, :], ALU.mult).then_inc(s_fac[par], 1)

                def scale(j, it, par):
                    dve.wait_ge(s_bc[par], it * 4 + j + 1)
                    nc.vector.tensor_tensor(qk[par][j][:, :], qk[par][j][:, :], ps[6 + j % 2][:, :], ALU.mult).then_inc(s_sc[par], 1)

                def rests(j, it, par):
                    dve.wait_ge(*before(s_lo, it, par, 4))
                    dve.wait_ge(s_hi[par], it * 4 + j + 1)
                    s, m = QK4[j]
                    nc.vector.tensor_tensor(rest[j][:, :], qk[par][j][:, :], parts[par][:, s, m, 0, :], ALU.subtract).then_inc(s_rest[par], 1)

                def back(it, par):
                    if own:
                        scale(0, it, par)
                        scale(1, it, par)
                        rests(0, it, par)
                        scale(2, it, par)
                        rests(1, it, par)
                        scale(3, it, par)
                        rests(2, it, par)
                        rests(3, it, par)
                    else:
                        for j in range(4):
                            rests(j, it, par)

                if own:
                    dve.wait_ge(k.x_first, 16)
                for p in ALLX:
                    norm.statistics(dve, p, 0, src(p))
                for p in ALLX:
                    norm.apply(dve, p, 0, src(p), lambda i: xn[p][:, i, :], s_xn[p])
                    if p == 0 and own:
                        nc.vector.memset(spread[:, :, :], 0.0).then_inc(s_spread, 1)
                        dve.wait_ge(s_spread, 1)
                        dve.wait_ge(s_same, 3)
                        dve.wait_ge(s_w, w_all)
                        for j in range(4):
                            nc.vector.tensor_scalar(spread[:, j, 32 * j:32 * j + 32], head_of[:, :], small[:, j:j + 1], None,
                                                    ALU.mult).then_inc(s_spread, 1)
                dve.wait_ge(s_w, w_all)
                dve.wait_ge(s_zero, 2)
                if own:
                    dve.wait_ge(k.x_rest, 16)
                for p in ALLX:
                    nc.vector.memset(vst[p][:, :, :, HD:HD + 1], 1.0).then_inc(s_ones, 1)
                for it, par, b, first, left in pipelined(dve):
                    if left == 2:
                        norm.statistics(dve, par, it + 1, src(b + 2))
                    if not first and own:
                        factors(*prior(it, par))
                    if left == 2:
                        dve.wait_ge(s_xT[par], it + 1)
                        norm.apply(dve, par, it + 1, src(b + 2), lambda i: xn[par][:, i, :], s_xn[par])
                    if not first:
                        back(*prior(it, par))
                    if not own:
                        dve.wait_ge(s_st[par], it * 80)
                        for i in range(TB):
                            dve.wait_ge(s_vm[par], it * 2 + i // 2 + 1)
                            nc.vector.tensor_tensor(vst[par][:, i, :, 0:HD],
                                                    ps[6 + i // 2][:, (i % 2) * D:(i % 2 + 1) * D].rearrange("p (h e) -> p h e", e=HD),
                                                    bv[:, :].rearrange("p (h e) -> p h e", e=HD), ALU.add).then_inc(s_vev[par], 1)
                if own:
                    factors(B // 2 - 1, 1)
                back(B // 2 - 1, 1)


def phase_core(k, tag, scale, causal=False, mask=None):
    nc = k.nc
    ahead = UNITS // 2 + (24 if causal else 20)
    next_step = (UNITS - ahead) // 4
    turn_step = next_step + 1
    with Phase(k, tag) as ph:
        p_ctx = ph.ctx
        s_bank = [p_ctx.enter_context(nc.psum_tensor(f"{tag}_s{j}", [P, N], F32)) for j in range(2)]
        t_bank = [p_ctx.enter_context(nc.psum_tensor(f"{tag}_t{j}", [P, 2, N], F32)) for j in range(2)]
        o_bank = p_ctx.enter_context(nc.psum_tensor(f"{tag}_o", [P, N], F32))
        m_bank = p_ctx.enter_context(nc.psum_tensor(f"{tag}_m", [P, N], F32))
        qs, ks = ph.two("qs", [P, H, N], BF16), ph.two("ks", [P, H, N], BF16)
        vs = ph.two("vs", [P, TB, H * VW])
        probs = ph.two("probs", [P, 4, N])
        rowmax = ph.two("rowmax", [P, TB, H])
        scratch = ph.two("scratch", [P, N])
        negmax, negrest = ph.sb("negmax", [H // 2, N]), ph.sb("negrest", [H // 2, N])
        negpart = ph.two("negpart", [H // 2, 3, N], BF16)
        turned = ph.two("turned", [P, N])
        recip = ph.sb("recip", [P, 4 * TB])
        attn = ph.two("attn", [P, TB, D])
        masked = causal or mask is not None
        neg = NEG_CAUSAL if causal else NEG
        if masked:
            neg_ident = ph.sb("neg_ident", [P, P], BF16)
        if causal:
            ahead_k = ph.sb("ahead_k", [P, P], BF16)
            ahead_q = ph.sb("ahead_q", [P, N])
        if mask is not None:
            raw_q, raw_k = ph.two("raw_q", [P, TB, N], U8), ph.two("raw_k", [P, TB, N], U8)
            add_q, one_k = ph.two("add_q", [P, TB, N], BF16), ph.two("one_k", [P, TB, N], BF16)
            s_raw, s_addq, s_onek = ph.pair("mask_loaded"), ph.pair("mask_added"), ph.pair("mask_ones")
        s_const, s_rows1, s_rows0 = ph.sem("constants"), ph.sem("one_rows_odd"), ph.sem("one_rows_even")
        s_ld = [ph.pair(f"stacks_loaded_half{h}") for h in range(2)]
        s_v = ph.pair("values_loaded")
        s_s, s_max = ph.pair("scores"), ph.pair("maxima")
        s_mt, s_nm, s_nh, s_nr, s_nmid, s_nlo = (ph.sem(x) for x in ("max_turned", "neg", "neg_high", "neg_rest", "neg_middle", "neg_low"))
        s_mrow = [ph.pair(f"max_rows_half{h}") for h in range(2)]
        s_t, s_exp = ph.pair("scoresT"), ph.pair("probs")
        s_pv, s_out = ph.pair("probs_used"), ph.sem("quad_out")
        s_ot, s_rc, s_norm = ph.pair("quad_turned"), ph.sem("reciprocals"), ph.sem("normalised")
        s_store = ph.pair("attn_stored")
        LOADS = len(Q_REPS) + len(K_REPS)

        def stack_loads(eng, b, par, half, reps, s, dst):
            for r, part in reps:
                src = k.split[ds(b, 1), s, part, half * P:(half + 1) * P, :].rearrange("b (h e) t -> e (b h) t", e=HD)
                eng.dma_start(dst[par][r * HD:(r + 1) * HD, half * 8:half * 8 + 8, :], src).then_inc(s_ld[half][par], 16)

        with nc.Block() as block:
            @block.sync
            def _(sp):
                def load_stacks(half, b, par):
                    stack_loads(sp, b, par, half, Q_REPS, 0, qs)
                    stack_loads(sp, b, par, half, K_REPS, 1, ks)

                def load_values(b, par):
                    sp.dma_start(vs[par][:, :, :], k.values[ds(b, 1)].rearrange("b (i p) f -> p (b i) f", p=P)).then_inc(s_v[par], 16)

                def load_mask(b, par):
                    for raw, src in ((raw_q, mask[0]), (raw_k, mask[1])):
                        sp.dma_start(raw[par][:, :, :], src[ds(b, 1)].rearrange("b (i p) t -> p (b i) t", p=P)).then_inc(s_raw[par], 16)

                def store(b, it, par, nth):
                    sp.wait_ge(s_norm, (nth * QUADS + QUADS) * 2)
                    sp.dma_start(k.attn[ds(b, 1)].rearrange("b (i p) d -> p (b i) d", p=P), attn[par][:, :, :]).then_inc(s_store[par], 16)

                for par in ALLX:
                    for half in range(2):
                        if par == 0:
                            stack_loads(sp, 0, 0, half, Q_REPS, 0, qs)
                        else:
                            load_stacks(half, par, par)
                    if mask is not None:
                        load_mask(par, par)
                    load_values(par, par)
                with sp.Fori(0, B // 2 - 1) as it:
                    for par in ALLX:
                        nth = it * 2 + par
                        if mask is not None:
                            sp.wait_ge(s_addq[par], it + 1)
                            sp.wait_ge(s_onek[par], it + 1)
                            load_mask(nth + 2, par)
                        for half in range(2):
                            sp.wait_ge(s_t[1], nth * STEPS + (half + 1) * STEPS // 2)
                            load_stacks(half, nth + 2, par)
                        wait_apart(ph, sp, s_pv[1], nth * (STEPS // 2) + STEPS // 2)
                        load_values(nth + 2, par)
                        store(nth, it, par, nth)
                for par in ALLX:
                    store(B - 2 + par, B // 2 - 1, par, B - 2 + par)
                for par in ALLX:
                    sp.wait_ge(s_store[par], B // 2 * 16)

            @block.gpsimd
            def _(pool):
                ph.clear_others(pool)
                n = 0
                if masked:
                    nc.gpsimd.memset(neg_ident[:, :], 0.0).then_inc(s_const, 1)
                    pool.wait_ge(s_const, 1)
                    nc.gpsimd.affine_select(out=neg_ident[:, :], in_=neg_ident[:, :], compare_op=ALU.not_equal, fill=neg,
                                            base=0, pattern=[[-1, P]], channel_multiplier=1).then_inc(s_const, 1)
                    n = 2
                if causal:
                    nc.gpsimd.memset(ahead_k[:, :], 1.0).then_inc(s_const, 1)
                    nc.gpsimd.memset(ahead_q[:, :], 0.0).then_inc(s_const, 1)
                    pool.wait_ge(s_const, n + 2)
                    nc.gpsimd.affine_select(out=ahead_k[:, :], in_=ahead_k[:, :], compare_op=ALU.is_gt, fill=0.0,
                                            base=0, pattern=[[-1, P]], channel_multiplier=1).then_inc(s_const, 1)
                    nc.gpsimd.affine_select(out=ahead_q[:, N - P:N], in_=ahead_q[:, N - P:N], compare_op=ALU.is_ge, fill=neg,
                                            base=0, pattern=[[-1, P]], channel_multiplier=1).then_inc(s_const, 1)
                    n += 4
                if n:
                    pool.wait_ge(s_const, n)
                nc.gpsimd.memset(ks[1][SROWS:MROWS, :, :], 1.0).then_inc(s_rows1, 1)
                pool.wait_ge(s_rows1, 1)

                def masks(it, par):
                    wait_apart(ph, pool, s_raw[par], it * 32 + 32)
                    nc.gpsimd.tensor_scalar(add_q[par][:, :, :], raw_q[par][:, :, :], neg, None, ALU.mult).then_inc(s_addq[par], 1)
                    nc.gpsimd.tensor_copy(one_k[par][:, :, :], raw_k[par][:, :, :]).then_inc(s_onek[par], 1)

                def rests(half, done):
                    pool.wait_ge(s_nh, done + 1)
                    nc.gpsimd.tensor_tensor(negrest[:, :], negmax[:, :], negpart[half][:, 0, :], ALU.subtract).then_inc(s_nr, 1)
                    pool.wait_ge(s_nmid, done + 1)
                    nc.gpsimd.tensor_tensor(negpart[half][:, 2, :], negrest[:, :], negpart[half][:, 1, :], ALU.subtract).then_inc(s_nlo, 1)

                if mask is not None:
                    for par in ALLX:
                        masks(0, par)
                rests(0, 0)
                for it, par, nth, first, left in pipelined(pool):
                    rests(1, nth * 2 + 1)
                    if left:
                        rests(0, nth * 2 + 2)
                    if mask is not None and left == 2:
                        for j in range(2):
                            pool.wait_ge(s_max[j], (nth + 1) * (UNITS // 2))
                        pool.wait_ge(s_t[1], (nth + 1) * STEPS)
                        masks(it + 1, par)

            def units_of(s, nth, par, last):
                first = ahead + 4 * s
                if first < UNITS:
                    return [(u, nth, par) for u in range(first, first + 4)]
                return [] if last else [(u - UNITS, nth + 1, 1 - par) for u in range(first, first + 4)]

            def unit(u):
                h, i = u // TB, u % TB
                return h, i, ((i + 1) * P if causal else N)

            @block.tensor
            def _(pe):
                def scores(u, nth, par):
                    h, i, n = unit(u)
                    pe.wait_ge(s_max[u % 2], nth * (UNITS // 2) + u // 2)
                    nc.tensor.matmul(s_bank[u % 2][:, 0:n], qs[par][0:SROWS, h, i * P:(i + 1) * P], ks[par][0:SROWS, h, 0:n],
                                     start=True, stop=True).then_inc(s_s[u % 2], 1)

                def turn(half, nth, par, emptied, count):
                    for j in range(2):
                        pe.wait_ge(s_max[j], nth * (UNITS // 2) + (half + 1) * UNITS // 4)
                    if emptied is not None:
                        pe.wait_ge(emptied, count)
                    for i in range(TB):
                        last = nc.tensor.transpose(m_bank[0:H // 2, i * P:(i + 1) * P], rowmax[par][:, i, half * 8:half * 8 + 8], k.ident[:, :])
                    last.then_inc(s_mt, 1)

                def turn_quad(q, nth, emptied, count):
                    pe.wait_ge(s_out, nth * QUADS + q + 1)
                    pe.wait_ge(emptied, count)
                    for i in range(TB):
                        last = nc.tensor.transpose(m_bank[:, i * P:(i + 1) * P], turned[q % 2][:, i * P:(i + 1) * P], k.ident[:, :])
                    last.then_inc(s_ot[q % 2], 1)

                def sum_values(s, pair, nth, par):
                    q, kt = s // TB, s % TB
                    pe.wait_ge(s_exp[pair], nth * STEPS + s + 1)
                    if kt == 0 and pair == 0:
                        pe.wait_ge(s_out, nth * QUADS + q)
                    c0 = kt * P if causal else 0
                    for j in (2 * pair, 2 * pair + 1):
                        last = nc.tensor.matmul(o_bank[j * VW:(j + 1) * VW, c0:N], vs[par][:, kt, (4 * q + j) * VW:(4 * q + j + 1) * VW],
                                                probs[s % 2][:, j, c0:N], start=(kt == 0), stop=(kt == TB - 1))
                    if pair:
                        last.then_inc(s_pv[s % 2], 1)

                def scores_t(s, pair, nth, par):
                    q, kt = s // TB, s % TB
                    c0 = kt * P if causal else 0
                    pe.wait_ge(s_exp[pair], nth * STEPS + s)
                    for j in range(2):
                        h = 4 * q + 2 * pair + j
                        out = t_bank[pair][:, j, c0:N]
                        last = nc.tensor.matmul(out, ks[par][0:MROWS, h, kt * P:(kt + 1) * P], qs[par][0:MROWS, h, c0:N],
                                                start=True, stop=not masked)
                        if mask is not None:
                            last = nc.tensor.matmul(out, neg_ident[:, :], one_k[par][:, kt, :], start=False, stop=True)
                        if causal:
                            last = nc.tensor.matmul(t_bank[pair][:, j, c0:c0 + P], neg_ident[:, :], ahead_k[:, :], start=False, stop=True)
                    last.then_inc(s_t[pair], 1)

                def wait_loaded(half, it, par):
                    pe.wait_ge(s_ld[half][par], it * 16 * LOADS + 16 * LOADS)

                def batch(it, par, nth, first=False, last=False):
                    nit, npar = (it, 1) if par == 0 else (it + 1, 0)
                    for s in range(STEPS):
                        if s == 0:
                            pe.wait_ge(s_v[par], it * 16 + 16)
                            if mask is not None:
                                pe.wait_ge(s_onek[par], it + 1)
                        if s % (STEPS // 2) == 0:
                            pe.wait_ge(s_mrow[s // (STEPS // 2)][par], it * 48 + 48)
                        units = units_of(s, nth, par, last)
                        if not last and s in (next_step, next_step + STEPS // 2):
                            wait_loaded((s - next_step) // (STEPS // 2), nit, npar)
                        for pair in range(2):
                            scores_t(s, pair, nth, par)
                            for v in units[pair:pair + 1]:
                                scores(*v)
                        for pair in range(2):
                            if s:
                                sum_values(s - 1, pair, nth, par)
                            elif not first:
                                sum_values(STEPS - 1, pair, nth - 1, 1 - par)
                            for v in units[2 + pair:3 + pair]:
                                scores(*v)
                        if s == 1 and not first:
                            turn_quad(QUADS - 1, nth - 1, s_norm, (nth * QUADS - 1) * 2)
                        if s % TB == 1 and s > TB:
                            q = s // TB - 1
                            if q == 1:
                                turn_quad(q, nth, s_norm, (nth * QUADS + 1) * 2)
                            elif q == 2 and last:
                                turn_quad(q, nth, s_norm, (nth * QUADS + 2) * 2)
                            else:
                                turn_quad(q, nth, s_nm, nth * 2 + (2 if q == 0 else 3))
                        if s == turn_step:
                            turn(1, nth, par, s_norm if not first else None, nth * QUADS * 2)
                        if s == turn_step + STEPS // 2 and not last:
                            turn(0, nth + 1, npar, s_norm, (nth * QUADS + 2) * 2)

                for u in range(ahead):
                    if u % (UNITS // 2) == 0:
                        wait_loaded(u // (UNITS // 2), 0, 0)
                    if u == 0 and masked:
                        pe.wait_ge(s_const, 6 if causal else 2)
                    scores(u, 0, 0)
                    if u == UNITS // 2:
                        turn(0, 0, 0, None, 0)
                pe.wait_ge(s_rows0, 1)
                pe.wait_ge(s_rows1, 1)
                batch(0, 0, 0, first=True)
                batch(0, 1, 1)
                with pe.Fori(1, B // 2 - 1) as it:
                    for par in ALLX:
                        batch(it, par, it * 2 + par)
                batch(B // 2 - 1, 0, B - 2)
                batch(B // 2 - 1, 1, B - 1, last=True)
                for pair in range(2):
                    sum_values(STEPS - 1, pair, B - 1, 1)
                turn_quad(QUADS - 1, B - 1, s_norm, (B * QUADS - 1) * 2)

            @block.scalar
            def _(act):
                def exps(s, pair, nth):
                    kt = s % TB
                    c0 = kt * P if causal else 0
                    act.wait_ge(s_t[pair], nth * STEPS + s + 1)
                    act.wait_ge(s_pv[s % 2], nth * (STEPS // 2) + s // 2)
                    nc.scalar.activation(probs[s % 2][:, 2 * pair:2 * pair + 2, c0:N], t_bank[pair][:, :, c0:N], ACT.Exp,
                                         scale=scale).then_inc(s_exp[pair], 1)

                def quad_out(q, nth):
                    act.wait_ge(s_pv[1], nth * (STEPS // 2) + 2 * q + 2)
                    act.wait_ge(s_ot[q % 2], nth * 2 + q // 2)
                    nc.scalar.activation(turned[q % 2][:, :], o_bank[:, :], ACT.Copy).then_inc(s_out, 1)

                def split_high(half, done, npar, sent):
                    act.wait_ge(s_mt, done + 1)
                    act.wait_ge(s_nlo, done)
                    act.wait_ge(s_mrow[half][1 - npar], sent * 48)
                    nc.scalar.activation(negmax[:, :], m_bank[0:H // 2, :], ACT.Copy, scale=-1.0).then_inc(s_nm, 1)
                    act.wait_ge(s_nm, done + 1)
                    nc.scalar.activation(negpart[half][:, 0, :], negmax[:, :], ACT.Copy).then_inc(s_nh, 1)

                def split_middle(half, done):
                    act.wait_ge(s_nr, done + 1)
                    nc.scalar.activation(negpart[half][:, 1, :], negrest[:, :], ACT.Copy).then_inc(s_nmid, 1)

                def send_max(half, done, npar):
                    act.wait_ge(s_nlo, done + 1)
                    for c in range(3):
                        act.dma_start(qs[npar][SROWS + c:SROWS + c + 1, half * 8:half * 8 + 8, :], negpart[half][:, c:c + 1, :]
                                      ).then_inc(s_mrow[half][npar], 16)

                def batch(it, par, nth, first=False, last=False):
                    for s in range(STEPS):
                        exps(s, 0, nth)
                        exps(s, 1, nth)
                        if s == 0 and not first:
                            quad_out(QUADS - 1, nth - 1)
                        if s % TB == 0 and s:
                            quad_out(s // TB - 1, nth)
                        if s == turn_step:
                            split_high(1, nth * 2 + 1, par, it if par == 0 else it + 1)
                        if s == turn_step + 1:
                            split_middle(1, nth * 2 + 1)
                        if s == turn_step + 2:
                            send_max(1, nth * 2 + 1, par)
                        if s == turn_step + STEPS // 2 and not last:
                            split_high(0, nth * 2 + 2, 1 - par, it + 1)
                        if s == turn_step + STEPS // 2 + 1 and not last:
                            split_middle(0, nth * 2 + 2)
                        if s == turn_step + STEPS // 2 + 2 and not last:
                            send_max(0, nth * 2 + 2, 1 - par)

                for half in range(2):
                    stack_loads(act, 0, 0, half, K_REPS, 1, ks)
                split_high(0, 0, 0, 0)
                split_middle(0, 0)
                send_max(0, 0, 0)
                batch(0, 0, 0, first=True)
                batch(0, 1, 1)
                with act.Fori(1, B // 2 - 1) as it:
                    for par in ALLX:
                        batch(it, par, it * 2 + par)
                batch(B // 2 - 1, 0, B - 2)
                batch(B // 2 - 1, 1, B - 1, last=True)
                quad_out(QUADS - 1, B - 1)
                for half in range(2):
                    for par in ALLX:
                        act.wait_ge(s_mrow[half][par], B // 2 * 48)

            @block.vector
            def _(dve):
                def maxima(u, nth, par):
                    h, i, n = unit(u)
                    wait_apart(ph, dve, s_s[u % 2], nth * (UNITS // 2) + u // 2 + 1)
                    out = rowmax[par][:, i, h:h + 1]
                    if masked:
                        add = ahead_q[:, N - n:N] if causal else add_q[par][:, i, :]
                        nc.vector.tensor_tensor_reduce(out=scratch[u % 2][:, 0:n], in0=s_bank[u % 2][:, 0:n], in1=add, scale=1.0,
                                                       scalar=-3.0e38, op0=ALU.add, op1=ALU.max, accum_out=out).then_inc(s_max[u % 2], 1)
                    else:
                        nc.vector.reduce_max(out, s_bank[u % 2][:, 0:n], AX.X).then_inc(s_max[u % 2], 1)

                def invert(q, it, nth, par):
                    dve.wait_ge(s_ot[q % 2], nth * 2 + q // 2 + 1)
                    if q == 0:
                        dve.wait_ge(s_store[par], it * 16)
                    dve.wait_ge(s_norm, (nth * QUADS + q) * 2)
                    sums = m_bank[:, :].rearrange("p (g w) -> p g w", w=VW)
                    nc.vector.reciprocal(recip[:, :].rearrange("p (g a) -> p g a", a=1), sums[:, :, HD:HD + 1]).then_inc(s_rc, 1)

                def normalise(q, part, nth, par):
                    dve.wait_ge(s_rc, nth * QUADS + q + 1)
                    tiles = slice(part * TB // 2, (part + 1) * TB // 2)
                    nc.vector.tensor_tensor(attn[par][:, tiles, q * 4 * HD:(q + 1) * 4 * HD].rearrange("p i (j e) -> p i j e", e=HD),
                                            m_bank[:, :].rearrange("p (i j w) -> p i j w", i=TB, w=VW)[:, tiles, :, 0:HD],
                                            recip[:, :].rearrange("p (i j a) -> p i j a", i=TB, a=1)[:, tiles].broadcast_to((P, TB // 2, 4, HD)),
                                            ALU.mult).then_inc(s_norm, 1)

                def quad_part(n, s, it, nth, par, first):
                    if s % TB not in (2, 3):
                        return
                    if s < TB:
                        if first:
                            return
                        q, it, nth, par = QUADS - 1, (it if par else it - 1), nth - 1, 1 - par
                    else:
                        q = s // TB - 1
                    if s % TB == 2 and n == 1:
                        invert(q, it, nth, par)
                    if s % TB == 2 and n == 3:
                        normalise(q, 0, nth, par)
                    if s % TB == 3 and n == 1:
                        normalise(q, 1, nth, par)

                def batch(it, par, nth, first=False, last=False):
                    nit, npar = (it, 1) if par == 0 else (it + 1, 0)
                    for s in range(STEPS):
                        if mask is not None and s == next_step and not last:
                            dve.wait_ge(s_addq[npar], nit + 1)
                        units = units_of(s, nth, par, last)
                        for n, v in enumerate(units or [None] * 4):
                            if v is not None:
                                maxima(*v)
                            quad_part(n, s, it, nth, par, first)

                nc.vector.memset(ks[0][SROWS:MROWS, :, :], 1.0).then_inc(s_rows0, 1)
                if masked:
                    dve.wait_ge(s_const, 6 if causal else 2)
                if mask is not None:
                    dve.wait_ge(s_addq[0], 1)
                for u in range(ahead):
                    maxima(u, 0, 0)
                batch(0, 0, 0, first=True)
                batch(0, 1, 1)
                with dve.Fori(1, B // 2 - 1) as it:
                    for par in ALLX:
                        batch(it, par, it * 2 + par)
                batch(B // 2 - 1, 0, B - 2)
                batch(B // 2 - 1, 1, B - 1, last=True)
                invert(QUADS - 1, B // 2 - 1, B - 1, 1)
                for part in range(2):
                    normalise(QUADS - 1, part, B - 1, 1)


class Output:

    def __init__(self, ph, w_out, b_out, turned, sums):
        self.ph, self.nc, self.k, self.w_out, self.b_out = ph, ph.nc, ph.k, w_out, b_out
        self.t_bank, self.y_bank, self.shared = turned, sums, len(turned) == KC
        self.wo, self.bias = ph.sb("wo", [P, KC, D]), ph.sb("bias_out", [P, D])
        self.at, self.atT = ph.two("at", [P, TB, D]), ph.two("atT", [P, KC, N])
        self.s_w, self.s_at, self.s_turn, self.s_atT = ph.sem("out_weights"), ph.pair("attn_loaded"), ph.pair("attn_turned"), ph.pair("attnT")
        self.s_y, self.s_x, self.s_b = ph.pair("out_product"), ph.pair("x_summed"), ph.pair("bias_added")
        self.w_all = 16 * (1 if b_out is None else 2)

    def freed(self, pair, it, par, each):
        return before(pair, it, par, each) if self.shared else (pair[par], it * each)

    def load_weights(self, eng):
        eng.dma_start(self.wo[:, :, :], rows(self.w_out)).then_inc(self.s_w, 16)
        if self.b_out is not None:
            eng.dma_start(self.bias[:, :], over_partitions(self.b_out)).then_inc(self.s_w, 16)

    def load(self, eng, b, it, par):
        eng.wait_ge(self.s_turn[par], it * KC)
        eng.dma_start(self.at[par][:, :, :], self.k.attn[ds(b, 1)].rearrange("b (i p) d -> p (b i) d", p=P)).then_inc(self.s_at[par], 16)

    def add_bias(self, pool, b, par):
        for i in range(TB):
            xi = self.k.x[:, ds(b * TB + i, 1), :]
            self.nc.gpsimd.tensor_tensor(xi, xi, self.bias[:, :].rearrange("p (a d) -> p a d", a=1), ALU.add).then_inc(self.s_b[par], 1)

    def turn(self, pe, it, par):
        pe.wait_ge(self.s_at[par], it * 16 + 16)
        pe.wait_ge(*self.freed(self.s_atT, it, par, KC))
        for c in range(KC):
            bank = self.t_bank[c if self.shared else KC * par + c]
            for i in range(TB):
                last = self.nc.tensor.transpose(bank[:, i * P:(i + 1) * P], self.at[par][:, i, c * P:(c + 1) * P], self.k.ident[:, :])
            last.then_inc(self.s_turn[par], 1)

    def sum_bank(self, par, i):
        return self.y_bank[i // 2 if self.shared else KC * par + i // 2][:, (i % 2) * D:(i % 2 + 1) * D]

    def products(self, pe, it, par):
        pe.wait_ge(self.s_atT[par], it * KC + KC)
        pe.wait_ge(*self.freed(self.s_x, it, par, TB))
        for i in range(TB):
            for c in range(KC):
                last = self.nc.tensor.matmul(self.sum_bank(par, i), self.atT[par][:, c, i * P:(i + 1) * P], self.wo[:, c, :],
                                             start=(c == 0), stop=(c == KC - 1))
            last.then_inc(self.s_y[par], 1)

    def copies(self, act, it, par):
        act.wait_ge(self.s_y[par], it * TB)
        for c in range(KC):
            act.wait_ge(self.s_turn[par], it * KC + c + 1)
            bank = self.t_bank[c if self.shared else KC * par + c]
            self.nc.scalar.activation(self.atT[par][:, c, :], bank[:, :], ACT.Copy).then_inc(self.s_atT[par], 1)

    def sums(self, dve, b, it, par):
        for i in range(TB):
            dve.wait_ge(self.s_y[par], it * TB + (i // 2 * 2 + 2))
            if self.b_out is not None:
                dve.wait_ge(self.s_b[par], it * TB + i + 1)
            xi = self.k.x[:, ds(b * TB + i, 1), :]
            self.nc.vector.tensor_tensor(xi, xi, self.sum_bank(par, i).rearrange("p (a d) -> p a d", a=1), ALU.add).then_inc(self.s_x[par], 1)


def phase_output(k, tag, w_out, b_out=None):
    nc = k.nc
    group = k.slots_in.shape[0] // P // B
    with Phase(k, tag) as ph:
        ps = ph.banks()
        out = Output(ph, w_out, b_out, ps[0:4], ps[4:8])
        zero, s_zero, s_st = ph.sb("zero", [P, D]), ph.sem("zero_made"), ph.sem("slots_zeroed")
        with nc.Block() as block:
            @block.sync
            def _(sp):
                out.load_weights(sp)
                for it, par, b in batches(sp):
                    out.load(sp, b, it, par)

            @block.gpsimd
            def _(pool):
                ph.clear_others(pool)
                nc.gpsimd.memset(zero[:, :], 0.0).then_inc(s_zero, 1)
                if b_out is not None:
                    pool.wait_ge(out.s_w, out.w_all)
                    for it, par, b in batches(pool):
                        out.add_bias(pool, b, par)

            @block.tensor
            def _(pe):
                out.turn(pe, 0, 0)
                pe.wait_ge(out.s_w, out.w_all)
                for it, par, b, first, left in pipelined(pe):
                    if left:
                        out.turn(pe, *after(it, par))
                    out.products(pe, it, par)

            @block.scalar
            def _(act):
                act.wait_ge(s_zero, 1)
                for it, par, b in batches(act):
                    out.copies(act, it, par)
                    act.dma_start(k.slots_in.rearrange("(j p) d -> p j d", p=P)[:, ds(b * group, group), :],
                                  zero[:, :].rearrange("p (a d) -> p a d", a=1).broadcast_to((P, group, D))).then_inc(s_st, 16)
                act.wait_ge(s_st, B * 16)

            @block.vector
            def _(dve):
                for it, par, b in batches(dve):
                    out.sums(dve, b, it, par)


def phase_store(k, out):
    with Phase(k, "store") as ph:
        done = ph.sem("stored")
        with k.nc.Block() as block:
            @block.sync
            def _(sp):
                sp.dma_start(out.rearrange("b (i p) d -> p (b i) d", p=P), k.x[:, :, :]).then_inc(done, 16)
                sp.wait_ge(done, 16)

            @block.gpsimd
            def _(pool):
                ph.clear_others(pool)
RING = 2 * TB
SLOTS = NT + E - 1
ROUND = 1.5 * 2.0 ** 23


def load_expert(k, eng, e, w1, w2):
    for wide, src in ((k.w1, w1), (k.w2, w2)):
        eng.dma_start(wide[:, ds(e, 1), :, :].rearrange("p e c n -> p (e c) n"), src[ds(e, 1)].rearrange("e (c p) n -> p (e c) n", p=P)
                      ).then_inc(k.experts_loaded, 16)


def phase_route(k, w_out, b_out, wr, br, w1, w2):
    nc = k.nc
    with Phase(k, "route") as ph:
        ps = ph.banks()
        attn_out = Output(ph, w_out, b_out, ps[2:4], ps[4:6])
        norm = Norm(ph, "ln", EPS_X)
        xn = ph.two("xn", [P, TB, D])
        ring = [attn_out.at[r // TB][:, r % TB, :] for r in range(RING)]
        xnT = ph.two("xnT", [P, KC, N])
        wr_s, br_s = ph.sb("wr", [P, KC, E]), ph.sb("br", [P, E])
        logits = ph.sb("logits", [P, NT, E])
        top = ph.sb("top", [P, NT, E])
        index = ph.sb("index", [P, NT, E], U32)
        diff = ph.sb("diff", [P, NT])
        best = ph.sb("best", [P, NT])
        chosen, chosen16 = ph.sb("chosen", [P, NT, E]), ph.sb("chosen16", [P, NT, E], BF16)
        earlier, ones16 = ph.sb("earlier", [P, P], BF16), ph.sb("ones16", [P, P], BF16)
        ones_t = ph.sb("ones_t", [P, NT])
        nth_e = ph.sb("nth_e", [P, E])
        nth_slot = ph.sb("nth_slot", [P, SLOTS])
        count, upto = ph.sb("count", [P, NT, E]), ph.sb("upto", [P, NT, E])
        tiles_i, tiles_f = ph.sb("tiles_i", [P, E], I32), ph.sb("tiles_f", [P, E])
        ends, first = ph.sb("ends", [P, E]), ph.sb("first", [P, E])
        passed = ph.sb("passed", [P, SLOTS, E])
        owner = ph.sb("owner", [P, SLOTS])
        place = ph.sb("place", [P, NT])
        s_w = ph.sem("weights")
        s_c = ph.sem("constants")
        s_xn, s_t, s_xT = ph.pair("xn"), ph.pair("x_turned"), ph.pair("xnT")
        s_l, s_lb = ph.pair("logits"), ph.pair("logits_out")
        s_dve, s_pe, s_act, s_top = ph.sem("routing_steps"), ph.sem("rank_products"), ph.sem("odds"), ph.sem("top")
        s_kept, s_back, s_sc = ph.pair("xn_stored"), [ph.sem(f"xn_back{r}") for r in range(RING)], [ph.own_sem(f"scattered{r}") for r in range(RING)]
        with nc.Block() as block:
            @block.sync
            def _(sp):
                attn_out.load(sp, 0, 0, 0)
                attn_out.load_weights(sp)
                attn_out.load(sp, 1, 0, 1)
                sp.dma_start(wr_s[:, :, :], rows(wr)).then_inc(s_w, 16)
                sp.dma_start(br_s[:, :], over_partitions(br)).then_inc(s_w, 16)
                for it, par, b, first, left in pipelined(sp):
                    if left == 2:
                        attn_out.load(sp, b + 2, it + 1, par)
                    sp.wait_ge(s_xn[par], it * TB + TB)
                    sp.dma_start(k.xn_rows[ds(b, 1)].rearrange("b (i p) d -> p (b i) d", p=P), xn[par][:, :, :]).then_inc(s_kept[par], 16)
                    if par == 0:
                        load_expert(k, sp, it, w1, w2)
                for par in ALLX:
                    sp.wait_ge(s_kept[par], B // 2 * 16)
                    sp.wait_ge(attn_out.s_turn[par], B // 2 * KC)
                for t in range(NT):
                    if t >= RING:
                        sp.wait_ge(s_sc[t % RING], 16 * (t // RING))
                    sp.dma_start(ring[t % RING], k.xn_rows[t // TB, (t % TB) * P:(t % TB + 1) * P, :]).then_inc(s_back[t % RING], 16)

            @block.gpsimd
            def _(pool):
                ph.clear_others(pool)
                nc.gpsimd.memset(earlier[:, :], 1.0).then_inc(s_c, 1)
                nc.gpsimd.memset(ones16[:, :], 1.0).then_inc(s_c, 1)
                nc.gpsimd.memset(ones_t[:, :], 1.0).then_inc(s_c, 1)
                nc.gpsimd.iota(nth_e[:, :], [[1, E]], base=0, channel_multiplier=0, allow_small_or_imprecise_dtypes=True).then_inc(s_c, 1)
                nc.gpsimd.iota(nth_slot[:, :], [[1, SLOTS]], base=0, channel_multiplier=0, allow_small_or_imprecise_dtypes=True).then_inc(s_c, 1)
                pool.wait_ge(s_c, 5)
                nc.gpsimd.affine_select(out=earlier[:, :], in_=earlier[:, :], compare_op=ALU.is_gt, fill=0.0,
                                        base=0, pattern=[[1, P]], channel_multiplier=-1).then_inc(s_c, 1)
                pool.wait_ge(attn_out.s_w, attn_out.w_all)
                for par in ALLX:
                    attn_out.add_bias(pool, par, par)
                norm.power(pool, 0, 0)
                for it, par, b, first, left in pipelined(pool):
                    if left == 2:
                        attn_out.add_bias(pool, b + 2, par)
                    if left:
                        nit, npar = after(it, par)
                        norm.power(pool, npar, nit)
                pool.wait_ge(s_dve, ROUTED)
                for t in range(NT):
                    pool.wait_ge(s_back[t % RING], 16 * (t // RING + 1))
                    nc.gpsimd.indirect_dma_start(out=k.slots_in, out_offset=bass.IndirectOffsetOnAxis(ap=k.place[:, t:t + 1], axis=0),
                                                 in_=ring[t % RING], in_offset=None).then_inc(s_sc[t % RING], 16)
                for r in range(RING):
                    pool.wait_ge(s_sc[r], NT // RING * 16)

            @block.tensor
            def _(pe):
                attn_out.turn(pe, 0, 0)
                pe.wait_ge(attn_out.s_w, attn_out.w_all)
                attn_out.products(pe, 0, 0)
                attn_out.turn(pe, 0, 1)
                pe.wait_ge(s_w, 32)
                for it, par, b, first, left in pipelined(pe):
                    if left:
                        attn_out.products(pe, *after(it, par))
                    pe.wait_ge(s_xn[par], it * TB + TB)
                    pe.wait_ge(*before(s_xT, it, par, KC))
                    for c in range(KC):
                        for i in range(TB):
                            last = nc.tensor.transpose(ps[c][:, i * P:(i + 1) * P], xn[par][:, i, c * P:(c + 1) * P], k.ident[:, :])
                    last.then_inc(s_t[par], 1)
                    if left == 2:
                        attn_out.turn(pe, it + 1, par)
                    pe.wait_ge(s_xT[par], it * KC + KC)
                    pe.wait_ge(s_lb[par], it)
                    for i in range(TB):
                        for c in range(KC):
                            last = nc.tensor.matmul(ps[6 + par][:, i * E:(i + 1) * E], xnT[par][:, c, i * P:(i + 1) * P], wr_s[:, c, :],
                                                    start=(c == 0), stop=(c == KC - 1))
                    last.then_inc(s_l[par], 1)
                pe.wait_ge(s_c, 6)
                pe.wait_ge(s_dve, CHOSEN)
                nc.tensor.matmul(ps[0][:, 0:NT * E], earlier[:, :], chosen16[:, :, :].rearrange("p t e -> p (t e)"), start=True, stop=True).then_inc(s_pe, 1)
                nc.tensor.matmul(ps[1][:, 0:NT * E], ones16[:, :], chosen16[:, :, :].rearrange("p t e -> p (t e)"), start=True, stop=True).then_inc(s_pe, 1)

            @block.scalar
            def _(act):
                for par in ALLX:
                    attn_out.copies(act, 0, par)
                for it, par, b, first, left in pipelined(act):
                    act.wait_ge(s_t[par], it + 1)
                    act.wait_ge(s_l[par], it)
                    for c in range(KC):
                        nc.scalar.activation(xnT[par][:, c, :], ps[c][:, :], ACT.Copy).then_inc(s_xT[par], 1)
                    if left == 2:
                        attn_out.copies(act, it + 1, par)
                for e in range(B // 2, E):
                    load_expert(k, act, e, w1, w2)
                act.wait_ge(s_dve, DIFFERED)
                nc.scalar.activation(diff[:, :], diff[:, :], ACT.Exp).then_inc(s_act, 1)

            @block.vector
            def _(dve):
                dve.wait_ge(s_c, 6)
                steps = [0]

                def step(ins):
                    steps[0] += 1
                    ins.then_inc(s_dve, 1)
                    dve.wait_ge(s_dve, steps[0])

                def normalise(b, it, par):
                    src = lambda i: k.x[:, ds(b * TB + i, 1), :].rearrange("p a d -> p (a d)")
                    attn_out.sums(dve, b, it, par)
                    wait_apart(ph, dve, attn_out.s_x[par], it * TB + TB)
                    norm.statistics(dve, par, it, src)
                    dve.wait_ge(s_t[par], it)
                    dve.wait_ge(s_kept[par], it * 16)
                    norm.apply(dve, par, it, src, lambda i: xn[par][:, i, :], s_xn[par])

                normalise(0, 0, 0)
                dve.wait_ge(s_w, 32)
                for it, par, b, _, left in pipelined(dve):
                    if left:
                        normalise(b + 1, *after(it, par))
                    dve.wait_ge(s_l[par], it + 1)
                    nc.vector.tensor_tensor(logits[:, ds(b * TB, TB), :], ps[6 + par][:, 0:TB * E].rearrange("p (i e) -> p i e", e=E),
                                            br_s[:, :].rearrange("p (a e) -> p a e", a=1).broadcast_to((P, TB, E)), ALU.add).then_inc(s_lb[par], 1)
                for par in ALLX:
                    dve.wait_ge(s_lb[par], B // 2)
                for t in range(NT):
                    nc.vector.max(top[:, t, :], logits[:, t, :]).then_inc(s_top, 1)
                dve.wait_ge(s_top, NT)
                for t in range(NT):
                    nc.vector.max_index(index[:, t, :], top[:, t, :], logits[:, t, :]).then_inc(s_top, 1)
                dve.wait_ge(s_top, 2 * NT)
                wide = lambda a, n: a.rearrange("p (t a) -> p t a", a=1).broadcast_to((P, a.shape[1], n))
                over_t = lambda a, n: a.rearrange("p (a e) -> p a e", a=1).broadcast_to((P, n, E))
                step(nc.vector.tensor_tensor(diff[:, :], top[:, :, 1], top[:, :, 0], ALU.subtract))
                assert steps[0] == DIFFERED
                step(nc.vector.tensor_copy(best[:, :], index[:, :, 0]))
                step(nc.vector.tensor_tensor(chosen[:, :, :], wide(best[:, :], E), over_t(nth_e[:, :], NT), ALU.is_equal))
                step(nc.vector.tensor_copy(chosen16[:, :, :], chosen[:, :, :]))
                assert steps[0] == CHOSEN
                dve.wait_ge(s_act, 1)
                step(nc.vector.tensor_scalar_add(diff[:, :], diff[:, :], 1.0))
                step(nc.vector.reciprocal(k.gate[:, :], diff[:, :]))
                dve.wait_ge(s_pe, 2)
                step(nc.vector.tensor_copy(count[:, :, :], ps[1][:, 0:NT * E].rearrange("p (t e) -> p t e", e=E)))
                for e in range(E):
                    step(nc.vector.tensor_tensor_scan(upto[:, :, e], ones_t[:, :], count[:, :, e], 0.0, ALU.mult, ALU.add))
                step(nc.vector.tensor_scalar_add(tiles_i[:, :], upto[:, NT - 1, :], float(P - 1)))
                step(nc.vector.tensor_scalar(tiles_i[:, :], tiles_i[:, :], 7, None, ALU.arith_shift_right))
                step(nc.vector.tensor_copy(tiles_f[:, :], tiles_i[:, :]))
                step(nc.vector.tensor_tensor_scan(ends[:, :], ones_t[:, 0:E], tiles_f[:, :], 0.0, ALU.mult, ALU.add))
                step(nc.vector.tensor_tensor(first[:, :], ends[:, :], tiles_f[:, :], ALU.subtract))
                step(nc.vector.tensor_scalar(first[:, :], first[:, :], float(P), None, ALU.mult))
                step(nc.vector.tensor_tensor(upto[:, :, :], upto[:, :, :], count[:, :, :], ALU.subtract))
                step(nc.vector.tensor_tensor(upto[:, :, :], upto[:, :, :], ps[0][:, 0:NT * E].rearrange("p (t e) -> p t e", e=E), ALU.add))
                step(nc.vector.tensor_tensor(upto[:, :, :], upto[:, :, :], over_t(first[:, :], NT), ALU.add))
                step(nc.vector.tensor_tensor(upto[:, :, :], upto[:, :, :], chosen[:, :, :], ALU.mult))
                step(nc.vector.tensor_reduce(place[:, :], upto[:, :, :], AX.X, ALU.add))
                step(nc.vector.tensor_copy(k.place[:, :], place[:, :]))
                step(nc.vector.tensor_tensor(passed[:, :, :], wide(nth_slot[:, :], E), over_t(ends[:, :], SLOTS), ALU.is_ge))
                step(nc.vector.tensor_reduce(owner[:, :], passed[:, :, :], AX.X, ALU.add))
                step(nc.vector.tensor_scalar(k.owner[:, :], owner[:, :], float(E - 1), None, ALU.min))
                assert steps[0] == ROUTED


DIFFERED, CHOSEN = 1, 4
ROUTED = 4 + 2 + 1 + E + 6 + 6 + 3


def phase_experts(k, b1T, b2):
    nc = k.nc
    with Phase(k, "moe") as ph:
        ps = ph.banks()
        xt, xT = ph.two("xt", [P, D]), ph.two("xT", [P, KC, P])
        hid = ph.sb("hid", [P, F])
        hidT = ph.sb("hidT", [P, FC, P])
        y = ph.two("y", [P, D])
        b1s, b2s = ph.sb("b1", [P, E * FC]), ph.sb("b2", [P, E, D])
        s_b, s_x, s_t, s_xT = ph.sem("biases"), ph.pair("x_loaded"), ph.sem("x_turned"), ph.sem("xT")
        s_h, s_ho, s_ht, s_g = ph.sem("hidden"), ph.sem("hidden_out"), ph.sem("hidden_turned"), ph.sem("gelu")
        s_y, s_yo, s_st = ph.sem("product"), ph.sem("y_out"), ph.pair("y_stored")

        def tiles(eng, body):
            body(0, 0, 0, True, False)
            body(1, 0, 1, False, False)
            body(2, 1, 0, False, False)
            with eng.Fori(1, (SLOTS - 1) // 2 - 1) as it:
                body(it * 2 + 1, it, 1, False, False)
                body(it * 2 + 2, it + 1, 0, False, False)
            body(SLOTS - 2, (SLOTS - 1) // 2 - 1, 1, False, False)
            body(SLOTS - 1, (SLOTS - 1) // 2, 0, False, True)

        with nc.Block() as block:
            @block.sync
            def _(sp):
                sp.dma_start(b1s[:, :], b1T).then_inc(s_b, 16)
                sp.dma_start(b2s[:, :, :], b2.rearrange("(a e) d -> a e d", a=1).broadcast_to((P, E, D))).then_inc(s_b, 16)

                def store(j, par):
                    wait_apart(ph, sp, s_yo, j + 1)
                    sp.dma_start(k.slots_out.rearrange("(j p) d -> j p d", p=P)[ds(j, 1)].rearrange("j p d -> p (j d)"), y[par][:, :]).then_inc(s_st[par], 16)

                def body(j, par, first):
                    if not first:
                        wait_apart(ph, sp, s_t, j - 1)
                    sp.dma_start(xt[par][:, :], k.slots_in.rearrange("(j p) d -> j p d", p=P)[ds(j, 1)].rearrange("j p d -> p (j d)")).then_inc(s_x[par], 16)
                    if not first:
                        store(j - 2, par)
                body(0, 0, True)
                body(1, 1, True)
                with sp.Fori(1, (SLOTS - 1) // 2) as it:
                    body(it * 2, 0, False)
                    body(it * 2 + 1, 1, False)
                body(SLOTS - 1, 0, False)
                store(SLOTS - 2, 1)
                store(SLOTS - 1, 0)
                sp.wait_ge(s_st[0], (SLOTS + 1) // 2 * 16)
                sp.wait_ge(s_st[1], SLOTS // 2 * 16)

            @block.gpsimd
            def _(pool):
                ph.clear_others(pool)

            @block.tensor
            def _(pe):
                def turn_x(j, before_par, par):
                    pe.wait_ge(s_x[par], before_par * 16 + 16)
                    pe.wait_ge(s_xT, j)
                    for c in range(KC):
                        last = nc.tensor.transpose(ps[0][:, c * P:(c + 1) * P], xt[par][:, c * P:(c + 1) * P], k.ident[:, :])
                    last.then_inc(s_t, 1)

                def expert(j):
                    return pe.value_load(k.owner[0:1, ds(j, 1)], min_val=0, max_val=E - 1)

                def up(j, par, e):
                    pe.wait_ge(s_xT, j + 1)
                    pe.wait_ge(s_ho, j * 2)
                    for half in range(2):
                        for c in range(KC):
                            last = nc.tensor.matmul(ps[1 + half][:, :], xT[par][:, c, :], k.w1[:, ds(e, 1), c, half * 512:half * 512 + 512],
                                                    start=(c == 0), stop=(c == KC - 1))
                        last.then_inc(s_h, 1)

                def down(j, par, left, e):
                    pe.wait_ge(s_yo, left)
                    for c in range(FC):
                        pe.wait_ge(s_g, j * FC + c + 1)
                        last = nc.tensor.matmul(ps[5 + par][:, 0:D], hidT[:, c, :], k.w2[:, ds(e, 1), c, :],
                                                start=(c == 0), stop=(c == FC - 1))
                    last.then_inc(s_y, 1)

                def turn_h(j):
                    pe.wait_ge(s_g, j * FC)
                    for half in range(2):
                        pe.wait_ge(s_ho, j * 2 + half + 1)
                        for c in range(4):
                            last = nc.tensor.transpose(ps[3 + half][:, c * P:(c + 1) * P], hid[:, (4 * half + c) * P:(4 * half + c + 1) * P], k.ident[:, :])
                        last.then_inc(s_ht, 1)

                def body(j, before_par, par, first, last):
                    e_before = None if first else expert(j - 1)
                    up(j, par, expert(j))
                    if not last:
                        turn_x(j + 1, before_par + par, 1 - par)
                    if not first:
                        down(j - 1, 1 - par, max(j - 2, 0) if isinstance(j, int) else j - 2, e_before)
                    turn_h(j)
                turn_x(0, 0, 0)
                pe.wait_ge(k.experts_loaded, 32 * E)
                tiles(pe, body)
                down(SLOTS - 1, (SLOTS - 1) % 2, SLOTS - 2, expert(SLOTS - 1))

            @block.scalar
            def _(act):
                act.wait_ge(s_b, 32)

                def copy_x(j, par):
                    act.wait_ge(s_t, j + 1)
                    nc.scalar.activation(xT[par][:, :, :], ps[0][:, 0:D].rearrange("p (c t) -> p c t", c=KC), ACT.Copy).then_inc(s_xT, 1)

                def body(j, before_par, par, first, last):
                    e = act.value_load(k.owner[0:1, ds(j, 1)], min_val=0, max_val=E - 1)
                    if not last:
                        if not first:
                            act.wait_ge(s_h, j * 2)
                        copy_x(j + 1, 1 - par)
                    act.wait_ge(s_y, j)
                    for c in range(FC):
                        if c % 4 == 0:
                            act.wait_ge(s_ht, j * 2 + c // 4 + 1)
                        nc.scalar.activation(hidT[:, c, :], ps[3 + c // 4][:, (c % 4) * P:(c % 4 + 1) * P], ACT.Gelu,
                                             bias=b1s[:, ds(e * FC + c, 1)]).then_inc(s_g, 1)
                copy_x(0, 0)
                tiles(act, body)

            @block.vector
            def _(dve):
                dve.wait_ge(s_b, 32)

                def out(j, before_par, par):
                    e = dve.value_load(k.owner[0:1, ds(j, 1)], min_val=0, max_val=E - 1)
                    dve.wait_ge(s_y, j + 1)
                    dve.wait_ge(s_st[par], before_par * 16)
                    nc.vector.tensor_tensor(y[par][:, :].rearrange("p (a d) -> p a d", a=1), ps[5 + par][:, 0:D].rearrange("p (a d) -> p a d", a=1),
                                            b2s[:, ds(e, 1), :], ALU.add).then_inc(s_yo, 1)

                def body(j, before_par, par, first, last):
                    dve.wait_ge(s_ht, j * 2)
                    for half in range(2):
                        dve.wait_ge(s_h, j * 2 + half + 1)
                        nc.vector.tensor_copy(hid[:, half * 512:half * 512 + 512], ps[1 + half][:, :]).then_inc(s_ho, 1)
                    if not first:
                        out(j - 1, before_par if par else before_par - 1, 1 - par)
                tiles(dve, body)
                out(SLOTS - 1, (SLOTS - 1) // 2, (SLOTS - 1) % 2)


def moe(k, attn_out, wr, br, w1, b1T, w2, b2):
    nc = k.nc
    keep = lambda name, shape, dt: k.ctx.enter_context(nc.sbuf_tensor(name, shape, dt))
    k.gate, k.place, k.owner = keep("gate", [P, NT], F32), keep("place", [P, NT], U32), keep("owner", [P, SLOTS], I32)
    with ExitStack() as ctx:
        sb = lambda name, shape, dt=F32: ctx.enter_context(nc.sbuf_tensor(name, shape, dt))
        k.w1, k.w2 = sb("expert_w1", [P, E, KC, F]), sb("expert_w2", [P, E, FC, D])
        k.experts_loaded = ctx.enter_context(nc.semaphore("experts_loaded", num=k.next_own_sem()))
        phase_route(k, *attn_out, wr, br, w1, w2)
        phase_experts(k, b1T, b2)
def phase_retention(k, w):
    nc = k.nc
    with Phase(k, "ret") as ph:
        ps = ph.banks()
        w_ret, w1, w2 = ph.sb("w_ret", [P, KC, D]), ph.sb("w1", [P, KC, F]), ph.sb("w2", [P, FC, D])
        b_ret, b1 = ph.sb("b_ret", [P, KC]), ph.sb("b1", [P, FC])
        ln1s, ln1b, ln2s, ln2b, b2 = (ph.sb(x, [P, D]) for x in ("ln1s", "ln1b", "ln2s", "ln2b", "b2"))
        half_t = ph.sb("half", [P, N])
        normx, norm1, norm2 = Norm(ph, "lnx", EPS_X), Norm(ph, "ln1", EPS_X), Norm(ph, "ln2", EPS_X)
        xn = ph.sb("xn", [P, TB, D])
        xnT, sig, yT = ph.sb("xnT", [P, KC, N]), ph.sb("sig", [P, KC, N]), ph.sb("yT", [P, KC, N])
        z = ph.sb("z", [P, TB, D])
        h, hT = ph.two("h", [P, TB, D]), ph.sb("hT", [P, KC, N])
        hb = ph.two("hb", [P, TB, D])
        g = ph.sb("g", [P, FC, N])
        o, on = ph.sb("o", [P, TB, D]), ph.sb("on", [P, TB, D])
        rows_in = ph.sb("rows_in", [P, NT, D])
        s_got, s_add = [ph.own_sem(f"fetched{par}") for par in ALLX], ph.sem("experts_added")
        s_wr, s_wn, s_wf, s_half = ph.sem("retention_weights"), ph.sem("norm_weights"), ph.sem("net_weights"), ph.sem("half")
        s_xn, s_t, s_xT, s_r, s_sg, s_z, s_y = (ph.sem(x) for x in ("xn", "x_turned", "xnT", "ret_product", "sigmoid", "scanned", "yT"))
        s_yt, s_ln1, s_hm, s_h, s_hb, s_ht, s_hT = (ph.sem(x) for x in ("y_turned", "ln1", "h_scaled", "h", "h_b2", "h_turned", "hT"))
        s_u, s_g, s_v, s_o, s_on, s_om, s_ob, s_x = (ph.sem(x) for x in ("hidden", "gelu", "product", "sum", "ln2", "out_scaled", "out", "x_updated"))
        with nc.Block() as block:
            @block.sync
            def _(sp):
                sp.dma_start(w_ret[:, :, :], rows(w["ret"])).then_inc(s_wr, 16)
                sp.dma_start(b_ret[:, :], w["b_ret"]).then_inc(s_wr, 16)
                for dst, name in ((ln1s, "ln1s"), (ln1b, "ln1b"), (ln2s, "ln2s"), (ln2b, "ln2b"), (b2, "b2")):
                    sp.dma_start(dst[:, :], over_partitions(w[name])).then_inc(s_wn, 16)
                sp.dma_start(w1[:, :, :], rows(w["w1"])).then_inc(s_wf, 16)
                sp.dma_start(b1[:, :], w["b1"]).then_inc(s_wf, 16)
                sp.dma_start(w2[:, :, :], rows(w["w2"])).then_inc(s_wf, 16)

            @block.gpsimd
            def _(pool):
                ph.clear_others(pool)
                nc.gpsimd.memset(half_t[:, :], 0.5).then_inc(s_half, 1)
                rep = lambda a: a[:, :].rearrange("p (a d) -> p a d", a=1).broadcast_to((P, TB, D))

                def finish(b, it, par):
                    norm2.power(pool, par, it)
                    pool.wait_ge(s_on, b * TB + TB)
                    nc.gpsimd.tensor_tensor(on[:, :, :], on[:, :, :], rep(ln2s), ALU.mult).then_inc(s_om, 1)
                    pool.wait_ge(s_om, b + 1)
                    nc.gpsimd.tensor_tensor(on[:, :, :], on[:, :, :], rep(ln2b), ALU.add).then_inc(s_ob, 1)

                def fetch(b):
                    if b >= 2:
                        pool.wait_ge(s_got[b % 2], b // 2 * 16 * TB)
                    for t in range(b * TB, b * TB + TB):
                        nc.gpsimd.indirect_dma_start(out=rows_in[:, t, :], out_offset=None, in_=k.slots_out,
                                                     in_offset=bass.IndirectOffsetOnAxis(ap=k.place[:, t:t + 1], axis=0)).then_inc(s_got[b % 2], 16)

                fetch(0)
                normx.power(pool, 0, 0)
                fetch(1)
                pool.wait_ge(s_wn, 16 * 5)
                for it, par, b, first, left in pipelined(pool):
                    if left:
                        nit, npar = after(it, par)
                        normx.power(pool, npar, nit)
                    norm1.power(pool, par, it)
                    pool.wait_ge(s_ln1, b * TB + TB)
                    nc.gpsimd.tensor_tensor(z[:, :, :], z[:, :, :], rep(ln1s), ALU.mult).then_inc(s_hm, 1)
                    pool.wait_ge(s_hm, b + 1)
                    if not first:
                        pool.wait_ge(s_o, (b - 1) * TB)
                    nc.gpsimd.tensor_tensor(h[par][:, :, :], z[:, :, :], rep(ln1b), ALU.add).then_inc(s_h, 1)
                    pool.wait_ge(s_h, b + 1)
                    nc.gpsimd.tensor_tensor(hb[par][:, :, :], h[par][:, :, :], rep(b2), ALU.add).then_inc(s_hb, 1)
                    if not first:
                        finish(b - 1, *prior(it, par))
                    if isinstance(b, int) and b < 2:
                        for other in range(2 + 3 * b, 5 + 3 * b):
                            fetch(other)
                finish(B - 1, B // 2 - 1, 1)

            @block.tensor
            def _(pe):
                def turn(src, bank, done):
                    for c in range(KC):
                        for i in range(TB):
                            last = nc.tensor.transpose(ps[bank + c][:, i * P:(i + 1) * P], src[:, i, c * P:(c + 1) * P], k.ident[:, :])
                    last.then_inc(done, 1)

                def up(b):
                    pe.wait_ge(s_hT, b * KC + KC)
                    for f in range(FC):
                        if f >= 2:
                            pe.wait_ge(s_g, b * FC + f - 1)
                        for c in range(KC):
                            last = nc.tensor.matmul(ps[4 + f % 2][:, :], w1[:, c, f * P:(f + 1) * P], hT[:, c, :],
                                                    start=(c == 0), stop=(c == KC - 1))
                        last.then_inc(s_u, 1)

                def down(b, tiles):
                    pe.wait_ge(s_g, b * FC + FC)
                    pe.wait_ge(s_o, b * TB)
                    for i in tiles:
                        for f in range(FC):
                            last = nc.tensor.matmul(ps[6 + i // 2][:, (i % 2) * D:(i % 2 + 1) * D], g[:, f, i * P:(i + 1) * P], w2[:, f, :],
                                                    start=(f == 0), stop=(f == FC - 1))
                        last.then_inc(s_v, 1)

                pe.wait_ge(s_xn, TB)
                turn(xn, 0, s_t)
                pe.wait_ge(s_wr, 16 * 2)
                for it, par, b, first, left in pipelined(pe):
                    pe.wait_ge(s_xT, b * KC + KC)
                    if not first:
                        pe.wait_ge(s_hT, b * KC)
                    for m in range(KC):
                        for c in range(KC):
                            last = nc.tensor.matmul(ps[2 + m][:, :], w_ret[:, c, m * P:(m + 1) * P], xnT[:, c, :], start=(c == 0), stop=(c == KC - 1))
                        last.then_inc(s_r, 1)
                    if first:
                        pe.wait_ge(s_wf, 16 * 3)
                    else:
                        up(b - 1)
                    pe.wait_ge(s_y, b * KC + KC)
                    for i in range(TB):
                        for c in range(KC):
                            last = nc.tensor.transpose(ps[i // 2][:, (i % 2) * D + c * P:(i % 2) * D + (c + 1) * P], yT[:, c, i * P:(i + 1) * P], k.ident[:, :])
                    last.then_inc(s_yt, 1)
                    if not first:
                        down(b - 1, range(TB - 1))
                    if left:
                        pe.wait_ge(s_xn, b * TB + 2 * TB)
                        pe.wait_ge(s_ln1, b * TB + TB)
                        turn(xn, 0, s_t)
                    pe.wait_ge(s_h, b + 1)
                    pe.wait_ge(s_sg, b * KC + KC)
                    turn(h[par], 2, s_ht)
                    if not first:
                        down(b - 1, range(TB - 1, TB))
                up(B - 1)
                down(B - 1, range(TB))

            @block.scalar
            def _(act):
                def gelus(b, first=False):
                    if not first:
                        act.wait_ge(s_v, b * TB)
                    for f in range(FC):
                        act.wait_ge(s_u, b * FC + f + 1)
                        nc.scalar.activation(g[:, f, :], ps[4 + f % 2][:, :], ACT.Gelu_apprx_tanh, bias=b1[:, f:f + 1]).then_inc(s_g, 1)

                act.wait_ge(s_t, 1)
                for c in range(KC):
                    nc.scalar.activation(xnT[:, c, :], ps[c][:, :], ACT.Copy).then_inc(s_xT, 1)
                act.wait_ge(s_wr, 16 * 2)
                for it, par, b, first, left in pipelined(act):
                    for m in range(KC):
                        act.wait_ge(s_r, b * KC + m + 1)
                        nc.scalar.activation(sig[:, m, :], ps[2 + m][:, :], ACT.Sigmoid, bias=b_ret[:, m:m + 1]).then_inc(s_sg, 1)
                    if first:
                        act.wait_ge(s_wf, 16 * 3)
                    else:
                        gelus(b - 1)
                    if left:
                        act.wait_ge(s_t, b + 2)
                        act.wait_ge(s_y, b * KC + KC)
                        for c in range(KC):
                            nc.scalar.activation(xnT[:, c, :], ps[c][:, :], ACT.Copy).then_inc(s_xT, 1)
                    act.wait_ge(s_ht, b + 1)
                    for c in range(KC):
                        nc.scalar.activation(hT[:, c, :], ps[2 + c][:, :], ACT.Copy).then_inc(s_hT, 1)
                gelus(B - 1)

            @block.vector
            def _(dve):
                def add_experts(b, it, par):
                    dve.wait_ge(s_got[par], it * 16 * TB + 16 * TB)
                    for i in range(TB):
                        xi = k.x[:, ds(b * TB + i, 1), :].rearrange("p a d -> p (a d)")
                        nc.vector.scalar_tensor_tensor(out=xi, in0=rows_in[:, ds(b * TB + i, 1), :].rearrange("p a d -> p (a d)"),
                                                       scalar=k.gate[:, ds(b * TB + i, 1)], in1=xi, op0=ALU.mult, op1=ALU.add).then_inc(s_add, 1)

                def norm_x(b, it, par, first=False):
                    add_experts(b, it, par)
                    wait_apart(ph, dve, s_add, b * TB + TB)
                    src = lambda i: k.x[:, ds(b * TB + i, 1), :].rearrange("p a d -> p (a d)")
                    normx.statistics(dve, par, it, src)
                    if not first:
                        dve.wait_ge(s_t, b)
                    normx.apply(dve, par, it, src, lambda i: xn[:, i, :], s_xn)

                def sums(b, it, par):
                    for i in range(TB):
                        dve.wait_ge(s_v, b * TB + i // 2 * 2 + 2)
                        dve.wait_ge(s_hb, b + 1)
                        nc.vector.tensor_tensor(o[:, i, :], ps[6 + i // 2][:, (i % 2) * D:(i % 2 + 1) * D], hb[par][:, i, :], ALU.add).then_inc(s_o, 1)
                    dve.wait_ge(s_o, b * TB + TB)
                    norm2.statistics(dve, par, it, lambda i: o[:, i, :])
                    norm2.apply(dve, par, it, lambda i: o[:, i, :], lambda i: on[:, i, :], s_on)

                def update(b):
                    dve.wait_ge(s_ob, b + 1)
                    xb = k.x[:, ds(b * TB, TB), :]
                    nc.vector.tensor_tensor(xb, xb, on[:, :, :], ALU.add).then_inc(s_x, 1)

                norm_x(0, 0, 0, True)
                dve.wait_ge(s_half, 1)
                for it, par, b, first, left in pipelined(dve):
                    for m in range(KC):
                        dve.wait_ge(s_sg, b * KC + m + 1)
                        if not first:
                            dve.wait_ge(s_yt, b)
                        nc.vector.tensor_tensor_scan(yT[:, m, :], half_t[:, :], sig[:, m, :], 0.0, ALU.mult, ALU.add).then_inc(s_z, 1)
                        dve.wait_ge(s_z, b * KC + m + 1)
                        nc.vector.scalar_tensor_tensor(out=yT[:, m, :], in0=yT[:, m, :], scalar=0.5, in1=xnT[:, m, :],
                                                       op0=ALU.mult, op1=ALU.add).then_inc(s_y, 1)
                    if left:
                        norm_x(b + 1, *after(it, par))
                    if not (isinstance(it, int) and it == 0):
                        update(b - 2)
                    dve.wait_ge(s_yt, b + 1)
                    y = lambda i: ps[i // 2][:, (i % 2) * D:(i % 2 + 1) * D]
                    norm1.statistics(dve, par, it, y)
                    if not first:
                        dve.wait_ge(s_h, b)
                    norm1.apply(dve, par, it, y, lambda i: z[:, i, :], s_ln1)
                    if not first:
                        sums(b - 1, *prior(it, par))
                update(B - 2)
                sums(B - 1, B // 2 - 1, 1)
                update(B - 1)


def phase_bitlinear(k, w, w_out, b_out, result):
    nc = k.nc
    with Phase(k, "bit") as ph:
        bank = lambda n, dt: ph.ctx.enter_context(nc.psum_tensor(f"bit_{n}", [P, 512], dt))
        t_bank, y_bank = [bank(f"t{c}", BF16) for c in range(KC)], [bank(f"y{j}", F32) for j in range(2)]
        attn_out = Output(ph, w_out, b_out, [bank(f"attn{c}", F32) for c in range(KC)], [bank(f"sum{j}", F32) for j in range(2)])
        wf, wi = ph.sb("w", [P, KC, D]), ph.sb("wi", [P, KC, D], BF16)
        ident16, ones = ph.sb("ident16", [P, P], BF16), ph.sb("ones", [P, P])
        wsum, wscale, winv = ph.sb("wsum", [P, 1]), ph.sb("wscale", [P, 1]), ph.sb("winv", [P, 1])
        norm = Norm(ph, "ln", EPS_X)
        xn, q = ph.two("xn", [P, TB, D]), ph.two("q", [P, TB, D])
        a, inv, factor = ph.two("a", [P, TB]), ph.two("inv", [P, TB]), ph.two("factor", [P, TB])
        qi, qT = ph.two("qi", [P, TB, D], BF16), ph.two("qT", [P, KC, N], BF16)
        s_w, s_c, s_ws, s_wp = ph.sem("weights"), ph.sem("constants"), ph.sem("weight_steps"), ph.sem("weight_sum")
        s_xn, s_a, s_ae, s_inv, s_fac, s_q = (ph.pair(x) for x in ("xn", "amax", "amax_eps", "inverse", "factor", "quant_steps"))
        s_round = ph.pair("rounded")
        s_qi, s_t, s_qT, s_y, s_x, s_st = (ph.pair(x) for x in ("quantised", "turned", "qT", "product", "x_updated", "stored"))
        WSTEPS = 7
        with nc.Block() as block:
            @block.sync
            def _(sp):
                sp.dma_start(wf[:, :, :], rows(w)).then_inc(s_w, 16)
                attn_out.load(sp, 0, 0, 0)
                attn_out.load_weights(sp)
                attn_out.load(sp, 1, 0, 1)
                with sp.Fori(1, B // 2) as it:
                    for par in ALLX:
                        attn_out.load(sp, it * 2 + par, it, par)

            @block.gpsimd
            def _(pool):
                ph.clear_others(pool)
                nc.gpsimd.memset(ones[:, :], 1.0).then_inc(s_c, 1)
                nc.gpsimd.tensor_copy(ident16[:, :], k.ident[:, :]).then_inc(s_c, 1)
                pool.wait_ge(attn_out.s_w, attn_out.w_all)
                for par in ALLX:
                    attn_out.add_bias(pool, par, par)
                norm.power(pool, 0, 0)
                for it, par, b, first, left in pipelined(pool):
                    if left == 2:
                        attn_out.add_bias(pool, b + 2, par)
                    if left:
                        nit, npar = after(it, par)
                        norm.power(pool, npar, nit)

            @block.tensor
            def _(pe):
                attn_out.turn(pe, 0, 0)
                pe.wait_ge(s_c, 2)
                pe.wait_ge(s_ws, 1)
                nc.tensor.matmul(y_bank[0][:, 0:1], ones[:, :], wsum[:, :], start=True, stop=True).then_inc(s_wp, 1)
                pe.wait_ge(attn_out.s_w, attn_out.w_all)
                attn_out.products(pe, 0, 0)
                attn_out.turn(pe, 0, 1)
                for it, par, b, first, left in pipelined(pe):
                    if left:
                        attn_out.products(pe, *after(it, par))
                    if left == 2:
                        attn_out.turn(pe, it + 1, par)
                    pe.wait_ge(s_qi[par], it + 1)
                    pe.wait_ge(*before(s_qT, it, par, KC))
                    for c in range(KC):
                        for i in range(TB):
                            last = nc.tensor.transpose(t_bank[c][:, i * P:(i + 1) * P], qi[par][:, i, c * P:(c + 1) * P], ident16[:, :])
                    last.then_inc(s_t[par], 1)
                    pe.wait_ge(s_qT[par], it * KC + KC)
                    if first:
                        pe.wait_ge(s_ws, WSTEPS)
                    pe.wait_ge(*before(s_x, it, par, TB))
                    for i in range(TB):
                        for c in range(KC):
                            last = nc.tensor.matmul(y_bank[i // 2][:, (i % 2) * D:(i % 2 + 1) * D], qT[par][:, c, i * P:(i + 1) * P], wi[:, c, :],
                                                    start=(c == 0), stop=(c == KC - 1))
                    last.then_inc(s_y[par], 1)

            @block.scalar
            def _(act):
                def store(b, it, par):
                    act.wait_ge(s_x[par], it * TB + TB)
                    act.dma_start(result[ds(b, 1)].rearrange("b (i p) d -> p (b i) d", p=P), k.x[:, ds(b * TB, TB), :]).then_inc(s_st[par], 16)

                for par in ALLX:
                    attn_out.copies(act, 0, par)
                for it, par, b, first, left in pipelined(act):
                    if left == 2:
                        attn_out.copies(act, it + 1, par)
                    if not first:
                        store(b - 1, *prior(it, par))
                    act.wait_ge(s_t[par], it + 1)
                    act.wait_ge(s_y[par], it)
                    for c in range(KC):
                        nc.scalar.activation(qT[par][:, c, :], t_bank[c][:, :], ACT.Copy).then_inc(s_qT[par], 1)
                store(B - 1, B // 2 - 1, 1)
                for par in ALLX:
                    act.wait_ge(s_st[par], B // 2 * 16)

            @block.vector
            def _(dve):
                dve.wait_ge(s_w, 16)
                n = [0]

                def step(ins):
                    n[0] += 1
                    ins.then_inc(s_ws, 1)
                    dve.wait_ge(s_ws, n[0])
                step(nc.vector.tensor_reduce(wsum[:, :], wf[:, :, :], AX.XY, ALU.add, apply_absolute_value=True))
                dve.wait_ge(s_wp, 1)
                step(nc.vector.tensor_scalar(wscale[:, :], y_bank[0][:, 0:1], 1.0 / (D * D), 1e-8, ALU.mult, ALU.add))
                step(nc.vector.reciprocal(winv[:, :], wscale[:, :]))
                step(nc.vector.tensor_scalar(wf[:, :, :], wf[:, :, :], winv[:, :], ROUND, ALU.mult, ALU.add))
                step(nc.vector.tensor_scalar(wf[:, :, :], wf[:, :, :], ROUND, 1.0, ALU.subtract, ALU.min))
                step(nc.vector.tensor_scalar(wi[:, :, :], wf[:, :, :], -1.0, None, ALU.max))
                step(nc.vector.tensor_scalar(wscale[:, :], wscale[:, :], 1.0 / 127.0, None, ALU.mult))
                assert n[0] == WSTEPS

                def update(it, par, b):
                    dve.wait_ge(s_fac[par], it + 1)
                    dve.wait_ge(s_y[par], it + 1)
                    for i in range(TB):
                        xi = k.x[:, ds(b * TB + i, 1), :].rearrange("p a d -> p (a d)")
                        nc.vector.scalar_tensor_tensor(out=xi, in0=y_bank[i // 2][:, (i % 2) * D:(i % 2 + 1) * D],
                                                       scalar=factor[par][:, i:i + 1], in1=xi, op0=ALU.mult, op1=ALU.add).then_inc(s_x[par], 1)

                src = lambda b: (lambda i: k.x[:, ds(b * TB + i, 1), :].rearrange("p a d -> p (a d)"))
                attn_out.sums(dve, 0, 0, 0)
                wait_apart(ph, dve, attn_out.s_x[0], TB)
                norm.statistics(dve, 0, 0, src(0))
                for it, par, b, first, left in pipelined(dve):
                    norm.apply(dve, par, it, src(b), lambda i: xn[par][:, i, :], s_xn[par])
                    dve.wait_ge(s_xn[par], it * TB + TB)
                    nc.vector.tensor_reduce(a[par][:, :], xn[par][:, :, :], AX.X, ALU.max, apply_absolute_value=True).then_inc(s_a[par], 1)
                    dve.wait_ge(s_a[par], it + 1)
                    nc.vector.tensor_scalar_add(a[par][:, :], a[par][:, :], 1e-8).then_inc(s_ae[par], 1)
                    dve.wait_ge(s_ae[par], it + 1)
                    nc.vector.reciprocal(inv[par][:, :], a[par][:, :]).then_inc(s_inv[par], 1)
                    nc.vector.tensor_scalar(factor[par][:, :], a[par][:, :], wscale[:, :], None, ALU.mult).then_inc(s_fac[par], 1)
                    dve.wait_ge(s_inv[par], it + 1)
                    for i in range(TB):
                        nc.vector.tensor_scalar(q[par][:, i, :], xn[par][:, i, :], inv[par][:, i:i + 1], 127.0, ALU.mult, ALU.mult).then_inc(s_q[par], 1)
                    dve.wait_ge(s_q[par], it * TB + TB)
                    nc.vector.tensor_scalar(q[par][:, :, :], q[par][:, :, :], ROUND, ROUND + 127.0, ALU.add, ALU.min).then_inc(s_round[par], 1)
                    if not first:
                        update(*prior(it, par), b - 1)
                    if left:
                        nit, npar = after(it, par)
                        attn_out.sums(dve, b + 1, nit, npar)
                        wait_apart(ph, dve, attn_out.s_x[npar], nit * TB + TB)
                        norm.statistics(dve, npar, nit, src(b + 1))
                    dve.wait_ge(s_round[par], it + 1)
                    dve.wait_ge(s_t[par], it)
                    nc.vector.tensor_scalar(qi[par][:, :, :], q[par][:, :, :], ROUND, -128.0, ALU.subtract, ALU.max).then_inc(s_qi[par], 1)
                update(B // 2 - 1, 1, B - 1)


def build(nc, a, out):
    with ExitStack() as ctx:
        k = Kernel(nc, ctx)
        scratch = lambda name, shape, dt: nc.dram_tensor(name, shape, dt, kind="Internal").ap()
        k.split = scratch("qk_split", [B, 2, 3, D, N], BF16)
        k.values = scratch("v_heads", [B, N, H * VW], F32)
        k.attn = scratch("attn_out", [B, N, D], F32)
        k.xn_rows = scratch("xn_rows", [B, N, D], F32)
        k.slots_in = scratch("slots_in", [-(-SLOTS // B) * B * P, D], F32)
        k.slots_out = scratch("slots_out", [SLOTS * P, D], F32)
        phase_start(k, a["x"])
        phase_project(k, "proj0", dict(q=a["wq0"], k=a["wk0"], v=a["wv0"], factors=a["factors0"]))
        phase_core(k, "core0", 1.0, causal=True)
        phase_output(k, "out0", a["wo0"])
        phase_project(k, "proj1", dict(q=a["wq1"], k=a["wk1"], v=a["wv1"], bqk=a["bqk1"], bv=a["bv1"]), a["ctx"])
        phase_core(k, "core1", HD ** -0.5, mask=(a["mask_q"], a["mask_k"]))
        moe(k, (a["wo1"], a["bo1"]), a["wr"], a["br"], a["moe_w1"], a["moe_b1"], a["moe_w2"], a["moe_b2"])
        phase_retention(k, dict(ret=a["w_ret"], b_ret=a["b_ret"], w1=a["ffn_w1"], b1=a["ffn_b1"], w2=a["ffn_w2"], b2=a["ffn_b2"],
                                ln1s=a["ln1s"], ln1b=a["ln1b"], ln2s=a["ln2s"], ln2b=a["ln2b"]))
        phase_project(k, "proj2", dict(q=a["wq2"], k=a["wk2"], v=a["wv2"], bqk=a["bqk2"], bv=a["bv2"]), a["ctx"])
        phase_core(k, "core2", HD ** -0.5)
        phase_bitlinear(k, a["bit_w"], a["wo2"], a["bo2"], out)


def kernel(**inputs):
    import numpy as np
    import concourse.bacc as bacc
    from concourse import mybir as mb
    from concourse.bass_utils import run_bass_kernel_spmd

    i = {n: np.asarray(v) for n, v in inputs.items()}
    turned = lambda w: np.ascontiguousarray(w.T)
    by_feature = lambda v: np.ascontiguousarray(v.reshape(-1, P).T)
    heads = lambda s: np.repeat(s, HD)
    mask = np.ascontiguousarray(i["mask_Bx1xSxS2_bk1"][:, 0])
    a = {
        "x": i["x"], "ctx": i["ctx_1024"],
        "mask_q": mask, "mask_k": np.ascontiguousarray(mask.transpose(0, 2, 1)),
        "wq0": turned(i["L0_attn_Wq"]), "wk0": turned(i["L0_attn_Wk"]), "wv0": turned(i["L0_attn_Wv"]), "wo0": turned(i["L0_attn_Wo"]),
        "factors0": by_feature(np.concatenate([heads(i["L0_attn_q_scale"]), heads(i["L0_attn_k_scale"])])),
        "wq1": i["L0_xattn_Wq"], "wk1": i["L0_xattn_Wk"], "wv1": i["L0_xattn_Wv"], "wo1": i["L0_xattn_Wo"],
        "bqk1": by_feature(np.concatenate([i["L0_xattn_bq"], i["L0_xattn_bk"]])), "bv1": i["L0_xattn_bv"], "bo1": i["L0_xattn_bo"],
        "wr": i["L0_ffn_wr"], "br": i["L0_ffn_br"], "moe_w1": i["L0_ffn_w1"], "moe_b1": by_feature(i["L0_ffn_b1"]),
        "moe_w2": i["L0_ffn_w2"], "moe_b2": i["L0_ffn_b2"],
        "w_ret": i["L1_attn_W_ret"], "b_ret": by_feature(i["L1_attn_b_ret"]), "ffn_w1": i["L1_attn_W1"], "ffn_b1": by_feature(i["L1_attn_b1"]),
        "ffn_w2": i["L1_attn_W2"], "ffn_b2": i["L1_attn_b2"], "ln1s": i["L1_attn_ln1_scale"], "ln1b": i["L1_attn_ln1_bias"],
        "ln2s": i["L1_attn_ln2_scale"], "ln2b": i["L1_attn_ln2_bias"],
        "wq2": i["L1_xattn_W_Q"], "wk2": i["L1_xattn_W_K"], "wv2": i["L1_xattn_W_V"], "wo2": i["L1_xattn_W_O"],
        "bqk2": by_feature(np.concatenate([i["L1_xattn_b_Q"], i["L1_xattn_b_K"]])), "bv2": i["L1_xattn_b_V"], "bo2": i["L1_xattn_b_O"],
        "bit_w": turned(i["L1_ffn_weight"]),
    }
    nc = bacc.Bacc("TRN2", target_bir_lowering=False, num_devices=1)
    arrays = {f"in_{n}": v for n, v in a.items()}
    args = {n: nc.dram_tensor(f"in_{n}", v.shape, mb.dt.from_np(v.dtype), kind="ExternalInput").ap() for n, v in a.items()}
    out = nc.dram_tensor("out_x", (B, N, D), F32, kind="ExternalOutput").ap()
    build(nc, args, out)
    r = run_bass_kernel_spmd(nc, [arrays], core_ids=[0])
    return r.results[0]["out_x"]
```
